# Optimizing a Trainium2 kernel written in Bass

```python
import numpy as np
import jax
import jax.numpy as jnp

def _softmax(x, axis=-1):
    return jax.nn.softmax(x, axis=axis)

def _gelu(x):
    return jax.nn.gelu(x, approximate=True)

def _silu(x):
    return jax.nn.silu(x)

def _sigmoid(x):
    return jax.nn.sigmoid(x)

def _layernorm(x, axis=-1, eps=1e-05):
    m = jnp.mean(x, axis=axis, keepdims=True)
    v = jnp.var(x, axis=axis, keepdims=True)
    return (x - m) / jnp.sqrt(v + eps)

def _scatter_add(tgt, idx, src, axis=0):
    return tgt.at[idx].add(src)

def _segment_sum(src, seg, n):
    return jax.ops.segment_sum(src, seg, n)
kernel_name = 'mk_decoder_preln_d2_seqx_r8_efcb64'

def setup_inputs(seed: int=0):
    np.random.seed(seed)
    _w = jnp.asarray

    def _rec_inputs():
        import jax
        import jax.numpy as jnp
        _rk = jax.random.key(seed)
        x = 7.22e-05 + 1 * jax.random.normal(jax.random.fold_in(_rk, 1), (8, 256, 128), jnp.float32)
        _lenS = 256 - jax.random.randint(jax.random.fold_in(_rk, 7), (8,), 0, max(1, 256 // 4) + 1, jnp.int32)
        _lenS2 = 256 - jax.random.randint(jax.random.fold_in(_rk, 8), (8,), 0, max(1, 256 // 4) + 1, jnp.int32)
        _ctx_1024P = jax.random.normal(jax.random.fold_in(_rk, 11), (8, 16, 128), jnp.float32)
        _ctx_1024c = jax.random.dirichlet(jax.random.fold_in(_rk, 511), 0.3 * jnp.ones((16,), jnp.float32), (8, 256))
        _ctx_1024t = jnp.einsum('bsk,bkd->bsd', _ctx_1024c, _ctx_1024P)
        _ctx_1024t = _ctx_1024t * jax.lax.rsqrt(jnp.mean(jnp.square(_ctx_1024t)) + 1e-12) * 0.953939
        ctx_1024 = 4.13588e-05 + 0.999923 * (_ctx_1024t + 0.3 * jax.random.normal(jax.random.fold_in(_rk, 611), (8, 256, 128), jnp.float32))
        return (x, ctx_1024)
    x, ctx_1024 = _rec_inputs()

    def _L0_attn_setup():
        import jax, jax.numpy as jnp
        import numpy as np
        DIM = 128
        N_HEADS = 16
        HEAD_DIM = DIM // N_HEADS
        key = jax.random.key(seed)
        ks = jax.random.split(key, 5)
        B, T = (4, 128)
        scale = 1.0 / np.sqrt(DIM)
        x = jax.random.normal(ks[0], (B, T, DIM), dtype=jnp.float32)
        W_qkv = jax.random.uniform(ks[1], (3 * DIM, DIM), dtype=jnp.float32, minval=-scale, maxval=scale)
        b_qkv = jax.random.uniform(ks[2], (3 * DIM,), dtype=jnp.float32, minval=-scale, maxval=scale)
        W_out = jax.random.uniform(ks[3], (DIM, DIM), dtype=jnp.float32, minval=-scale, maxval=scale)
        b_out = jax.random.uniform(ks[4], (DIM,), dtype=jnp.float32, minval=-scale, maxval=scale)
        return {'x': x, 'W_qkv': W_qkv, 'b_qkv': b_qkv, 'W_out': W_out, 'b_out': b_out}
    _L0_attn_all = _L0_attn_setup()
    _L0_attn_in = {k: v for k, v in _L0_attn_all.items() if k in ('W_qkv', 'b_qkv', 'W_out', 'b_out')}
    del _L0_attn_all

    def _L0_xattn_setup():
        import jax, jax.numpy as jnp
        import numpy as np
        DIM = 128
        key = jax.random.key(seed)
        ks = jax.random.split(key, 8)
        B, Sx, Sy, D = (4, 256, 256, DIM)
        s = 1.0 / np.sqrt(D)
        return {'x': jax.random.normal(ks[0], (B, Sx, D), jnp.float32), 'y': jax.random.normal(ks[1], (B, Sy, D), jnp.float32), 'Wq': jax.random.normal(ks[2], (D, D), jnp.float32) * s, 'bq': jnp.zeros((D,), jnp.float32), 'Wk': jax.random.normal(ks[3], (D, D), jnp.float32) * s, 'bk': jnp.zeros((D,), jnp.float32), 'Wv': jax.random.normal(ks[4], (D, D), jnp.float32) * s, 'bv': jnp.zeros((D,), jnp.float32)}
    _L0_xattn_all = _L0_xattn_setup()
    _L0_xattn_in = {k: v for k, v in _L0_xattn_all.items() if k in ('Wq', 'bq', 'Wk', 'bk', 'Wv', 'bv')}
    del _L0_xattn_all

    def _L0_ffn_setup():
        import jax, jax.numpy as jnp
        import numpy as np
        NUM_EXPERTS = 8
        TOP_K = 2
        HIDDEN = 128
        INTER_TOTAL = 1024
        B, S = (2, 256)
        key = jax.random.key(seed)
        k1, k2, k3, k4, k5, k6 = jax.random.split(key, 6)
        T = B * S
        x = jax.random.normal(k1, (B, S, HIDDEN), dtype=jnp.float32)
        scores = jax.random.uniform(k2, (T, NUM_EXPERTS), dtype=jnp.float32)
        expert_weights = jax.random.uniform(k3, (T, TOP_K), dtype=jnp.float32)
        top_experts = jax.random.randint(k4, (T, TOP_K), 0, NUM_EXPERTS, dtype=jnp.int32)
        w1 = jax.random.normal(k5, (HIDDEN, INTER_TOTAL), dtype=jnp.float32) * 0.02
        w2 = jax.random.normal(k6, (INTER_TOTAL, HIDDEN), dtype=jnp.float32) * 0.02
        return {'x': x, 'scores': scores, 'expert_weights': expert_weights, 'top_experts': top_experts, 'w1': w1, 'w2': w2}
    _L0_ffn_all = _L0_ffn_setup()
    _L0_ffn_in = {k: v for k, v in _L0_ffn_all.items() if k in ('scores', 'expert_weights', 'top_experts', 'w1', 'w2')}
    del _L0_ffn_all

    def _L1_attn_setup():
        import jax, jax.numpy as jnp
        import numpy as np
        import math
        DIM = 128
        ATTN_DIM = 128
        B, S = (2, 512)
        key = jax.random.key(seed)
        k1, k2, k3 = jax.random.split(key, 3)
        x = jax.random.normal(k1, (B, S, DIM), dtype=jnp.float32)
        W_qkv = jax.random.normal(k2, (3 * ATTN_DIM, DIM), dtype=jnp.float32) * (1.0 / math.sqrt(DIM))
        b_qkv = jax.random.normal(k3, (3 * ATTN_DIM,), dtype=jnp.float32) * 0.01
        return {'x': x, 'W_qkv': W_qkv, 'b_qkv': b_qkv}
    _L1_attn_all = _L1_attn_setup()
    _L1_attn_in = {k: v for k, v in _L1_attn_all.items() if k in ('W_qkv', 'b_qkv')}
    del _L1_attn_all

    def _L1_xattn_setup():
        import jax, jax.numpy as jnp
        import numpy as np
        D_MODEL = 128
        NUM_HEADS = 16
        HEAD_DIM = D_MODEL // NUM_HEADS
        key = jax.random.key(seed)
        ks = jax.random.split(key, 11)
        B, S = (2, 256)
        scale = 1.0 / np.sqrt(D_MODEL)
        inp = {'query': jax.random.normal(ks[0], (B, S, D_MODEL), jnp.float32), 'key': jax.random.normal(ks[1], (B, S, D_MODEL), jnp.float32), 'value': jax.random.normal(ks[2], (B, S, D_MODEL), jnp.float32), 'Wq': jax.random.normal(ks[3], (D_MODEL, D_MODEL), jnp.float32) * scale, 'bq': jnp.zeros((D_MODEL,), jnp.float32), 'Wk': jax.random.normal(ks[4], (D_MODEL, D_MODEL), jnp.float32) * scale, 'bk': jnp.zeros((D_MODEL,), jnp.float32), 'Wv': jax.random.normal(ks[5], (D_MODEL, D_MODEL), jnp.float32) * scale, 'bv': jnp.zeros((D_MODEL,), jnp.float32), 'Wo': jax.random.normal(ks[6], (D_MODEL, D_MODEL), jnp.float32) * scale, 'bo': jnp.zeros((D_MODEL,), jnp.float32)}
        return inp
    _L1_xattn_all = _L1_xattn_setup()
    _L1_xattn_in = {k: v for k, v in _L1_xattn_all.items() if k in ('Wq', 'bq', 'Wk', 'bk', 'Wv', 'bv', 'Wo', 'bo')}
    del _L1_xattn_all

    def _L1_ffn_setup():
        import jax, jax.numpy as jnp
        import numpy as np
        NUM_HEAVY = 128
        N_ITERS = 50
        FETCH_K_RATIO = 9.0 / 8.0
        EPS = 1.0

        def rmsnorm(x, gamma):
            scale = gamma.shape[0] ** 0.5
            normed = x / jnp.maximum(jnp.linalg.norm(x, axis=-1, keepdims=True), 1e-12)
            return normed * scale * gamma

        def feedforward(x, gamma, w1, b1, w2, b2):
            h = rmsnorm(x, gamma)
            h = jax.nn.gelu(h @ w1.T + b1, approximate=False)
            return h @ w2.T + b2

        def coor_descent(s, n_iters, k, eps):
            logk = jnp.log(jnp.asarray(k, s.dtype))
            a0 = jnp.zeros_like(s[..., :1])
            b0 = -s

            def body(carry, _):
                a, b = carry
                a = eps * (logk - jax.nn.logsumexp((s + b) / eps, axis=-1, keepdims=True))
                b = -jax.nn.relu(s + a)
                return ((a, b), None)
            (a, b), _ = jax.lax.scan(body, (a0, b0), None, length=n_iters)
            return jnp.exp((s + a + b) / eps)
        key = jax.random.key(seed)
        ks = jax.random.split(key, 12)
        b, n, dim = (8, 1024, 128)
        d_light, d_heavy = (int(dim * 0.5), dim * 4)

        def lin(k, dout, din):
            bound = 1.0 / np.sqrt(din)
            k1, k2 = jax.random.split(k)
            w = jax.random.uniform(k1, (dout, din), jnp.float32, -bound, bound)
            bb = jax.random.uniform(k2, (dout,), jnp.float32, -bound, bound)
            return (w, bb)
        x = jax.random.normal(ks[0], (b, n, dim), jnp.float32)
        routing_token = jax.random.normal(ks[1], (dim,), jnp.float32)
        w1_l, b1_l = lin(ks[2], d_light, dim)
        w2_l, b2_l = lin(ks[3], dim, d_light)
        w1_h, b1_h = lin(ks[4], d_heavy, dim)
        w2_h, b2_h = lin(ks[5], dim, d_heavy)
        return dict(x=x, routing_token=routing_token, gamma_l=jnp.ones((dim,), jnp.float32), w1_l=w1_l, b1_l=b1_l, w2_l=w2_l, b2_l=b2_l, gamma_h=jnp.ones((dim,), jnp.float32), w1_h=w1_h, b1_h=b1_h, w2_h=w2_h, b2_h=b2_h)
    _L1_ffn_all = _L1_ffn_setup()
    _L1_ffn_in = {k: v for k, v in _L1_ffn_all.items() if k in ('routing_token', 'gamma_l', 'w1_l', 'b1_l', 'w2_l', 'b2_l', 'gamma_h', 'w1_h', 'b1_h', 'w2_h', 'b2_h')}
    del _L1_ffn_all
    return {'x': x, 'ctx_1024': ctx_1024, 'L0_attn_W_qkv': _L0_attn_in['W_qkv'], 'L0_attn_b_qkv': _L0_attn_in['b_qkv'], 'L0_attn_W_out': _L0_attn_in['W_out'], 'L0_attn_b_out': _L0_attn_in['b_out'], 'L0_xattn_Wq': _L0_xattn_in['Wq'], 'L0_xattn_bq': _L0_xattn_in['bq'], 'L0_xattn_Wk': _L0_xattn_in['Wk'], 'L0_xattn_bk': _L0_xattn_in['bk'], 'L0_xattn_Wv': _L0_xattn_in['Wv'], 'L0_xattn_bv': _L0_xattn_in['bv'], 'L0_ffn_scores': _L0_ffn_in['scores'], 'L0_ffn_expert_weights': _L0_ffn_in['expert_weights'], 'L0_ffn_top_experts': _L0_ffn_in['top_experts'], 'L0_ffn_w1': _L0_ffn_in['w1'], 'L0_ffn_w2': _L0_ffn_in['w2'], 'L1_attn_W_qkv': _L1_attn_in['W_qkv'], 'L1_attn_b_qkv': _L1_attn_in['b_qkv'], 'L1_xattn_Wq': _L1_xattn_in['Wq'], 'L1_xattn_bq': _L1_xattn_in['bq'], 'L1_xattn_Wk': _L1_xattn_in['Wk'], 'L1_xattn_bk': _L1_xattn_in['bk'], 'L1_xattn_Wv': _L1_xattn_in['Wv'], 'L1_xattn_bv': _L1_xattn_in['bv'], 'L1_xattn_Wo': _L1_xattn_in['Wo'], 'L1_xattn_bo': _L1_xattn_in['bo'], 'L1_ffn_routing_token': _L1_ffn_in['routing_token'], 'L1_ffn_gamma_l': _L1_ffn_in['gamma_l'], 'L1_ffn_w1_l': _L1_ffn_in['w1_l'], 'L1_ffn_b1_l': _L1_ffn_in['b1_l'], 'L1_ffn_w2_l': _L1_ffn_in['w2_l'], 'L1_ffn_b2_l': _L1_ffn_in['b2_l'], 'L1_ffn_gamma_h': _L1_ffn_in['gamma_h'], 'L1_ffn_w1_h': _L1_ffn_in['w1_h'], 'L1_ffn_b1_h': _L1_ffn_in['b1_h'], 'L1_ffn_w2_h': _L1_ffn_in['w2_h'], 'L1_ffn_b2_h': _L1_ffn_in['b2_h']}

def reference(x, ctx_1024, L0_attn_W_qkv, L0_attn_b_qkv, L0_attn_W_out, L0_attn_b_out, L0_xattn_Wq, L0_xattn_bq, L0_xattn_Wk, L0_xattn_bk, L0_xattn_Wv, L0_xattn_bv, L0_ffn_scores, L0_ffn_expert_weights, L0_ffn_top_experts, L0_ffn_w1, L0_ffn_w2, L1_attn_W_qkv, L1_attn_b_qkv, L1_xattn_Wq, L1_xattn_bq, L1_xattn_Wk, L1_xattn_bk, L1_xattn_Wv, L1_xattn_bv, L1_xattn_Wo, L1_xattn_bo, L1_ffn_routing_token, L1_ffn_gamma_l, L1_ffn_w1_l, L1_ffn_b1_l, L1_ffn_w2_l, L1_ffn_b2_l, L1_ffn_gamma_h, L1_ffn_w1_h, L1_ffn_b1_h, L1_ffn_w2_h, L1_ffn_b2_h):
    import jax
    import jax.numpy as jnp

    def _L0_attn_ref(x, W_qkv, b_qkv, W_out, b_out):
        import jax, jax.numpy as jnp
        import numpy as np
        DIM = 128
        N_HEADS = 16
        HEAD_DIM = DIM // N_HEADS
        B, T, D = x.shape
        qkv = x @ W_qkv.T + b_qkv
        q, k, v = jnp.split(qkv, 3, axis=-1)
        q = q.reshape(B, T, N_HEADS, HEAD_DIM).transpose(0, 2, 1, 3)
        k = k.reshape(B, T, N_HEADS, HEAD_DIM).transpose(0, 2, 1, 3)
        v = v.reshape(B, T, N_HEADS, HEAD_DIM).transpose(0, 2, 1, 3)
        scores = jnp.einsum('bhqd,bhkd->bhqk', q, k) / jnp.sqrt(jnp.float32(HEAD_DIM))
        att = jax.nn.softmax(scores, axis=-1)
        out = jnp.einsum('bhqk,bhkd->bhqd', att, v)
        out = out.transpose(0, 2, 1, 3).reshape(B, T, D)
        return out @ W_out.T + b_out

    def _L0_xattn_ref(x, y, Wq, bq, Wk, bk, Wv, bv):
        import jax, jax.numpy as jnp
        import numpy as np
        DIM = 128
        D = x.shape[-1]
        scale = jnp.sqrt(jnp.asarray(D, x.dtype))
        Q = jnp.einsum('bsd,de->bse', x, Wq) + bq
        K = jnp.einsum('btd,de->bte', y, Wk) + bk
        V = jnp.einsum('btd,de->bte', y, Wv) + bv
        scores = jnp.einsum('bse,bte->bst', Q, K) / scale
        probs = jax.nn.softmax(scores, axis=-1)
        out = jnp.einsum('bst,bte->bse', probs, V)
        return out

    def _L0_ffn_ref(x, scores, expert_weights, top_experts, w1, w2):
        import jax, jax.numpy as jnp
        import numpy as np
        NUM_EXPERTS = 8
        TOP_K = 2
        HIDDEN = 128
        INTER_TOTAL = 1024
        B, S = (2, 256)
        in_shape = x.shape
        T = in_shape[0] * in_shape[1]
        H = in_shape[-1]
        x_flat = x.reshape(T, H)
        flat_experts = top_experts.reshape(-1)
        flat_weights = expert_weights.reshape(-1)
        order = jnp.argsort(flat_experts, stable=True)
        token_idx = order // TOP_K
        xg = x_flat[token_idx]
        h = jax.nn.gelu(xg @ w1, approximate=True)
        y = h @ w2
        w_sorted = flat_weights[order]
        out = jnp.zeros((T, H), dtype=x.dtype).at[token_idx].add(w_sorted[:, None] * y)
        return out.reshape(in_shape)

    def _L1_attn_ref(x, W_qkv, b_qkv):
        import jax, jax.numpy as jnp
        import numpy as np
        import math
        DIM = 128
        ATTN_DIM = 128
        B, S = (2, 512)
        b, s, d = x.shape
        qkv = jnp.einsum('bsd,ed->bse', x, W_qkv) + b_qkv
        q, k, v = jnp.split(qkv, 3, axis=-1)
        score = jnp.einsum('bqd,bkd->bqk', q, k)
        causal = jnp.tril(jnp.ones((s, s), dtype=bool))
        score = jnp.where(causal, score, -jnp.inf)
        attn = jax.nn.softmax(score / math.sqrt(ATTN_DIM), axis=-1)
        y = jnp.einsum('bqk,bkd->bqd', attn, v)
        return y

    def _L1_xattn_ref(query, key, value, Wq, bq, Wk, bk, Wv, bv, Wo, bo):
        import jax, jax.numpy as jnp
        import numpy as np
        D_MODEL = 128
        NUM_HEADS = 16
        HEAD_DIM = D_MODEL // NUM_HEADS
        B, S, _ = query.shape
        q = query @ Wq + bq
        k = key @ Wk + bk
        v = value @ Wv + bv
        q = q.reshape(B, S, NUM_HEADS, HEAD_DIM).transpose(0, 2, 1, 3)
        k = k.reshape(B, -1, NUM_HEADS, HEAD_DIM).transpose(0, 2, 1, 3)
        v = v.reshape(B, -1, NUM_HEADS, HEAD_DIM).transpose(0, 2, 1, 3)
        scores = jnp.einsum('bhqd,bhkd->bhqk', q, k) / jnp.sqrt(jnp.asarray(HEAD_DIM, q.dtype))
        attn = jax.nn.softmax(scores, axis=-1)
        out = jnp.einsum('bhqk,bhkd->bhqd', attn, v)
        out = out.transpose(0, 2, 1, 3).reshape(B, S, D_MODEL)
        return out @ Wo + bo

    def _L1_ffn_ref(x, routing_token, gamma_l, w1_l, b1_l, w2_l, b2_l, gamma_h, w1_h, b1_h, w2_h, b2_h):
        import jax, jax.numpy as jnp
        import numpy as np
        NUM_HEAVY = 128
        N_ITERS = 50
        FETCH_K_RATIO = 9.0 / 8.0
        EPS = 1.0

        def rmsnorm(x, gamma):
            scale = gamma.shape[0] ** 0.5
            normed = x / jnp.maximum(jnp.linalg.norm(x, axis=-1, keepdims=True), 1e-12)
            return normed * scale * gamma

        def feedforward(x, gamma, w1, b1, w2, b2):
            h = rmsnorm(x, gamma)
            h = jax.nn.gelu(h @ w1.T + b1, approximate=False)
            return h @ w2.T + b2

        def coor_descent(s, n_iters, k, eps):
            logk = jnp.log(jnp.asarray(k, s.dtype))
            a0 = jnp.zeros_like(s[..., :1])
            b0 = -s

            def body(carry, _):
                a, b = carry
                a = eps * (logk - jax.nn.logsumexp((s + b) / eps, axis=-1, keepdims=True))
                b = -jax.nn.relu(s + a)
                return ((a, b), None)
            (a, b), _ = jax.lax.scan(body, (a0, b0), None, length=n_iters)
            return jnp.exp((s + a + b) / eps)
        b, n, dim = x.shape
        light_out = feedforward(x, gamma_l, w1_l, b1_l, w2_l, b2_l)
        s = jnp.einsum('bnd,d->bn', x, routing_token)
        effective_k = min(NUM_HEAVY * FETCH_K_RATIO, n)
        scores = coor_descent(s, N_ITERS, effective_k, EPS)
        selected_scores, selected_indices = jax.lax.top_k(scores, NUM_HEAVY)
        selected_scores = selected_scores + jax.lax.stop_gradient(1.0 - selected_scores)
        routed = jnp.take_along_axis(x, selected_indices[..., None], axis=1)
        routed_out = feedforward(routed, gamma_h, w1_h, b1_h, w2_h, b2_h)
        routed_out = routed_out * selected_scores[..., None]
        batch_range = jnp.arange(b)[:, None]
        heavy_out = jnp.zeros_like(x).at[batch_range, selected_indices].set(routed_out)
        return light_out + heavy_out
    x = x + _L0_attn_ref(_layernorm(x, axis=-1), L0_attn_W_qkv, L0_attn_b_qkv, L0_attn_W_out, L0_attn_b_out)
    x = x + _L0_xattn_ref(_layernorm(x, axis=-1), ctx_1024, L0_xattn_Wq, L0_xattn_bq, L0_xattn_Wk, L0_xattn_bk, L0_xattn_Wv, L0_xattn_bv)
    x = x + _L0_ffn_ref(_layernorm(x, axis=-1), L0_ffn_scores, L0_ffn_expert_weights, L0_ffn_top_experts, L0_ffn_w1, L0_ffn_w2)
    x = x + _L1_attn_ref(_layernorm(x, axis=-1), L1_attn_W_qkv, L1_attn_b_qkv)
    x = x + _L1_xattn_ref(_layernorm(x, axis=-1), ctx_1024, ctx_1024, L1_xattn_Wq, L1_xattn_bq, L1_xattn_Wk, L1_xattn_bk, L1_xattn_Wv, L1_xattn_bv, L1_xattn_Wo, L1_xattn_bo)
    x = x + _L1_ffn_ref(_layernorm(x, axis=-1), L1_ffn_routing_token, L1_ffn_gamma_l, L1_ffn_w1_l, L1_ffn_b1_l, L1_ffn_w2_l, L1_ffn_b2_l, L1_ffn_gamma_h, L1_ffn_w1_h, L1_ffn_b1_h, L1_ffn_w2_h, L1_ffn_b2_h)
    return x

_drawn_inputs = setup_inputs


def setup_inputs(seed=0):
    import zlib

    import numpy as np

    out = dict(_drawn_inputs(seed))
    spreads = {'L0_xattn_bq': (0.0, 0.304),
     'L0_xattn_bk': (0.0, 0.8),
     'L0_xattn_bv': (0.0, 0.1),
     'L1_xattn_bq': (0.0, 0.401),
     'L1_xattn_bk': (0.0, 0.8),
     'L1_xattn_bv': (0.0, 0.1),
     'L1_xattn_bo': (0.0, 0.1),
     'L1_ffn_gamma_l': (1.0, 0.54),
     'L1_ffn_gamma_h': (1.0, 0.6)}
    factors = {'L0_ffn_expert_weights': 4.063,
     'L1_attn_b_qkv': 5.271,
     'L1_ffn_b1_l': 4.551,
     'L1_ffn_b1_h': 6.013,
     'L1_ffn_b2_h': 4.28}
    for name, (base, spread) in spreads.items():
        noise = np.random.default_rng([zlib.crc32(name.encode()), seed]).standard_normal(out[name].shape)
        drawn = base * np.exp(spread * noise) if base else spread * noise
        out[name] = jnp.asarray(drawn.astype(out[name].dtype))
    for name, factor in factors.items():
        out[name] = (out[name] * factor).astype(out[name].dtype)
    return out
```

```python
import concourse.bass as bass
from concourse import mybir
from contextlib import ExitStack
import numpy as np

fp32 = mybir.dt.float32
bf16 = mybir.dt.bfloat16
int32 = mybir.dt.int32
ALU = mybir.AluOpType
ACT = mybir.ActivationFunctionType
AX = mybir.AxisListType

B, S, D = 8, 256, 128
P = 128
NT = S // P
H, DH = 16, 8
G = 4
NG = H // G
EPS = 1e-5
L = 4
FT = 4
NF = 8
NC = 5
KEFF = 144.0
TOPK = 128
BLOCKS = (25, 24)
LEVEL0 = 62.0
SHIFT_AT = 2
TOP = 80.0
LN2 = float(np.log(2.0))
SELF = (0, 2)
ONES_BF16 = 1.0019378662109375


def build(nc, t):
    ctx = ExitStack()
    with ctx:
        def sb(name, shape, dt=fp32):
            return ctx.enter_context(nc.sbuf_tensor(name + "_sb", shape, dt))

        def ps(name, shape, dt=fp32):
            return ctx.enter_context(nc.psum_tensor(name, shape, dt))

        def sem(name):
            return ctx.enter_context(nc.semaphore(name))

        x_all = sb("x_all", [P, B * NT, D])
        ctxT = sb("ctxT", [P, B * S])
        ident = sb("ident", [P, P])
        ident_bf = sb("ident_bf", [P, P], bf16)
        minus_half = sb("minus_half", [P, FT])
        w_att = sb("w_att", [P, L, 4, D])
        b_qk = sb("b_qk", [P, L, 2])
        b_vo = sb("b_vo", [P, L, 2, D])

        stats = sb("stats", [P, 2, NT, 6])
        mv = sb("mv", [P, 2, NT, 2])
        rstd = sb("rstd", [P, 2, NT])
        xn = sb("xn", [P, 2, NT, D])
        xnT = sb("xnT", [P, 2, S])
        qkf = sb("qkf", [P, 2, 2, S])
        rest = sb("rest", [P, 2, S])
        parts = sb("parts", [P, 2, 2, 3, S], bf16)
        stack = sb("stack", [P, 3, 2, H, S], bf16)
        v_aug = sb("v_aug", [P, 4, NT, H, 32])
        negmax = sb("negmax", [P, 2, NT, H], bf16)
        maxrow = sb("maxrow", [DH, 2, 2, S], bf16)
        probT = sb("probT", [P, 8, NT, S])
        uT = sb("uT", [P, 2, NG, S])
        den_inv = sb("den_inv", [P, NT, H])
        o_tok = sb("o_tok", [P, 2, NT, D])
        oT = sb("oT", [P, 2, S])

        v_one = sb("v_one", [P, 2, NT, D])
        negbias = sb("negbias", [P, 2, NT])
        negbias_raw = sb("negbias_raw", [P, 2, NT])
        prob = sb("prob", [P, 2, NT, S])
        probT1 = sb("probT1", [P, 2, NT * S])
        den = sb("den", [P, 2, NT])
        den_inv1 = sb("den_inv1", [P, 2, NT])
        causal = sb("causal", [P, P])

        f_stats = sb("f_stats", [P, FT, 6])
        f_mv = sb("f_mv", [P, FT, 2])
        f_rstd = sb("f_rstd", [P, FT])
        f_xn = sb("f_xn", [P, FT, D])
        f_xnT = sb("f_xnT", [P, FT * P])
        f_hT = sb("f_hT", [P, NF, FT * P])
        f_w1 = sb("f_w1", [P, NF, P])
        f_w2 = sb("f_w2", [P, NF, D])
        f_ew = sb("f_ew", [P, FT, 2])
        f_wsum = sb("f_wsum", [P, FT])

        route = sb("route", [P, D])
        s_tok = sb("s_tok", [P, B, NT])
        z = sb("z", [P, 2, NT, D])
        z_stats = sb("z_stats", [P, 2, NT, 6])
        z_mv = sb("z_mv", [P, B, NT, 2])
        z_rstd = sb("z_rstd", [P, B, NT])
        s_junk = sb("s_junk", [P, D])
        rnorm = sb("rnorm", [P, B, NT])
        xr = sb("xr", [P, 2, NT, D])
        xrT = sb("xrT", [P, B * S])
        d_w1 = sb("d_w1", [P, NC, P])
        d_b1 = sb("d_b1", [P, NC])
        d_w2 = sb("d_w2", [P, NC, D])
        d_b2 = sb("d_b2", [P, 2, D])
        gamma = sb("gamma", [P, 2])
        stack_free = stack[:, :, :, :, :].rearrange("p s a h n -> p (s a h n)").bitcast(fp32)
        d_hT = stack_free[:, 0:8 * NC * P].rearrange("p (u f q) -> p u f q", u=2, f=NC)
        heavy = stack_free[:, 8 * NC * P:8 * NC * P + B * S].rearrange("p (t d) -> p t d", d=D)

        s_row = sb("s_row", [B, S])
        shifted = sb("shifted", [B, S])
        e_row = sb("e_row", [B, S])
        k_inv = sb("k_inv", [B, S])
        min_junk = sb("min_junk", [B, S])
        level = sb("level", [B, 2])
        exponent = sb("exponent", [B, 1], int32)
        expo_f = sb("expo_f", [B, 1])
        shift = sb("shift", [B, 1])
        log_level = sb("log_level", [B, 1])
        score = sb("score", [B, S])
        work = sb("work", [B, 2, S])
        top8 = sb("top8", [B, 8])
        weight = sb("weight", [B, S])
        w_tok = sb("w_tok", [P, NT, B])

        s1_ps = [ps(f"s1_ps{i}", [P, NT, S]) for i in range(2)]
        s2_ps = [ps(f"s2_ps{i}", [P, NT, S]) for i in range(2)]
        pv_ps = [ps(f"pv_ps{i}", [P, 2, S]) for i in range(2)]
        prep_ps = ps("prep_ps", [P, 2, S])
        out_ps = ps("out_ps", [P, 512])
        prep_bf = prep_ps[:, :, :].bitcast(bf16)

        scratch = [nc.dram_tensor(f"scratch{i}", [2, 3, DH, H, S], bf16).ap() for i in range(2)]

        x_in, ctx_in, w_in = sem("x_in"), sem("ctx_in"), sem("w_in")
        zeroed = [sem(f"zeroed{i}") for i in range(3)]
        pool_zeroed = sem("pool_zeroed")
        const_ready, pool_const = sem("const_ready"), sem("pool_const")
        one_row = sem("one_row")
        stats_ready, mv_ready, rstd_step, rstd_ready, xn_ready = (
            sem("stats_ready"), sem("mv_ready"), sem("rstd_step"), sem("rstd_ready"), sem("xn_ready"))
        xnT_psum, xnT_ready, qk_psum, qk_ready = sem("xnT_psum"), sem("xnT_ready"), sem("qk_psum"), sem("qk_ready")
        part1_ready, rest_ready, parts_ready = sem("part1_ready"), sem("rest_ready"), sem("parts_ready")
        v_psum, v_ready = sem("v_psum"), sem("v_ready")
        scratch_in = [sem(f"scratch_in{i}") for i in range(2)]
        stacked = [sem(f"stacked{i}") for i in range(3)]
        s1_psum, max_ready, maxT_psum, maxT_ready = sem("s1_psum"), sem("max_ready"), sem("maxT_psum"), sem("maxT_ready")
        max_in = [[sem(f"max_in{i}{hf}") for hf in range(2)] for i in range(3)]
        s2_psum, exp_ready, pv_psum, uT_ready = sem("s2_psum"), sem("exp_ready"), sem("pv_psum"), sem("uT_ready")
        u_psum, inv_ready, o_ready = sem("u_psum"), sem("inv_ready"), sem("o_ready")
        oT_psum, oT_ready, y_psum = sem("oT_psum"), sem("oT_ready"), sem("y_psum")
        biased, x_ready = sem("biased"), sem("x_ready")
        causal_step = sem("causal_step")
        sc_psum, mask_step, negmax1_ready, bias_ready, prob_ready = (
            sem("sc_psum"), sem("mask_step"), sem("negmax1_ready"), sem("bias_ready"), sem("prob_ready"))
        probT_psum, probT_ready, o1_psum, inv1_ready, x_mid = (
            sem("probT_psum"), sem("probT_ready"), sem("o1_psum"), sem("inv1_ready"), sem("x_mid"))
        f_in, f_stats_ready, f_mv_ready, f_rstd_ready, f_xn_ready = (
            sem("f_in"), sem("f_stats_ready"), sem("f_mv_ready"), sem("f_rstd_ready"), sem("f_xn_ready"))
        f_xnT_psum, f_xnT_ready, f_h_psum, f_h_ready, f_y_psum, f_wsum_ready, f_x = (
            sem("f_xnT_psum"), sem("f_xnT_ready"), sem("f_h_psum"), sem("f_h_ready"), sem("f_y_psum"), sem("f_wsum_ready"), sem("f_x"))
        d_in, d_folded, s_tok_ready, z_stats_ready, z_mv_ready, z_ready, rn_step, rn_ready = (
            sem("d_in"), sem("d_folded"), sem("s_tok_ready"), sem("z_stats_ready"), sem("z_mv_ready"), sem("z_ready"), sem("rn_step"), sem("rn_ready"))
        xr_ready, xrT_psum, xrT_ready, light_bias = sem("xr_ready"), sem("xrT_psum"), sem("xrT_ready"), sem("light_bias")
        d_h_psum, d_h_ready, d_y_psum, light_done, heavy_copied, heavy_ready = (
            sem("d_h_psum"), sem("d_h_ready"), sem("d_y_psum"), sem("light_done"), sem("heavy_copied"), sem("heavy_ready"))
        shift_step, top_step = sem("shift_step"), sem("top_step")
        s_row_psum, s_row_ready, chain, shifted_ready, e_ready, log_ready = (
            sem("s_row_psum"), sem("s_row_ready"), sem("chain"), sem("shifted_ready"), sem("e_ready"), sem("log_ready"))
        score_ready, weight_ready, w_psum, w_ready, x_final = (
            sem("score_ready"), sem("weight_ready"), sem("w_psum"), sem("w_ready"), sem("x_final"))
        out_done = [sem(f"out_done{i}") for i in range(4)]

        block = ctx.enter_context(nc.Block())
        MANY = (0, B)

        def has(n, lo):
            return lo <= n < lo + B

        def item(m):
            return m if m < B else m + 2 * B

        def many(n):
            return n if n < B else n - 2 * B

        out_ps2 = out_ps[:, :].rearrange("p (t q) -> p t q", q=S)

        def heavy_bank(b):
            return s1_ps[b % 2][:, 0, :].rearrange("p (t d) -> p t d", d=D)

        def light_bank(b):
            return (prep_ps, out_ps2)[b % 2][:, 0, :].rearrange("p (t d) -> p t d", d=D)

        @block.sync
        def _(sp):
            for c in range(4):
                sp.dma_start(x_all[:, 4 * c:4 * c + 4, :], t["x"].rearrange("b (t p) d -> p (b t) d", p=P)[:, 4 * c:4 * c + 4, :]).then_inc(x_in, 16)
            sp.dma_start(w_att[:, :, :, :], t["w_att"].rearrange("l w p d -> p l w d")).then_inc(w_in, 16)
            sp.dma_start(b_qk[:, :, :], t["b_qk"]).then_inc(w_in, 16)
            sp.dma_start(b_vo[:, :, :, :].rearrange("p l w d -> p (l w d)"), t["b_vo"].rearrange("l w d -> (l w d)").partition_broadcast(P)).then_inc(w_in, 16)
            sp.dma_start(ctxT[:, :], t["ctxT"]).then_inc(ctx_in, 16)
            for dst, name in ((f_w1[:, :, :], "f_w1"), (f_w2[:, :, :], "f_w2"), (f_ew[:, :, :], "f_ew")):
                sp.dma_start(dst, t[name]).then_inc(f_in, 16)
            for dst, name in ((d_w1[:, :, :], "d_w1"), (d_w2[:, :, :], "d_w2"), (d_b1[:, :], "d_b1"), (gamma[:, :], "gamma")):
                sp.dma_start(dst, t[name]).then_inc(d_in, 16)
            sp.dma_start(d_b2[:, :, :].rearrange("p l d -> p (l d)"), t["d_b2"].rearrange("l d -> (l d)").partition_broadcast(P)).then_inc(d_in, 16)
            sp.dma_start(route[:, :], t["route"].partition_broadcast(P)).then_inc(d_in, 16)

            def bounce(n):
                u, s3 = n % 2, n % 3
                sp.wait_ge(parts_ready, n + 1)
                if n >= 2:
                    sp.wait_ge(stacked[(n - 2) % 3], 96 * ((n - 2) // 3 + 1))
                sp.dma_start(scratch[u].rearrange("a j d h n -> (d h) (a j) n"),
                             parts[:, u].rearrange("p a j n -> p (a j) n")).then_inc(scratch_in[u], 16)

            def load_stack(n):
                u, s3 = n % 2, n % 3
                sp.wait_ge(scratch_in[u], 16 * (n // 2 + 1))
                if n < 3:
                    sp.wait_ge(zeroed[s3], 2)
                    sp.wait_ge(pool_zeroed, n + 1)
                if n >= 3:
                    sp.wait_ge(s2_psum, H * (n - 2))
                for r, m, j in ((0, 3, 0), (3, 2, 1), (5, 1, 2)):
                    sp.dma_start(stack[DH * r:DH * (r + m), s3, 1], scratch[u][1, 0:m].rearrange("j d h n -> (j d) h n")
                                 ).then_inc(stacked[s3], 16)
                    sp.dma_start(stack[DH * r:DH * (r + m), s3, 0].rearrange("p h n -> p (h n)"),
                                 scratch[u][0, j:j + 1].rearrange("j d h n -> j d (h n)").broadcast_to([m, DH, H * S])
                                 ).then_inc(stacked[s3], 16)

            def place_max(n, hf):
                u, s3 = n % 2, n % 3
                sp.wait_ge(maxT_ready, 2 * n + hf + 1)
                sp.dma_start(stack[96:97, s3, 0, 8 * hf:8 * hf + 8, :],
                             maxrow[:, u, hf, :]).then_inc(max_in[s3][hf], 16)

            for lo in MANY:
                for i in range(lo - 3, lo + B):
                    if has(i + 2, lo):
                        load_stack(i + 2)
                    if has(i, lo):
                        place_max(i, 1)
                    if has(i + 1, lo):
                        place_max(i + 1, 0)
                    if has(i + 3, lo):
                        bounce(i + 3)
            for c in range(4):
                sp.wait_ge(x_final, 4 * c + 4)
                sp.dma_start(t["out"].rearrange("b (t p) d -> p (b t) d", p=P)[:, 4 * c:4 * c + 4, :],
                             x_all[:, 4 * c:4 * c + 4, :]).then_inc(out_done[c], 16)
            for c in range(4):
                sp.wait_ge(out_done[c], 16)

        @block.gpsimd
        def _(pool):
            pool.memset(ident[:, :], 0.0).then_inc(pool_const, 1)
            pool.memset(minus_half[:, :], -0.5).then_inc(pool_const, 1)
            pool.wait_ge(pool_const, 2)
            pool.affine_select(out=ident[:, :], in_=ident[:, :], compare_op=ALU.not_equal, fill=1.0, base=0,
                               pattern=[[-1, P]], channel_multiplier=1).then_inc(pool_const, 1)
            pool.wait_ge(pool_const, 3)
            pool.tensor_copy(ident_bf[:, :], ident[:, :]).then_inc(pool_const, 1)
            pool.memset(v_aug[:, :, :, :, :].rearrange("p s t h d -> p (s t h d)"), 0.0).then_inc(pool_const, 1)
            pool.wait_ge(pool_const, 5)
            pool.memset(v_aug[:, :, :, :, DH:DH + 1].rearrange("p s t h d -> p (s t h) d"), 1.0).then_inc(const_ready, 1)
            pool.wait_ge(w_in, 48)

            pool.memset(causal[:, :], 0.0).then_inc(causal_step, 1)
            pool.wait_ge(causal_step, 1)
            pool.affine_select(out=causal[:, :], in_=causal[:, :], compare_op=ALU.is_ge, fill=-1e30, base=0,
                               pattern=[[-1, P]], channel_multiplier=1).then_inc(causal_step, 1)

            def rstd_step_(n):
                u = n % 2
                pool.wait_ge(mv_ready, NT * (n + 1))
                pool.tensor_scalar(rstd[:, u, :], mv[:, u, :, 1], EPS, None, ALU.add).then_inc(rstd_step, 1)
                pool.wait_ge(rstd_step, n + 1)
                pool.tensor_tensor(rstd[:, u, :], rstd[:, u, :], minus_half[:, 0:NT], ALU.pow).then_inc(rstd_ready, 1)

            def add_bias(m):
                n = item(m)
                b, l = n % B, n // B
                pool.wait_ge(xn_ready, n + 1)
                x2 = x_all[:, NT * b:NT * b + NT, :]
                pool.tensor_tensor(x2, x2, b_vo[:, l, 1:2, :].broadcast_to([P, NT, D]), ALU.add).then_inc(biased, 1)

            def split(m):
                n, u = m, m % 2
                pool.wait_ge(part1_ready, n + 1)
                pool.tensor_tensor(rest[:, :, :], qkf[:, u], parts[:, u, :, 0, :], ALU.subtract).then_inc(rest_ready, 1)
                pool.tensor_tensor(parts[:, u, :, 1, :], qkf[:, u], parts[:, u, :, 0, :], ALU.subtract).then_inc(rest_ready, 1)
                pool.wait_ge(rest_ready, 2 * n + 2)
                pool.tensor_tensor(parts[:, u, :, 2, :], rest[:, :, :], parts[:, u, :, 1, :], ALU.subtract).then_inc(parts_ready, 1)
                pool.wait_ge(parts_ready, n + 1)

            def z_norms(b):
                if b == 0:
                    pool.wait_ge(d_in, 96)
                pool.wait_ge(z_mv_ready, NT * (b + 1))
                rs, rn, var = z_rstd[:, b, :], rnorm[:, b, :], z_mv[:, b, :, 1]
                pool.tensor_scalar(rs, var, EPS, None, ALU.add).then_inc(rn_step, 1)
                pool.wait_ge(rn_step, 5 * b + 1)
                pool.tensor_tensor(rs, rs, minus_half[:, 0:NT], ALU.pow).then_inc(rn_step, 1)
                pool.wait_ge(rn_step, 5 * b + 2)
                pool.tensor_tensor(rn, var, rs, ALU.mult).then_inc(rn_step, 1)
                pool.wait_ge(rn_step, 5 * b + 3)
                pool.tensor_tensor(rn, rn, rs, ALU.mult).then_inc(rn_step, 1)
                pool.wait_ge(rn_step, 5 * b + 4)
                pool.tensor_scalar(rn, rn, float(D), 1e-24, ALU.mult, ALU.max).then_inc(rn_step, 1)
                pool.wait_ge(rn_step, 5 * b + 5)
                pool.tensor_tensor(rn, rn, minus_half[:, 0:NT], ALU.pow).then_inc(rn_ready, 1)
                pool.wait_ge(z_ready, b + 1)
                x2 = x_all[:, NT * b:NT * b + NT, :]
                pool.tensor_tensor(x2, x2, d_b2[:, 1:2, :].broadcast_to([P, NT, D]), ALU.add).then_inc(light_bias, 1)

            def f_rstd_step():
                pool.wait_ge(f_mv_ready, FT)
                pool.tensor_scalar(f_rstd[:, :], f_mv[:, :, 1], EPS, None, ALU.add).then_inc(f_rstd_ready, 1)
                pool.wait_ge(f_rstd_ready, 1)
                pool.tensor_tensor(f_rstd[:, :], f_rstd[:, :], minus_half[:, :], ALU.pow).then_inc(f_rstd_ready, 1)

            for lo in MANY:
                if lo == B:
                    for n in range(B, 3 * B):
                        rstd_step_(n)
                        if n == B + 6:
                            f_rstd_step()
                for n in range(lo, lo + B):
                    rstd_step_(item(n))
                    add_bias(n)
                    if lo == B and n >= lo + 5:
                        z_norms(n - lo - 5)
                    if n < 3:
                        pool.wait_ge(biased, n + 1)
                        pool.memset(stack[64:96, n].rearrange("p a h n -> p (a h n)").bitcast(fp32), 0.0).then_inc(pool_zeroed, 1)
                        pool.wait_ge(pool_zeroed, n + 1)
                    split(n)

            for b in range(3, B):
                z_norms(b)
            for b in range(B):
                pool.wait_ge(heavy_copied, b + 1)
                h2 = heavy[:, NT * b:NT * b + NT, :]
                pool.tensor_tensor(h2, h2, d_b2[:, 0:1, :].broadcast_to([P, NT, D]), ALU.add).then_inc(heavy_ready, 1)

        @block.scalar
        def _(act):
            def exps(n, h):
                c = H * n + h
                act.wait_ge(s2_psum, c + 1)
                if c >= 8:
                    act.wait_ge(pv_psum, c // G - 1)
                act.activation(probT[:, c % 8], s2_ps[c % 2][:, :, :], ACT.Exp, scale=DH ** -0.5).then_inc(exp_ready, 1)

            def xnT_copy(n):
                bank = pv_ps[0] if B <= n < 3 * B else prep_ps
                act.wait_ge(xnT_psum, n + 1)
                if n >= 2:
                    act.wait_ge(v_psum, n - 1)
                act.activation(xnT[:, n % 2, :], bank[:, 0, :], ACT.Copy).then_inc(xnT_ready, 1)

            def qk_copy(n):
                act.wait_ge(qk_psum, n + 1)
                if n >= 2:
                    if B <= n - 2 < 3 * B:
                        act.wait_ge(sc_psum, n - 2 - B + 1)
                    else:
                        act.wait_ge(parts_ready, many(n - 2) + 1)
                for a in range(2):
                    act.activation(qkf[:, n % 2, a, :], prep_ps[:, a, :], ACT.Identity,
                                   bias=b_qk[:, n // B, a:a + 1]).then_inc(qk_ready, 1)

            def max_copy(n, hf):
                act.wait_ge(maxT_psum, 2 * n + hf + 1)
                if n >= 2:
                    act.wait_ge(max_in[(n - 2) % 3][hf], 16 * ((n - 2) // 3 + 1))
                act.activation(maxrow[:, n % 2, hf, :], prep_bf[0:8, 0, 0:S], ACT.Copy).then_inc(maxT_ready, 1)

            def u_copy(n, gb):
                act.wait_ge(pv_psum, NG * n + 2 * gb + 2)
                if n >= 2:
                    act.wait_ge(u_psum, 2 * (n - 1))
                act.activation(uT[:, n % 2, 2 * gb:2 * gb + 2, :], pv_ps[gb][:, :, :], ACT.Copy).then_inc(uT_ready, 1)

            def xrT_copy(b):
                act.wait_ge(xrT_psum, b + 1)
                act.activation(xrT[:, S * b:S * b + S], prep_ps[:, 0, :], ACT.Copy).then_inc(xrT_ready, 1)

            def oT_copy(n):
                act.wait_ge(oT_psum, n + 1)
                if n >= 2:
                    act.wait_ge(y_psum, n - 1)
                act.activation(oT[:, n % 2, :], out_ps[:, 0:S], ACT.Copy).then_inc(oT_ready, 1)

            def softmax_exps(n):
                r = n - B
                act.wait_ge(bias_ready, r + 1)
                if r >= 2:
                    act.wait_ge(probT_psum, r - 1)
                for k in range(NT):
                    w = P if n >= 2 * B and k == 0 else S
                    act.activation(prob[:, r % 2, k, 0:w], s1_ps[r % 2][:, k, 0:w], ACT.Exp, bias=negbias[:, r % 2, k:k + 1],
                                   scale=D ** -0.5, accum_out=den[:, r % 2, k:k + 1]).then_inc(prob_ready, 1)

            def probT_copy(n):
                r = n - B
                w = 3 * P if n >= 2 * B else 4 * P
                act.wait_ge(probT_psum, r + 1)
                if r >= 2:
                    act.wait_ge(o1_psum, r - 1)
                act.activation(probT1[:, r % 2, 0:w], s2_ps[r % 2][:, :, :].rearrange("p t q -> p (t q)")[:, 0:w],
                               ACT.Copy).then_inc(probT_ready, 1)

            def f_acts():
                act.wait_ge(f_xnT_psum, 1)
                act.activation(f_xnT[:, :], prep_ps[:, :, :].rearrange("p t q -> p (t q)"), ACT.Copy).then_inc(f_xnT_ready, 1)
                for f in range(NF):
                    act.wait_ge(f_h_psum, f + 1)
                    act.activation(f_hT[:, f, :], s2_ps[f % 2][:, :, :].rearrange("p t q -> p (t q)"),
                                   ACT.Gelu_apprx_tanh).then_inc(f_h_ready, 1)

            act.wait_ge(w_in, 48)
            for lo in MANY:
                if lo == B:
                    for i in range(B - 3, 3 * B + 1):
                        if B <= i - 1 < 3 * B:
                            probT_copy(i - 1)
                        if i == B + 4:
                            f_acts()
                        if B <= i < 3 * B:
                            softmax_exps(i)
                        if B <= i + 1 < 3 * B:
                            qk_copy(i + 1)
                        if B <= i + 2 < 3 * B:
                            xnT_copy(i + 2)
                for i in range(lo - 3, lo + B + 1 + lo // B):
                    for h in range(H):
                        if has(i, lo):
                            exps(i, h)
                        if h == 3 and has(i, lo):
                            max_copy(i, 1)
                        if h == 3 and has(i - 1, lo):
                            u_copy(i - 1, 1)
                        if h == 6 and has(i + 3, lo):
                            xnT_copy(item(i + 3))
                        if h == 9 and has(i + 3, lo):
                            qk_copy(item(i + 3))
                        if h == 11 and has(i, lo):
                            u_copy(i, 0)
                        if h == 11 and has(i + 1, lo):
                            max_copy(i + 1, 0)
                        if h == 12 and has(i - 1, lo):
                            oT_copy(i - 1)
                        if h == 0 and lo == B and has(i - 3, lo):
                            xrT_copy(i - 3 - B)

            def shift_exp(j):
                act.wait_ge(shifted_ready, j + 1)
                act.activation(e_row[:, :], shifted[:, :], ACT.Exp).then_inc(e_ready, 1)

            def branch_copies(q):
                for b in (2 * q, 2 * q + 1):
                    act.wait_ge(d_y_psum, 2 * b + 1)
                    act.activation(heavy[:, NT * b:NT * b + NT, :], heavy_bank(b), ACT.Copy).then_inc(heavy_copied, 1)
                    act.wait_ge(d_y_psum, 2 * b + 2)
                    act.activation(x_all[:, NT * b:NT * b + NT, :], light_bank(b), ACT.Copy).then_inc(light_done, 1)

            act.wait_ge(d_in, 96)
            xrT_copy(B - 1)
            shift_exp(0)
            for q in range(4):
                for f in range(NC):
                    c = NC * q + f
                    act.wait_ge(d_h_psum, c + 1)
                    if q >= 2:
                        act.wait_ge(d_y_psum, 4 * (q - 1))
                    act.activation(d_hT[:, q % 2, f, :], s2_ps[c % 2][:, :, :].rearrange("p t q -> p (t q)"), ACT.Gelu,
                                   bias=d_b1[:, f:f + 1]).then_inc(d_h_ready, 1)
                if q >= 1:
                    branch_copies(q - 1)
                if q == SHIFT_AT:
                    shift_exp(1)
            branch_copies(3)
            act.wait_ge(chain, sum(BLOCKS) + 4)
            act.activation(log_level[:, :], level[:, sum(BLOCKS) % 2:sum(BLOCKS) % 2 + 1], ACT.Ln).then_inc(log_ready, 1)
            act.wait_ge(shifted_ready, 3)
            act.activation(score[:, :], shifted[:, :], ACT.Exp).then_inc(score_ready, 1)

        @block.vector
        def _(dve):
            def zero_low(s3):
                dve.memset(stack[32:64, s3].rearrange("p a h n -> p (a h n)").bitcast(fp32), 0.0).then_inc(zeroed[s3], 1)
                dve.memset(stack[96:97, s3, 1].rearrange("p h n -> p (h n)").bitcast(fp32), ONES_BF16).then_inc(zeroed[s3], 1)

            dve.wait_ge(x_in, 64)
            dve.wait_ge(w_in, 48)

            def ln_stats(n):
                u, b, l = n % 2, n % B, n // B
                if l == 1:
                    dve.wait_ge(x_ready, b + 1)
                if l == 2:
                    dve.wait_ge(x_mid, b + 1)
                    if b < FT // NT:
                        dve.wait_ge(f_x, FT)
                if l == 3:
                    dve.wait_ge(x_mid, B + b + 1)
                for k in range(NT):
                    dve.bn_stats(stats[:, u, k, :], x_all[:, NT * b + k, :]).then_inc(stats_ready, 1)
                for k in range(NT):
                    dve.wait_ge(stats_ready, NT * n + k + 1)
                    dve.bn_aggr(mv[:, u, k, :], stats[:, u, k, :]).then_inc(mv_ready, 1)

            def ln_apply(n):
                u, b = n % 2, n % B
                dve.wait_ge(rstd_ready, n + 1)
                if n >= 2:
                    dve.wait_ge(xnT_psum, n - 1)
                for k in range(NT):
                    i = dve.tensor_scalar(xn[:, u, k, :], x_all[:, NT * b + k, :], mv[:, u, k, 0:1], rstd[:, u, k:k + 1],
                                          ALU.subtract, ALU.mult)
                    if k == NT - 1:
                        i.then_inc(xn_ready, 1)

            def part1(m):
                u = m % 2
                dve.wait_ge(qk_ready, 2 * item(m) + 2)
                if m >= 2:
                    dve.wait_ge(scratch_in[u], 16 * (m // 2))
                dve.tensor_copy(parts[:, u, :, 0, :], qkf[:, u]).then_inc(part1_ready, 1)

            def v_copy(m):
                n = item(m)
                dve.wait_ge(v_psum, n + 1)
                if m == 0:
                    dve.wait_ge(const_ready, 1)
                if m >= 4:
                    dve.wait_ge(pv_psum, NG * (m - 3))
                for k in range(NT):
                    i = dve.tensor_tensor(v_aug[:, m % 4, k, :, 0:DH], prep_ps[:, 0, k * D:(k + 1) * D].rearrange("p (h d) -> p h d", d=DH),
                                          b_vo[:, n // B, 0, :].rearrange("p (h d) -> p h d", d=DH), ALU.add)
                    if k == NT - 1:
                        i.then_inc(v_ready, 1)

            def row_max(n, h):
                c = H * n + h
                dve.wait_ge(s1_psum, c + 1)
                if h == 0 and n >= 2:
                    dve.wait_ge(maxT_psum, 2 * (n - 1))
                dve.tensor_reduce(negmax[:, n % 2, :, h], s1_ps[c % 2][:, :, :], axis=AX.X, op=ALU.max,
                                  negate=True).then_inc(max_ready, 1)

            def normalise(n, k):
                u = n % 2
                dve.wait_ge(u_psum, 2 * n + k + 1)
                if n >= 2 and k == 0:
                    dve.wait_ge(oT_psum, n - 1)
                u4 = out_ps[:, :].rearrange("p (h d) -> p h d", d=32)
                dve.reciprocal(den_inv[:, k, :], u4[:, :, DH]).then_inc(inv_ready, 1)
                dve.wait_ge(inv_ready, 2 * n + k + 1)
                dve.tensor_tensor(o_tok[:, u, k, :].rearrange("p (h d) -> p h d", d=DH), u4[:, :, 0:DH],
                                  den_inv[:, k, :].unsqueeze(2).broadcast_to([P, H, DH]), ALU.mult).then_inc(o_ready, 1)

            def residual(n):
                b = n % B
                dve.wait_ge(y_psum, n + 1)
                dve.wait_ge(biased, n + 1)
                x2 = x_all[:, NT * b:NT * b + NT, :]
                dve.tensor_tensor(x2, out_ps[:, 0:S].rearrange("p (t d) -> p t d", d=D), x2, ALU.add).then_inc(x_ready, 1)

            def v_copy_one(n):
                r = n - B
                dve.wait_ge(v_psum, n + 1)
                if r >= 2:
                    dve.wait_ge(o1_psum, r - 1)
                dve.tensor_tensor(v_one[:, r % 2], pv_ps[1][:, 0, :].rearrange("p (t d) -> p t d", d=D),
                                  b_vo[:, n // B, 0:1, :].broadcast_to([P, NT, D]), ALU.add).then_inc(v_ready, 1)

            def softmax_bias(n):
                r = n - B
                sc = s1_ps[r % 2]
                dve.wait_ge(sc_psum, r + 1)
                if n >= 2 * B:
                    for k in range(NT):
                        dve.tensor_tensor(sc[:, k, k * P:(k + 1) * P], sc[:, k, k * P:(k + 1) * P], causal[:, :],
                                          ALU.add).then_inc(mask_step, 1)
                    dve.wait_ge(mask_step, NT * (n - 2 * B + 1))
                    dve.tensor_reduce(negbias_raw[:, r % 2, 0:1], sc[:, 0, 0:P], axis=AX.X, op=ALU.max,
                                      negate=True).then_inc(negmax1_ready, 1)
                    dve.tensor_reduce(negbias_raw[:, r % 2, 1:2], sc[:, 1, :], axis=AX.X, op=ALU.max,
                                      negate=True).then_inc(negmax1_ready, 1)
                else:
                    dve.tensor_reduce(negbias_raw[:, r % 2, :], sc[:, :, :], axis=AX.X, op=ALU.max,
                                      negate=True).then_inc(negmax1_ready, 2)
                dve.wait_ge(negmax1_ready, 2 * (r + 1))
                if r >= 2:
                    dve.wait_ge(prob_ready, NT * (r - 1))
                dve.tensor_scalar(negbias[:, r % 2, :], negbias_raw[:, r % 2, :], D ** -0.5, None,
                                  ALU.mult).then_inc(bias_ready, 1)

            def residual_one(n):
                r, b = n - B, n % B
                dve.wait_ge(prob_ready, NT * (r + 1))
                dve.reciprocal(den_inv1[:, r % 2, :], den[:, r % 2, :]).then_inc(inv1_ready, 1)
                dve.wait_ge(inv1_ready, r + 1)
                dve.wait_ge(o1_psum, r + 1)
                for k in range(NT):
                    i = dve.scalar_tensor_tensor(out=x_all[:, NT * b + k, :], in0=out_ps[:, k * D:(k + 1) * D],
                                                 scalar=den_inv1[:, r % 2, k:k + 1], in1=x_all[:, NT * b + k, :],
                                                 op0=ALU.mult, op1=ALU.add)
                i.then_inc(x_mid, 1)

            def f_norm():
                dve.wait_ge(x_mid, FT // NT)
                for k in range(FT):
                    dve.bn_stats(f_stats[:, k, :], x_all[:, k, :]).then_inc(f_stats_ready, 1)
                dve.wait_ge(f_stats_ready, FT)
                for k in range(FT):
                    dve.bn_aggr(f_mv[:, k, :], f_stats[:, k, :]).then_inc(f_mv_ready, 1)
                dve.wait_ge(f_rstd_ready, 2)
                for k in range(FT):
                    dve.tensor_scalar(f_xn[:, k, :], x_all[:, k, :], f_mv[:, k, 0:1], f_rstd[:, k:k + 1],
                                      ALU.subtract, ALU.mult).then_inc(f_xn_ready, 1)
                dve.wait_ge(f_in, 48)
                dve.tensor_tensor(f_wsum[:, :], f_ew[:, :, 0], f_ew[:, :, 1], ALU.add).then_inc(f_wsum_ready, 1)

            def f_residual():
                dve.wait_ge(f_wsum_ready, 1)
                dve.wait_ge(f_y_psum, 1)
                for k in range(FT):
                    dve.scalar_tensor_tensor(out=x_all[:, k, :], in0=out_ps[:, k * D:(k + 1) * D], scalar=f_wsum[:, k:k + 1],
                                             in1=x_all[:, k, :], op0=ALU.mult, op1=ALU.add).then_inc(f_x, 1)

            def z_norm_stats(b):
                dve.wait_ge(x_ready, B + b + 1)
                for k in range(NT):
                    dve.bn_stats(z_stats[:, b % 2, k, :], x_all[:, NT * b + k, :]).then_inc(z_stats_ready, 1)
                for k in range(NT):
                    dve.wait_ge(z_stats_ready, NT * b + k + 1)
                    dve.bn_aggr(z_mv[:, b, k, :], z_stats[:, b % 2, k, :]).then_inc(z_mv_ready, 1)

            def z_apply(b):
                dve.wait_ge(rn_ready, b + 1)
                for k in range(NT):
                    i = dve.tensor_scalar(z[:, b % 2, k, :], x_all[:, NT * b + k, :], z_mv[:, b, k, 0:1], z_rstd[:, b, k:k + 1],
                                          ALU.subtract, ALU.mult)
                i.then_inc(z_ready, 1)

            def z_route(b):
                if b == 0:
                    dve.wait_ge(d_in, 96)
                dve.wait_ge(z_ready, b + 1)
                for k in range(NT):
                    c = NT * b + k
                    if c >= 1:
                        dve.wait_ge(s_tok_ready, c)
                    dve.scalar_tensor_tensor(out=s_junk[:, :], in0=z[:, b % 2, k, :], scalar=1.0, in1=route[:, :], op0=ALU.mult,
                                             op1=ALU.mult, accum_out=s_tok[:, b, k:k + 1]).then_inc(s_tok_ready, 1)
                if b >= 2:
                    dve.wait_ge(xrT_psum, b - 1)
                for k in range(NT):
                    i = dve.tensor_scalar(xr[:, b % 2, k, :], z[:, b % 2, k, :], rnorm[:, b, k:k + 1], None, ALU.mult)
                i.then_inc(xr_ready, 1)

            def fold_gamma():
                dve.wait_ge(d_in, 96)
                dve.tensor_scalar(d_w1[:, 0:NC - 1, :], d_w1[:, 0:NC - 1, :], gamma[:, 0:1], D ** 0.5, ALU.mult, ALU.mult).then_inc(d_folded, 1)
                dve.tensor_scalar(d_w1[:, NC - 1, :], d_w1[:, NC - 1, :], gamma[:, 1:2], D ** 0.5, ALU.mult, ALU.mult).then_inc(d_folded, 1)
                dve.memset(k_inv[:, :], 1.0 / KEFF).then_inc(s_row_ready, 1)
                dve.memset(level[:, 0:1], S / KEFF * float(np.exp(LEVEL0))).then_inc(chain, 1)

            for lo in MANY:
                if lo == B:
                    fold_gamma()
                    for i in range(B - 3, 3 * B + 1):
                        if i == B + 4:
                            f_residual()
                        if B <= i + 3 < 3 * B:
                            ln_stats(i + 3)
                        if B <= i < 3 * B:
                            softmax_bias(i)
                        if B <= i - 1 < 3 * B:
                            residual_one(i - 1)
                        if B <= i + 1 < 3 * B:
                            v_copy_one(i + 1)
                        if B <= i + 3 < 3 * B:
                            ln_apply(i + 3)
                        if i == B + 3:
                            f_norm()
                for i in range(lo - 3, lo + B + 1 + lo // B):
                    for h in range(H):
                        if h == 0 and has(i + 3, lo):
                            ln_stats(item(i + 3))
                        if has(i + 1, lo):
                            row_max(i + 1, h)
                        if h == 2 and has(i + 3, lo):
                            ln_apply(item(i + 3))
                        if h == 3 and lo == 0 and i < 0:
                            zero_low(i + 3)
                        if h == 5 and has(i - 1, lo):
                            normalise(i - 1, 0)
                        if h == 7 and has(i - 1, lo):
                            normalise(i - 1, 1)
                        if h == 10 and has(i + 3, lo):
                            part1(i + 3)
                        if h == 14 and has(i + 3, lo):
                            v_copy(i + 3)
                        if h == 15 and has(i - 1, lo):
                            residual(i - 1)
                        if lo == B and has(i - 2, lo):
                            if h == 1:
                                z_norm_stats(i - 2 - B)
                            if h == 6:
                                z_apply(i - 2 - B)
                            if h == 8:
                                z_route(i - 2 - B)

            dve.wait_ge(s_row_psum, 1)
            dve.tensor_copy(s_row[:, :], pv_ps[0][0:B, 0, :]).then_inc(s_row_ready, 1)
            dve.wait_ge(s_row_ready, 2)
            dve.tensor_reduce(shift[:, :], s_row[:, :], axis=AX.X, op=ALU.max).then_inc(s_row_ready, 1)
            dve.wait_ge(s_row_ready, 3)
            dve.tensor_scalar(shift[:, :], shift[:, :], 0.0, -LEVEL0, ALU.min, ALU.add).then_inc(s_row_ready, 1)
            dve.wait_ge(s_row_ready, 4)

            def reshift():
                dve.tensor_scalar(shifted[:, :], s_row[:, :], shift[:, 0:1], TOP, ALU.subtract, ALU.min).then_inc(shifted_ready, 1)

            reshift()
            steps = 0
            for j, count in enumerate(BLOCKS):
                dve.wait_ge(e_ready, j + 1)
                for k in range(count):
                    a = steps % 2
                    dve.wait_ge(chain, steps + 2 * j + 1)
                    dve.scalar_tensor_tensor(out=min_junk[:, :], in0=e_row[:, :], scalar=level[:, a:a + 1], in1=k_inv[:, :],
                                             op0=ALU.min, op1=ALU.mult, accum_out=level[:, 1 - a:2 - a]).then_inc(chain, 1)
                    steps += 1
                a = steps % 2
                bits = level[:, a:a + 1].bitcast(int32)
                dve.wait_ge(chain, steps + 2 * j + 1)
                dve.tensor_scalar(exponent[:, :], bits, 23, None, ALU.logical_shift_right).then_inc(shift_step, 1)
                dve.wait_ge(shift_step, 3 * j + 1)
                dve.tensor_scalar(bits, bits, 0x7FFFFF, 0x3F800000, ALU.bitwise_and, ALU.bitwise_or).then_inc(chain, 1)
                last = j == len(BLOCKS) - 1
                dve.tensor_scalar(expo_f[:, :], exponent[:, :], LN2, -127 * LN2 - (0.0 if last else LEVEL0),
                                  ALU.mult, ALU.add).then_inc(shift_step, 1)
                dve.wait_ge(shift_step, 3 * j + 2)
                dve.tensor_tensor(shift[:, :], shift[:, :], expo_f[:, :], ALU.add).then_inc(shift_step, 1)
                dve.wait_ge(shift_step, 3 * j + 3)
                dve.wait_ge(chain, steps + 2 * j + 2)
                if not last:
                    reshift()
                    dve.tensor_scalar(level[:, a:a + 1], level[:, a:a + 1], float(np.exp(LEVEL0)), None, ALU.mult).then_inc(chain, 1)
                else:
                    dve.wait_ge(log_ready, 1)
                    dve.tensor_tensor(shift[:, :], log_level[:, :], shift[:, :], ALU.add).then_inc(shift_step, 1)
                    dve.wait_ge(shift_step, 3 * len(BLOCKS) + 1)
                    dve.tensor_scalar(shifted[:, :], s_row[:, :], shift[:, 0:1], 0.0, ALU.subtract, ALU.min).then_inc(shifted_ready, 1)
            dve.wait_ge(score_ready, 1)
            src = score[:, :]
            for r in range(TOPK // 8):
                dve.max(out=top8[:, :], in_=src).then_inc(top_step, 1)
                dve.wait_ge(top_step, 2 * r + 1)
                dve.match_replace(out=work[:, r % 2, :], in_to_replace=top8[:, :], in_values=src, imm_value=-1.0).then_inc(top_step, 1)
                dve.wait_ge(top_step, 2 * r + 2)
                src = work[:, r % 2, :]
            dve.tensor_scalar(weight[:, :], score[:, :], -1.0, 1.0, ALU.mult, ALU.add).then_inc(top_step, 1)
            dve.wait_ge(top_step, 2 * (TOPK // 8) + 1)
            dve.tensor_tensor(weight[:, :], weight[:, :], score[:, :], ALU.add).then_inc(top_step, 1)
            dve.wait_ge(top_step, 2 * (TOPK // 8) + 2)
            dve.scalar_tensor_tensor(out=weight[:, :], in0=src, scalar=-1.0, in1=weight[:, :], op0=ALU.is_equal,
                                     op1=ALU.mult).then_inc(weight_ready, 1)
            dve.wait_ge(w_psum, 1)
            dve.tensor_copy(w_tok[:, :, :].rearrange("p t b -> p (t b)"), pv_ps[1][:, 0, 0:NT * B]).then_inc(w_ready, 1)
            dve.wait_ge(w_ready, 1)
            for b in range(B):
                for k in range(NT):
                    c = NT * b + k
                    if k == 0:
                        dve.wait_ge(heavy_ready, b + 1)
                        dve.wait_ge(light_done, b + 1)
                    dve.scalar_tensor_tensor(out=x_all[:, c, :], in0=heavy[:, c, :], scalar=w_tok[:, k, b:b + 1], in1=x_all[:, c, :],
                                             op0=ALU.mult, op1=ALU.add).then_inc(x_final, 1)

        @block.tensor
        def _(pe):
            pe.wait_ge(w_in, 48)
            pe.wait_ge(pool_const, 4)
            pe.wait_ge(const_ready, 1)

            def xn_transpose(n):
                u = n % 2
                bank = pv_ps[0] if B <= n < 3 * B else prep_ps
                pe.wait_ge(xn_ready, n + 1)
                for k in range(NT):
                    i = pe.transpose(bank[:, 0, k * P:(k + 1) * P], xn[:, u, k, :], ident[:, :])
                i.then_inc(xnT_psum, 1)

            def qk_project(n):
                u, l = n % 2, n // B
                pe.wait_ge(xnT_ready, n + 1)
                pe.matmul(prep_ps[:, 0, :], w_att[:, l, 0, :], xnT[:, u, :], start=True, stop=True)
                pe.matmul(prep_ps[:, 1, :], w_att[:, l, 1, :], xnT[:, u, :] if l in SELF else ctxT[:, S * (n % B):S * (n % B + 1)],
                          start=True, stop=True).then_inc(qk_psum, 1)

            def v_project(n):
                u, l = n % 2, n // B
                bank = pv_ps[1] if B <= n < 3 * B else prep_ps
                for k in range(NT):
                    src = xnT[:, u, k * P:(k + 1) * P] if l in SELF else ctxT[:, S * (n % B) + k * P:S * (n % B) + (k + 1) * P]
                    i = pe.matmul(bank[:, 0, k * D:(k + 1) * D], src, w_att[:, l, 2, :], start=True, stop=True)
                i.then_inc(v_psum, 1)

            def scores_for_max(n, h):
                c, s3 = H * n + h, n % 3
                if h == 0:
                    pe.wait_ge(stacked[s3], 96 * (n // 3 + 1))
                if c >= 2:
                    pe.wait_ge(max_ready, c - 1)
                for k in range(NT):
                    i = pe.matmul(s1_ps[c % 2][:, k, :], stack[0:96, s3, 0, h, k * P:(k + 1) * P], stack[0:96, s3, 1, h, :],
                                  start=True, stop=True)
                i.then_inc(s1_psum, 1)

            def max_transpose(n, hf):
                pe.wait_ge(max_ready, H * n + 8 * hf + 8)
                for k in range(NT):
                    i = pe.transpose(prep_bf[0:8, 0, k * P:(k + 1) * P], negmax[:, n % 2, k, 8 * hf:8 * hf + 8], ident_bf[:, :])
                i.then_inc(maxT_psum, 1)

            def scores(n, h):
                c, s3 = H * n + h, n % 3
                if h % 8 == 0:
                    pe.wait_ge(max_in[s3][h // 8], 16 * (n // 3 + 1))
                if c >= 2:
                    pe.wait_ge(exp_ready, c - 1)
                for k in range(NT):
                    i = pe.matmul(s2_ps[c % 2][:, k, :], stack[0:97, s3, 1, h, k * P:(k + 1) * P], stack[0:97, s3, 0, h, :],
                                  start=True, stop=True)
                i.then_inc(s2_psum, 1)

            def weighted_sum(n, g):
                pe.wait_ge(exp_ready, H * n + G * (g + 1))
                if g == 0:
                    pe.wait_ge(v_ready, item(n) + 1)
                if g % 2 == 0 and n >= 1:
                    pe.wait_ge(uT_ready, 2 * (n - 1) + g // 2 + 1)
                for k in range(NT):
                    for j in range(G):
                        i = pe.matmul(pv_ps[g // 2][32 * j:32 * j + 32, g % 2, :], v_aug[:, n % 4, k, G * g + j, :],
                                      probT[:, (G * g + j) % 8, k, :], start=(k == 0), stop=(k == NT - 1))
                i.then_inc(pv_psum, 1)

            def u_transpose(n, k):
                if k == 0:
                    pe.wait_ge(uT_ready, 2 * n + 2)
                    if n >= 1:
                        pe.wait_ge(x_ready, n)
                else:
                    pe.wait_ge(o_ready, 2 * n + 1)
                for g in range(NG):
                    i = pe.transpose(out_ps[:, g * P:(g + 1) * P], uT[:, n % 2, g, k * P:(k + 1) * P], ident[:, :])
                i.then_inc(u_psum, 1)

            def o_transpose(n):
                pe.wait_ge(o_ready, 2 * n + 2)
                for k in range(NT):
                    i = pe.transpose(out_ps[:, k * P:(k + 1) * P], o_tok[:, n % 2, k, :], ident[:, :])
                i.then_inc(oT_psum, 1)

            def xr_transpose(b):
                pe.wait_ge(xr_ready, b + 1)
                for k in range(NT):
                    i = pe.transpose(prep_ps[:, 0, k * P:(k + 1) * P], xr[:, b % 2, k, :], ident[:, :])
                i.then_inc(xrT_psum, 1)

            def out_project(n):
                pe.wait_ge(oT_ready, n + 1)
                for k in range(NT):
                    i = pe.matmul(out_ps[:, k * D:(k + 1) * D], oT[:, n % 2, k * P:(k + 1) * P], w_att[:, item(n) // B, 3, :],
                                  start=True, stop=True)
                i.then_inc(y_psum, 1)

            def scores_one(n):
                r, u = n - B, n % 2
                pe.wait_ge(qk_ready, 2 * n + 2)
                if r >= 2:
                    pe.wait_ge(prob_ready, NT * (r - 1))
                for k in range(NT):
                    w = P if n >= 2 * B and k == 0 else S
                    i = pe.matmul(s1_ps[r % 2][:, k, 0:w], qkf[:, u, 0, k * P:(k + 1) * P], qkf[:, u, 1, 0:w], start=True, stop=True)
                i.then_inc(sc_psum, 1)

            def prob_tiles(n):
                tiles = [(0, 0), (1, 0), (1, 1)] if n >= 2 * B else [(0, 0), (1, 0), (1, 1), (0, 1)]
                return [(q, k, c * P) for c, (q, k) in enumerate(tiles)]

            def prob_transpose(n):
                r = n - B
                pe.wait_ge(prob_ready, NT * (r + 1))
                if r >= 2:
                    pe.wait_ge(probT_ready, r - 1)
                bank = s2_ps[r % 2][:, :, :].rearrange("p t q -> p (t q)")
                for q, k, c in prob_tiles(n):
                    i = pe.transpose(bank[:, c:c + P], prob[:, r % 2, q, k * P:(k + 1) * P], ident[:, :])
                i.then_inc(probT_psum, 1)

            def weighted_sum_one(n):
                r = n - B
                pe.wait_ge(probT_ready, r + 1)
                pe.wait_ge(v_ready, n + 1)
                if r >= 1:
                    pe.wait_ge(x_mid, r)
                for q in range(NT):
                    tiles = sorted((k, c) for q2, k, c in prob_tiles(n) if q2 == q)
                    for k, c in tiles:
                        i = pe.matmul(out_ps[:, q * D:(q + 1) * D], probT1[:, r % 2, c:c + P], v_one[:, r % 2, k, :],
                                      start=(k == 0), stop=(k == tiles[-1][0]))
                i.then_inc(o1_psum, 1)

            def expert_ffn():
                pe.wait_ge(f_xn_ready, FT)
                pe.wait_ge(qk_ready, 2 * (B + 5))
                for k in range(FT):
                    i = pe.transpose(prep_ps[:, k // 2, (k % 2) * P:(k % 2 + 1) * P], f_xn[:, k, :], ident[:, :])
                i.then_inc(f_xnT_psum, 1)
                pe.wait_ge(f_xnT_ready, 1)
                pe.wait_ge(f_in, 48)
                pe.wait_ge(probT_ready, 4)
                for f in range(NF):
                    if f >= 2:
                        pe.wait_ge(f_h_ready, f - 1)
                    pe.matmul(s2_ps[f % 2][:, :, :].rearrange("p t q -> p (t q)"), f_w1[:, f, :], f_xnT[:, :],
                              start=True, stop=True).then_inc(f_h_psum, 1)
                pe.wait_ge(f_h_ready, NF)
                pe.wait_ge(x_mid, 3)
                for k in range(FT):
                    for f in range(NF):
                        i = pe.matmul(out_ps[:, k * D:(k + 1) * D], f_hT[:, f, k * P:(k + 1) * P], f_w2[:, f, :],
                                      start=(f == 0), stop=(f == NF - 1))
                i.then_inc(f_y_psum, 1)

            for lo in MANY:
                if lo == B:
                    pe.wait_ge(ctx_in, 16)
                    pe.wait_ge(v_ready, B)
                    pe.wait_ge(uT_ready, 2 * B)
                    pe.wait_ge(x_ready, B)
                    pe.wait_ge(exp_ready, H * B)
                    pe.wait_ge(max_ready, H * B)
                    for i in range(B - 3, 3 * B + 1):
                        if i == B + 4:
                            expert_ffn()
                            pe.wait_ge(f_h_ready, NF)
                            pe.wait_ge(f_x, FT)
                        if B <= i < 3 * B:
                            scores_one(i)
                        if B <= i + 1 < 3 * B:
                            if i + 1 > B:
                                pe.wait_ge(qk_ready, 2 * (i + 1))
                            qk_project(i + 1)
                        if B <= i - 1 < 3 * B:
                            weighted_sum_one(i - 1)
                        if B <= i + 2 < 3 * B:
                            if i + 2 > B:
                                pe.wait_ge(xnT_ready, i + 2)
                            xn_transpose(i + 2)
                        if B <= i + 1 < 3 * B:
                            if i + 1 > B:
                                pe.wait_ge(v_ready, i + 1)
                            v_project(i + 1)
                        if B <= i < 3 * B:
                            prob_transpose(i)
                    pe.wait_ge(prob_ready, NT * 2 * B)
                    pe.wait_ge(probT_ready, 2 * B)
                    pe.wait_ge(x_mid, 2 * B)
                    pe.wait_ge(v_ready, 3 * B)
                    pe.wait_ge(qk_ready, 6 * B)
                prep_free = None
                for i in range(lo - 3, lo + B + 1 + lo // B):
                    for h in range(H):
                        if has(i, lo):
                            scores(i, h)
                        if has(i + 1, lo):
                            scores_for_max(i + 1, h)
                        if h == 1 and has(i - 1, lo):
                            weighted_sum(i - 1, 3)
                        if h == 2 and has(i, lo):
                            if prep_free:
                                pe.wait_ge(*prep_free)
                            max_transpose(i, 1)
                            prep_free = (maxT_ready, 2 * i + 2)
                        if h == 4 and has(i - 1, lo):
                            u_transpose(i - 1, 0)
                        if h == 5 and has(i + 3, lo):
                            if prep_free:
                                pe.wait_ge(*prep_free)
                            xn_transpose(item(i + 3))
                            prep_free = (xnT_ready, item(i + 3) + 1)
                        if h % 4 == 1 and h >= 5 and has(i, lo):
                            weighted_sum(i, (h - 5) // 4)
                        if h == 6 and has(i - 1, lo):
                            u_transpose(i - 1, 1)
                        if h == 8 and has(i + 3, lo):
                            qk_project(item(i + 3))
                            prep_free = (qk_ready, 2 * (item(i + 3) + 1))
                        if h == 10 and has(i - 1, lo):
                            o_transpose(i - 1)
                        if h == 10 and has(i + 1, lo):
                            if prep_free:
                                pe.wait_ge(*prep_free)
                            max_transpose(i + 1, 0)
                            prep_free = (maxT_ready, 2 * (i + 1) + 1)
                        if h == 13 and has(i + 3, lo):
                            if prep_free:
                                pe.wait_ge(*prep_free)
                            v_project(item(i + 3))
                            prep_free = (v_ready, item(i + 3) + 1)
                        if h == 14 and has(i - 1, lo):
                            out_project(i - 1)
                        if h == 15 and lo == B and has(i - 2, lo):
                            if prep_free:
                                pe.wait_ge(*prep_free)
                            xr_transpose(i - 2 - B)
                            prep_free = (xrT_ready, i - 2 - B + 1)
            pe.wait_ge(x_ready, 2 * B)
            pe.wait_ge(v_ready, 4 * B)
            pe.wait_ge(maxT_ready, 4 * B)
            pe.wait_ge(max_ready, 2 * H * B)
            pe.wait_ge(exp_ready, 2 * H * B)
            pe.wait_ge(uT_ready, 4 * B)
            pe.wait_ge(s_tok_ready, NT * B)
            for k in range(NT):
                i = pe.transpose(pv_ps[0][0:B, 0, k * P:(k + 1) * P], s_tok[:, :, k], ident[:, :])
            i.then_inc(s_row_psum, 1)
            pe.wait_ge(d_folded, 2)

            def up(q):
                pe.wait_ge(xrT_ready, 2 * q + 2)
                for f in range(NC):
                    c = NC * q + f
                    if c >= 2:
                        pe.wait_ge(d_h_ready, c - 1)
                    pe.matmul(s2_ps[c % 2][:, :, :].rearrange("p t q -> p (t q)"), d_w1[:, f, :], xrT[:, 2 * S * q:2 * S * (q + 1)],
                              start=True, stop=True).then_inc(d_h_psum, 1)

            def down(q):
                pe.wait_ge(xrT_ready, B)
                for e in range(2):
                    b = 2 * q + e
                    pe.wait_ge(d_h_ready, NC * (q + 1))
                    if b >= 2:
                        pe.wait_ge(light_done, b - 1)
                        pe.wait_ge(heavy_copied, b - 1)
                    toks = [slice((NT * e + k) * P, (NT * e + k + 1) * P) for k in range(NT)]
                    for k in range(NT):
                        for f in range(NC - 1):
                            i = pe.matmul(heavy_bank(b)[:, k, :], d_hT[:, q % 2, f, toks[k]], d_w2[:, f, :],
                                          start=(f == 0), stop=(f == NC - 2))
                    i.then_inc(d_y_psum, 1)
                    pe.wait_ge(light_bias, b + 1)
                    for k in range(NT):
                        pe.matmul(light_bank(b)[:, k, :], ident[:, :], x_all[:, NT * b + k, :], start=True, stop=False)
                        i = pe.matmul(light_bank(b)[:, k, :], d_hT[:, q % 2, NC - 1, toks[k]], d_w2[:, NC - 1, :],
                                      start=False, stop=True)
                    i.then_inc(d_y_psum, 1)

            for q in range(5):
                if q < 4:
                    up(q)
                if q >= 1:
                    down(q - 1)
            pe.wait_ge(weight_ready, 1)
            for k in range(NT):
                i = pe.transpose(pv_ps[1][:, 0, k * B:(k + 1) * B], weight[:, k * P:(k + 1) * P], ident[0:B, 0:B])
            i.then_inc(w_psum, 1)


def laid_out(i):
    def pad(a, axis):
        return np.concatenate([a, np.zeros(a.shape[:axis] + (P - a.shape[axis],) + a.shape[axis + 1:], a.dtype)], axis)

    perm = np.arange(D).reshape(H, DH).T.reshape(-1)
    wqkv = i["L0_attn_W_qkv"].T
    bqkv = i["L0_attn_b_qkv"]
    out = {"x": i["x"], "ctxT": i["ctx_1024"].reshape(B * S, D).T}
    none, nob = np.zeros((D, D), np.float32), np.zeros(D, np.float32)
    w3, b3 = i["L1_attn_W_qkv"].T, i["L1_attn_b_qkv"]
    out["w_att"] = np.stack([
        np.stack([wqkv[:, 0:D][:, perm], wqkv[:, D:2 * D][:, perm], wqkv[:, 2 * D:], i["L0_attn_W_out"].T]),
        np.stack([i["L0_xattn_Wq"], i["L0_xattn_Wk"], i["L0_xattn_Wv"], none]),
        np.stack([w3[:, 0:D], w3[:, D:2 * D], w3[:, 2 * D:], none]),
        np.stack([i["L1_xattn_Wq"][:, perm], i["L1_xattn_Wk"][:, perm], i["L1_xattn_Wv"], i["L1_xattn_Wo"]])])
    out["b_qk"] = np.stack([np.stack([bqkv[0:D][perm], bqkv[D:2 * D][perm]], -1),
                            np.stack([i["L0_xattn_bq"], i["L0_xattn_bk"]], -1),
                            np.stack([b3[0:D], b3[D:2 * D]], -1),
                            np.stack([i["L1_xattn_bq"][perm], i["L1_xattn_bk"][perm]], -1)], 1)
    out["b_vo"] = np.stack([np.stack([bqkv[2 * D:], i["L0_attn_b_out"]]), np.stack([i["L0_xattn_bv"], nob]),
                            np.stack([b3[2 * D:], nob]), np.stack([i["L1_xattn_bv"], i["L1_xattn_bo"]])])
    out["f_w1"] = i["L0_ffn_w1"].reshape(D, NF, P)
    out["f_w2"] = i["L0_ffn_w2"].reshape(NF, P, D).transpose(1, 0, 2)
    out["f_ew"] = i["L0_ffn_expert_weights"].reshape(FT, P, 2).transpose(1, 0, 2)
    out["d_w1"] = np.concatenate([i["L1_ffn_w1_h"].T, pad(i["L1_ffn_w1_l"].T, 1)], 1).reshape(D, NC, P)
    out["d_w2"] = np.concatenate([i["L1_ffn_w2_h"].T, pad(i["L1_ffn_w2_l"].T, 0)], 0).reshape(NC, P, D).transpose(1, 0, 2)
    out["d_b1"] = np.concatenate([i["L1_ffn_b1_h"], pad(i["L1_ffn_b1_l"], 0)]).reshape(NC, P).T
    out["d_b2"] = np.stack([i["L1_ffn_b2_h"], i["L1_ffn_b2_l"]])
    out["gamma"] = np.stack([i["L1_ffn_gamma_h"], i["L1_ffn_gamma_l"]], -1)
    out["route"] = i["L1_ffn_routing_token"]
    return {k: np.ascontiguousarray(v) for k, v in out.items()}


def kernel(**inputs):
    import concourse.bacc as bacc
    from concourse.bass_utils import run_bass_kernel_spmd
    arrays = laid_out({k: np.asarray(v) for k, v in inputs.items()})
    nc = bacc.Bacc("TRN2", target_bir_lowering=False, num_devices=1)
    dram = {k: nc.dram_tensor(k, a.shape, mybir.dt.from_np(a.dtype), kind="ExternalInput").ap() for k, a in arrays.items()}
    dram["out"] = nc.dram_tensor("out", (B, S, D), fp32, kind="ExternalOutput").ap()
    build(nc, dram)
    r = run_bass_kernel_spmd(nc, [arrays], core_ids=[0])
    return r.results[0]["out"]
```

```python
import concourse.bass as bass
from concourse import mybir
from contextlib import ExitStack
import numpy as np

fp32 = mybir.dt.float32
bf16 = mybir.dt.bfloat16
int32 = mybir.dt.int32
ALU = mybir.AluOpType
ACT = mybir.ActivationFunctionType
AX = mybir.AxisListType

B, S, D = 8, 256, 128
P = 128
NT = S // P
H, DH = 16, 8
G = 4
NG = H // G
EPS = 1e-5
L = 4
FT = 4
NF = 8
NC = 5
KEFF = 144.0
TOPK = 128
NEVER = -3e38
TOP_HALVES_AHEAD = (4, 4)
BLOCKS = (25, 24)
LEVEL0 = 62.0
SHIFT_AT = (2, 4)
TOP = 80.0
LN2 = float(np.log(2.0))
AHEAD = 2
AHEAD_C = 3
SELF = (0, 2)


def build(nc, t):
    ctx = ExitStack()
    with ctx:
        def sb(name, shape, dt=fp32):
            return ctx.enter_context(nc.sbuf_tensor(name + "_sb", shape, dt))

        def ps(name, shape, dt=fp32):
            return ctx.enter_context(nc.psum_tensor(name, shape, dt))

        def sem(name):
            return ctx.enter_context(nc.semaphore(name))

        x_all = sb("x_all", [P, B * NT, D])
        ctxT = sb("ctxT", [P, B * S])
        ident = sb("ident", [P, P])
        ident_bf = sb("ident_bf", [P, P], bf16)
        minus_half = sb("minus_half", [P, FT])
        fill = sb("fill", [97, S], bf16)
        w_att = sb("w_att", [P, L, 4, D])
        b_qk = sb("b_qk", [P, L, 2])
        b_vo = sb("b_vo", [P, L, 2, D])

        stats = sb("stats", [P, 2, NT, 6])
        mv = sb("mv", [P, 2, NT, 2])
        rstd = sb("rstd", [P, 2, NT])
        xn = sb("xn", [P, 2, NT, D])
        xnT = sb("xnT", [P, 2, S])
        qkf = sb("qkf", [P, 2, 2, S])
        rest = sb("rest", [P, 2, S])
        parts = sb("parts", [P, 2, 2, 3, S], bf16)
        stack = sb("stack", [P, 3, 2, H, S], bf16)
        v_aug = sb("v_aug", [P, 4, NT, H, 32])
        negmax = sb("negmax", [P, 2, NT, H], bf16)
        maxrow = sb("maxrow", [DH, 2, 2, S], bf16)
        probT = sb("probT", [P, 8, NT, S])
        uT = sb("uT", [P, 2, NG, S])
        den_inv = sb("den_inv", [P, NT, H])
        o_tok = sb("o_tok", [P, 2, NT, D])
        oT = sb("oT", [P, 2, S])

        v_one = sb("v_one", [P, 2, NT, D])
        negbias = sb("negbias", [P, 2, NT])
        negbias_raw = sb("negbias_raw", [P, 2, NT])
        prob = sb("prob", [P, 2, NT, S])
        probT1 = sb("probT1", [P, 2, NT * S])
        den = sb("den", [P, 2, NT])
        den_inv1 = sb("den_inv1", [P, 2, NT])
        causal = sb("causal", [P, P])

        f_stats = sb("f_stats", [P, FT, 6])
        f_mv = sb("f_mv", [P, FT, 2])
        f_rstd = sb("f_rstd", [P, FT])
        f_xn = sb("f_xn", [P, FT, D])
        f_xnT = sb("f_xnT", [P, FT * P])
        f_hT = sb("f_hT", [P, NF, FT * P])
        f_w1 = sb("f_w1", [P, NF, P])
        f_w2 = sb("f_w2", [P, NF, D])
        f_ew = sb("f_ew", [P, FT, 2])
        f_wsum = sb("f_wsum", [P, FT])

        route = sb("route", [P, D])
        s_tok = sb("s_tok", [P, B, NT])
        z = sb("z", [P, 2, NT, D])
        z_stats = sb("z_stats", [P, 2, NT, 6])
        z_mv = sb("z_mv", [P, B, NT, 2])
        z_rstd = sb("z_rstd", [P, B, NT])
        s_junk = sb("s_junk", [P, D])
        rnorm = sb("rnorm", [P, B, NT])
        xr = sb("xr", [P, 2, NT, D])
        xrT = sb("xrT", [P, B * S])
        d_w1 = sb("d_w1", [P, NC, P])
        d_b1 = sb("d_b1", [P, NC])
        d_w2 = sb("d_w2", [P, NC, D])
        d_b2 = sb("d_b2", [P, 2, D])
        gamma = sb("gamma", [P, 2])
        stack_free = stack[:, :, :, :, :].rearrange("p s a h n -> p (s a h n)").bitcast(fp32)
        d_hT = stack_free[:, 0:8 * NC * P].rearrange("p (u f q) -> p u f q", u=2, f=NC)
        heavy = stack_free[:, 8 * NC * P:8 * NC * P + B * S].rearrange("p (t d) -> p t d", d=D)

        rows_free = iter(range(8 * NC * P + B * S, 3 * H * S, S))

        def row():
            first = next(rows_free)
            return stack_free[0:B, first:first + S]

        s_row = row()
        shifted = row()
        e_row = row()
        k_inv = sb("k_inv", [B, S])
        min_junk = row()
        level = sb("level", [B, 2])
        exponent = sb("exponent", [B, 1], int32)
        expo_f = sb("expo_f", [B, 1])
        shift = sb("shift", [B, 1])
        ones = sb("ones", [B, S])
        at_one = row()
        n_at_one = sb("n_at_one", [B, 1])
        place = row()
        highest = row()
        inv_level = sb("inv_level", [B, 1])
        score = row()
        work = [row(), row()]
        top8 = sb("top8", [B, 8])
        weight = row()
        w_tok = sb("w_tok", [P, NT, B])

        s1_ps = [ps(f"s1_ps{i}", [P, NT, S]) for i in range(2)]
        s2_ps = [ps(f"s2_ps{i}", [P, NT, S]) for i in range(2)]
        pv_ps = [ps(f"pv_ps{i}", [P, 2, S]) for i in range(2)]
        prep_ps = ps("prep_ps", [P, 2, S])
        out_ps = ps("out_ps", [P, 512])
        prep_bf = prep_ps[:, :, :].bitcast(bf16)

        scratch = [nc.dram_tensor(f"scratch{i}", [2, 3, DH, H, S], bf16).ap() for i in range(2)]

        x_in = [sem(f"x_in{i}") for i in range(4)]
        w_in, w_rest_in, ctx_in = sem("w_in"), sem("w_rest_in"), sem("ctx_in")
        fill_ready = sem("fill_ready")
        filled = [sem(f"filled{i}") for i in range(3)]
        v_aug_ready, pool_const = sem("v_aug_ready"), sem("pool_const")
        one_row = sem("one_row")
        stats_ready, mv_ready, rstd_step, rstd_ready, xn_ready = (
            sem("stats_ready"), sem("mv_ready"), sem("rstd_step"), sem("rstd_ready"), sem("xn_ready"))
        xnT_psum, xnT_ready, qk_psum, qk_ready = sem("xnT_psum"), sem("xnT_ready"), sem("qk_psum"), sem("qk_ready")
        part1_ready, rest_ready, parts_ready = sem("part1_ready"), sem("rest_ready"), sem("parts_ready")
        v_psum, v_ready = sem("v_psum"), sem("v_ready")
        scratch_in = [sem(f"scratch_in{i}") for i in range(2)]
        stacked = [sem(f"stacked{i}") for i in range(3)]
        s1_psum, max_ready, maxT_psum, maxT_ready = sem("s1_psum"), sem("max_ready"), sem("maxT_psum"), sem("maxT_ready")
        max_in = [[sem(f"max_in{i}{hf}") for hf in range(2)] for i in range(3)]
        s2_psum, exp_ready, pv_psum, uT_ready = sem("s2_psum"), sem("exp_ready"), sem("pv_psum"), sem("uT_ready")
        u_psum, inv_ready, o_ready = sem("u_psum"), sem("inv_ready"), sem("o_ready")
        oT_psum, oT_ready, y_psum = sem("oT_psum"), sem("oT_ready"), sem("y_psum")
        biased, x_ready = sem("biased"), sem("x_ready")
        causal_step = sem("causal_step")
        sc_psum, mask_step, negmax1_ready, bias_ready, prob_ready = (
            sem("sc_psum"), sem("mask_step"), sem("negmax1_ready"), sem("bias_ready"), sem("prob_ready"))
        probT_psum, probT_ready, o1_psum, inv1_ready, x_mid = (
            sem("probT_psum"), sem("probT_ready"), sem("o1_psum"), sem("inv1_ready"), sem("x_mid"))
        f_in, f_stats_ready, f_mv_ready, f_rstd_ready, f_xn_ready = (
            sem("f_in"), sem("f_stats_ready"), sem("f_mv_ready"), sem("f_rstd_ready"), sem("f_xn_ready"))
        f_xnT_psum, f_xnT_ready, f_h_psum, f_h_ready, f_y_psum, f_wsum_ready, f_x = (
            sem("f_xnT_psum"), sem("f_xnT_ready"), sem("f_h_psum"), sem("f_h_ready"), sem("f_y_psum"), sem("f_wsum_ready"), sem("f_x"))
        d_in, d_folded, s_tok_ready, z_stats_ready, z_mv_ready, z_ready, rn_step, rn_ready = (
            sem("d_in"), sem("d_folded"), sem("s_tok_ready"), sem("z_stats_ready"), sem("z_mv_ready"), sem("z_ready"), sem("rn_step"), sem("rn_ready"))
        xr_ready, xrT_psum, xrT_ready, light_bias = sem("xr_ready"), sem("xrT_psum"), sem("xrT_ready"), sem("light_bias")
        d_h_psum, d_h_ready, d_y_psum, light_done, heavy_copied, heavy_ready = (
            sem("d_h_psum"), sem("d_h_ready"), sem("d_y_psum"), sem("light_done"), sem("heavy_copied"), sem("heavy_ready"))
        shift_step, top_step, pick_step, score_step = sem("shift_step"), sem("top_step"), sem("pick_step"), sem("score_step")
        s_row_psum, s_row_ready, chain, shifted_ready, e_ready = (
            sem("s_row_psum"), sem("s_row_ready"), sem("chain"), sem("shifted_ready"), sem("e_ready"))
        weight_ready, w_psum, w_ready, x_final = (
            sem("weight_ready"), sem("w_psum"), sem("w_ready"), sem("x_final"))
        out_done = [sem(f"out_done{i}") for i in range(4)]

        block = ctx.enter_context(nc.Block())
        MANY = (0, B)

        def has(n, lo):
            return lo <= n < lo + B

        def prepared(i, lo):
            if lo == 0 and i + 3 < B + AHEAD:
                return i + 3
            if lo == B and lo + AHEAD_C <= i + 3 < lo + B:
                return item(i + 3)
            return None

        def in_middle(n):
            return B + AHEAD <= n < 3 * B + AHEAD_C

        def ahead(i, d):
            return [n for n in (i + d, i + d + 1) if n - i == d + (n >= 3 * B) and in_middle(n)]

        def steps_of(lo):
            return range(-3, B) if lo == 0 else range(B - 1, 2 * B + 2)

        def item(m):
            return m if m < B else m + 2 * B

        def many(n):
            return n if n < B else n - 2 * B

        out_ps2 = out_ps[:, :].rearrange("p (t q) -> p t q", q=S)

        def heavy_bank(b):
            return s1_ps[b % 2][:, 0, :].rearrange("p (t d) -> p t d", d=D)

        def light_bank(b):
            return (prep_ps, out_ps2)[b % 2][:, 0, :].rearrange("p (t d) -> p t d", d=D)

        @block.sync
        def _(sp):
            def load_x(c):
                tiles = slice(4 * c, 4 * c + 4)
                sp.dma_start(x_all[:, tiles, :], t["x"].rearrange("b (t p) d -> p (b t) d", p=P)[:, tiles, :]).then_inc(x_in[c], 16)

            load_x(0)
            sp.dma_start(w_att[:, 0:1, :, :], t["w_att"][0:1].rearrange("l w p d -> p l w d")).then_inc(w_in, 16)
            sp.dma_start(b_qk[:, :, :], t["b_qk"]).then_inc(w_in, 16)
            sp.dma_start(b_vo[:, :, :, :].rearrange("p l w d -> p (l w d)"), t["b_vo"].rearrange("l w d -> (l w d)").partition_broadcast(P)).then_inc(w_in, 16)
            sp.wait_ge(fill_ready, 2)
            for s3 in range(3):
                sp.dma_start(stack[6 * DH:96, s3].rearrange("p a h n -> p (a h) n"),
                             fill[6 * DH:96, :].unsqueeze(1).broadcast_to([96 - 6 * DH, 2 * H, S])).then_inc(filled[s3], 16)
                sp.dma_start(stack[96:97, s3, 1], fill[96:97, :].unsqueeze(1).broadcast_to([1, H, S])).then_inc(filled[s3], 16)
                load_x(s3 + 1)
            sp.dma_start(w_att[:, 1:L, :, :], t["w_att"][1:L].rearrange("l w p d -> p l w d")).then_inc(w_rest_in, 16)
            sp.dma_start(ctxT[:, :], t["ctxT"]).then_inc(ctx_in, 16)
            for dst, name in ((f_w1[:, :, :], "f_w1"), (f_w2[:, :, :], "f_w2"), (f_ew[:, :, :], "f_ew")):
                sp.dma_start(dst, t[name]).then_inc(f_in, 16)
            for dst, name in ((d_w1[:, :, :], "d_w1"), (d_w2[:, :, :], "d_w2"), (d_b1[:, :], "d_b1"), (gamma[:, :], "gamma")):
                sp.dma_start(dst, t[name]).then_inc(d_in, 16)
            sp.dma_start(d_b2[:, :, :].rearrange("p l d -> p (l d)"), t["d_b2"].rearrange("l d -> (l d)").partition_broadcast(P)).then_inc(d_in, 16)
            sp.dma_start(route[:, :], t["route"].partition_broadcast(P)).then_inc(d_in, 16)

            def bounce(n):
                u, s3 = n % 2, n % 3
                sp.wait_ge(parts_ready, n + 1)
                if n >= 2:
                    sp.wait_ge(stacked[(n - 2) % 3], 96 * ((n - 2) // 3 + 1))
                sp.dma_start(scratch[u].rearrange("a j d h n -> (d h) (a j) n"),
                             parts[:, u].rearrange("p a j n -> p (a j) n")).then_inc(scratch_in[u], 16)

            def load_stack(n):
                u, s3 = n % 2, n % 3
                sp.wait_ge(scratch_in[u], 16 * (n // 2 + 1))
                if n >= 3:
                    sp.wait_ge(s2_psum, H * (n - 2))
                for r, m, j in ((0, 3, 0), (3, 2, 1), (5, 1, 2)):
                    sp.dma_start(stack[DH * r:DH * (r + m), s3, 1], scratch[u][1, 0:m].rearrange("j d h n -> (j d) h n")
                                 ).then_inc(stacked[s3], 16)
                    sp.dma_start(stack[DH * r:DH * (r + m), s3, 0].rearrange("p h n -> p (h n)"),
                                 scratch[u][0, j:j + 1].rearrange("j d h n -> j d (h n)").broadcast_to([m, DH, H * S])
                                 ).then_inc(stacked[s3], 16)

            def place_max(n, hf):
                u, s3 = n % 2, n % 3
                sp.wait_ge(maxT_ready, 2 * n + hf + 1)
                sp.dma_start(stack[96:97, s3, 0, 8 * hf:8 * hf + 8, :],
                             maxrow[:, u, hf, :]).then_inc(max_in[s3][hf], 16)

            for lo in MANY:
                for i in range(lo - 3, lo + B):
                    if has(i + 2, lo):
                        load_stack(i + 2)
                    if has(i, lo):
                        place_max(i, 1)
                    if has(i + 1, lo):
                        place_max(i + 1, 0)
                    if has(i + 3, lo):
                        bounce(i + 3)
            for c in range(4):
                sp.wait_ge(x_final, 4 * c + 4)
                sp.dma_start(t["out"].rearrange("b (t p) d -> p (b t) d", p=P)[:, 4 * c:4 * c + 4, :],
                             x_all[:, 4 * c:4 * c + 4, :]).then_inc(out_done[c], 16)
            for c in range(4):
                sp.wait_ge(out_done[c], 16)

        @block.gpsimd
        def _(pool):
            pool.memset(ident[:, :], 0.0).then_inc(pool_const, 1)
            pool.memset(minus_half[:, :], -0.5).then_inc(pool_const, 1)
            pool.wait_ge(pool_const, 2)
            pool.affine_select(out=ident[:, :], in_=ident[:, :], compare_op=ALU.not_equal, fill=1.0, base=0,
                               pattern=[[-1, P]], channel_multiplier=1).then_inc(pool_const, 1)
            pool.wait_ge(pool_const, 3)
            pool.tensor_copy(ident_bf[:, :], ident[:, :]).then_inc(pool_const, 1)

            pool.memset(causal[:, :], 0.0).then_inc(causal_step, 1)
            pool.wait_ge(causal_step, 1)
            pool.affine_select(out=causal[:, :], in_=causal[:, :], compare_op=ALU.is_ge, fill=-1e30, base=0,
                               pattern=[[-1, P]], channel_multiplier=1).then_inc(causal_step, 1)

            def rstd_step_(n):
                u = n % 2
                pool.wait_ge(mv_ready, NT * (n + 1))
                pool.tensor_scalar(rstd[:, u, :], mv[:, u, :, 1], EPS, None, ALU.add).then_inc(rstd_step, 1)
                pool.wait_ge(rstd_step, n + 1)
                pool.tensor_tensor(rstd[:, u, :], rstd[:, u, :], minus_half[:, 0:NT], ALU.pow).then_inc(rstd_ready, 1)

            def add_bias(m):
                n = item(m)
                b, l = n % B, n // B
                if m == 0:
                    pool.wait_ge(w_in, 48)
                pool.wait_ge(xn_ready, n + 1)
                x2 = x_all[:, NT * b:NT * b + NT, :]
                pool.tensor_tensor(x2, x2, b_vo[:, l, 1:2, :].broadcast_to([P, NT, D]), ALU.add).then_inc(biased, 1)

            def split(m):
                n, u = m, m % 2
                pool.wait_ge(part1_ready, n + 1)
                pool.tensor_tensor(rest[:, :, :], qkf[:, u], parts[:, u, :, 0, :], ALU.subtract).then_inc(rest_ready, 1)
                pool.tensor_tensor(parts[:, u, :, 1, :], qkf[:, u], parts[:, u, :, 0, :], ALU.subtract).then_inc(rest_ready, 1)
                pool.wait_ge(rest_ready, 2 * n + 2)
                pool.tensor_tensor(parts[:, u, :, 2, :], rest[:, :, :], parts[:, u, :, 1, :], ALU.subtract).then_inc(parts_ready, 1)
                pool.wait_ge(parts_ready, n + 1)

            def z_norms(b):
                if b == 0:
                    pool.wait_ge(d_in, 96)
                pool.wait_ge(z_mv_ready, NT * (b + 1))
                rs, rn, var = z_rstd[:, b, :], rnorm[:, b, :], z_mv[:, b, :, 1]
                pool.tensor_scalar(rs, var, EPS, None, ALU.add).then_inc(rn_step, 1)
                pool.wait_ge(rn_step, 5 * b + 1)
                pool.tensor_tensor(rs, rs, minus_half[:, 0:NT], ALU.pow).then_inc(rn_step, 1)
                pool.wait_ge(rn_step, 5 * b + 2)
                pool.tensor_tensor(rn, var, rs, ALU.mult).then_inc(rn_step, 1)
                pool.wait_ge(rn_step, 5 * b + 3)
                pool.tensor_tensor(rn, rn, rs, ALU.mult).then_inc(rn_step, 1)
                pool.wait_ge(rn_step, 5 * b + 4)
                pool.tensor_scalar(rn, rn, float(D), 1e-24, ALU.mult, ALU.max).then_inc(rn_step, 1)
                pool.wait_ge(rn_step, 5 * b + 5)
                pool.tensor_tensor(rn, rn, minus_half[:, 0:NT], ALU.pow).then_inc(rn_ready, 1)
                pool.wait_ge(z_ready, b + 1)
                x2 = x_all[:, NT * b:NT * b + NT, :]
                pool.tensor_tensor(x2, x2, d_b2[:, 1:2, :].broadcast_to([P, NT, D]), ALU.add).then_inc(light_bias, 1)

            def f_rstd_step():
                pool.wait_ge(f_mv_ready, FT)
                pool.tensor_scalar(f_rstd[:, :], f_mv[:, :, 1], EPS, None, ALU.add).then_inc(f_rstd_ready, 1)
                pool.wait_ge(f_rstd_ready, 1)
                pool.tensor_tensor(f_rstd[:, :], f_rstd[:, :], minus_half[:, :], ALU.pow).then_inc(f_rstd_ready, 1)

            for lo in MANY:
                if lo == B:
                    for n in range(B, 3 * B + AHEAD_C):
                        rstd_step_(n)
                        if n == B + 6:
                            f_rstd_step()
                for n in range(lo, lo + B):
                    if n < B or n >= B + AHEAD_C:
                        rstd_step_(item(n))
                    add_bias(n)
                    if lo == B and n >= lo + 5:
                        z_norms(n - lo - 5)
                    split(n)

            for b in range(3, B):
                z_norms(b)
            for b in range(B):
                pool.wait_ge(heavy_copied, b + 1)
                h2 = heavy[:, NT * b:NT * b + NT, :]
                pool.tensor_tensor(h2, h2, d_b2[:, 0:1, :].broadcast_to([P, NT, D]), ALU.add).then_inc(heavy_ready, 1)

        @block.scalar
        def _(act):
            def exps(n, h):
                c = H * n + h
                act.wait_ge(s2_psum, c + 1)
                if c >= 8:
                    act.wait_ge(pv_psum, c // G - 1)
                act.activation(probT[:, c % 8], s2_ps[c % 2][:, :, :], ACT.Exp, scale=DH ** -0.5).then_inc(exp_ready, 1)

            def xnT_copy(n):
                bank = pv_ps[0] if in_middle(n) else prep_ps
                act.wait_ge(xnT_psum, n + 1)
                if n >= 2:
                    act.wait_ge(v_psum, n - 1)
                act.activation(xnT[:, n % 2, :], bank[:, 0, :], ACT.Copy).then_inc(xnT_ready, 1)

            def qk_copy(n):
                act.wait_ge(qk_psum, n + 1)
                if n >= 2:
                    if B <= n - 2 < 3 * B:
                        act.wait_ge(sc_psum, n - 2 - B + 1)
                    else:
                        act.wait_ge(parts_ready, many(n - 2) + 1)
                if n == 0:
                    act.wait_ge(w_in, 48)
                for a in range(2):
                    act.activation(qkf[:, n % 2, a, :], prep_ps[:, a, :], ACT.Identity,
                                   bias=b_qk[:, n // B, a:a + 1]).then_inc(qk_ready, 1)

            def max_copy(n, hf):
                act.wait_ge(maxT_psum, 2 * n + hf + 1)
                if n >= 2:
                    act.wait_ge(max_in[(n - 2) % 3][hf], 16 * ((n - 2) // 3 + 1))
                act.activation(maxrow[:, n % 2, hf, :], prep_bf[0:8, 0, 0:S], ACT.Copy).then_inc(maxT_ready, 1)

            def u_copy(n, gb):
                act.wait_ge(pv_psum, NG * n + 2 * gb + 2)
                if n >= 2:
                    act.wait_ge(u_psum, 2 * (n - 1))
                act.activation(uT[:, n % 2, 2 * gb:2 * gb + 2, :], pv_ps[gb][:, :, :], ACT.Copy).then_inc(uT_ready, 1)

            def xrT_copy(b):
                act.wait_ge(xrT_psum, b + 1)
                act.activation(xrT[:, S * b:S * b + S], prep_ps[:, 0, :], ACT.Copy).then_inc(xrT_ready, 1)

            def oT_copy(n):
                act.wait_ge(oT_psum, n + 1)
                if n >= 2:
                    act.wait_ge(y_psum, n - 1)
                act.activation(oT[:, n % 2, :], out_ps[:, 0:S], ACT.Copy).then_inc(oT_ready, 1)

            def softmax_exps(n):
                r = n - B
                act.wait_ge(bias_ready, r + 1)
                if r >= 2:
                    act.wait_ge(probT_psum, r - 1)
                for k in range(NT):
                    w = P if n >= 2 * B and k == 0 else S
                    act.activation(prob[:, r % 2, k, 0:w], s1_ps[r % 2][:, k, 0:w], ACT.Exp, bias=negbias[:, r % 2, k:k + 1],
                                   scale=D ** -0.5, accum_out=den[:, r % 2, k:k + 1]).then_inc(prob_ready, 1)

            def probT_copy(n):
                r = n - B
                w = 3 * P if n >= 2 * B else 4 * P
                act.wait_ge(probT_psum, r + 1)
                if r >= 2:
                    act.wait_ge(o1_psum, r - 1)
                act.activation(probT1[:, r % 2, 0:w], s2_ps[r % 2][:, :, :].rearrange("p t q -> p (t q)")[:, 0:w],
                               ACT.Copy).then_inc(probT_ready, 1)

            def f_acts():
                act.wait_ge(f_xnT_psum, 1)
                act.activation(f_xnT[:, :], prep_ps[:, :, :].rearrange("p t q -> p (t q)"), ACT.Copy).then_inc(f_xnT_ready, 1)
                for f in range(NF):
                    act.wait_ge(f_h_psum, f + 1)
                    act.activation(f_hT[:, f, :], s2_ps[f % 2][:, :, :].rearrange("p t q -> p (t q)"),
                                   ACT.Gelu_apprx_tanh).then_inc(f_h_ready, 1)

            for lo in MANY:
                if lo == B:
                    for i in range(B, 3 * B + 1):
                        if B <= i - 1 < 3 * B:
                            probT_copy(i - 1)
                        if i == B:
                            u_copy(B - 1, 1)
                        if i == B + 4:
                            f_acts()
                        if B <= i < 3 * B:
                            softmax_exps(i)
                        for n in ahead(i, 1):
                            qk_copy(n)
                        for n in ahead(i, 2):
                            xnT_copy(n)
                        if i == B:
                            oT_copy(B - 1)
                for i in steps_of(lo):
                    x = prepared(i, lo)
                    for h in range(H):
                        if has(i, lo):
                            exps(i, h)
                        if h == 3 and has(i, lo):
                            max_copy(i, 1)
                        if h == 3 and has(i - 1, lo):
                            u_copy(i - 1, 1)
                        if h == 6 and x is not None:
                            xnT_copy(x)
                        if h == 9 and x is not None:
                            qk_copy(x)
                        if h == 11 and has(i, lo):
                            u_copy(i, 0)
                        if h == 11 and has(i + 1, lo):
                            max_copy(i + 1, 0)
                        if h == 12 and has(i - 1, lo):
                            oT_copy(i - 1)
                        if h == 0 and lo == B and has(i - 3, lo):
                            xrT_copy(i - 3 - B)

            def shift_exp(j):
                act.wait_ge(shifted_ready, j + 1)
                act.activation(e_row[:, :], shifted[:, :], ACT.Exp).then_inc(e_ready, 1)

            def branch_copies(q):
                for b in (2 * q, 2 * q + 1):
                    act.wait_ge(d_y_psum, 2 * b + 1)
                    act.activation(heavy[:, NT * b:NT * b + NT, :], heavy_bank(b), ACT.Copy).then_inc(heavy_copied, 1)
                    act.wait_ge(d_y_psum, 2 * b + 2)
                    act.activation(x_all[:, NT * b:NT * b + NT, :], light_bank(b), ACT.Copy).then_inc(light_done, 1)

            act.wait_ge(d_in, 96)
            for q in range(4):
                for f in range(NC):
                    c = NC * q + f
                    if (q, f) == SHIFT_AT:
                        shift_exp(1)
                    act.wait_ge(d_h_psum, c + 1)
                    if q >= 2:
                        act.wait_ge(d_y_psum, 4 * (q - 1))
                    act.activation(d_hT[:, q % 2, f, :], s2_ps[c % 2][:, :, :].rearrange("p t q -> p (t q)"), ACT.Gelu,
                                   bias=d_b1[:, f:f + 1]).then_inc(d_h_ready, 1)
                if q == 0:
                    xrT_copy(B - 1)
                    shift_exp(0)
                if q >= 1:
                    branch_copies(q - 1)
            branch_copies(3)

        @block.vector
        def _(dve):
            dve.memset(fill[0:96, :], 0.0).then_inc(fill_ready, 1)
            dve.memset(fill[96:97, :], 1.0).then_inc(fill_ready, 1)

            def prepare_v_aug(slots, count):
                dve.memset(v_aug[:, slots].rearrange("p s t h d -> p (s t h d)"), 0.0).then_inc(v_aug_ready, 1)
                dve.wait_ge(v_aug_ready, count + 1)
                dve.memset(v_aug[:, slots, :, :, DH:DH + 1].rearrange("p s t h d -> p (s t h) d"), 1.0).then_inc(v_aug_ready, 1)

            prepare_v_aug(slice(0, 2), 0)

            def ln_stats(n):
                u, b, l = n % 2, n % B, n // B
                if l == 0 and b % 2 == 0:
                    dve.wait_ge(x_in[b // 2], 16)
                if l == 1:
                    dve.wait_ge(x_ready, b + 1)
                if l == 2:
                    dve.wait_ge(x_mid, b + 1)
                    if b < FT // NT:
                        dve.wait_ge(f_x, FT)
                if l == 3:
                    dve.wait_ge(x_mid, B + b + 1)
                for k in range(NT):
                    dve.bn_stats(stats[:, u, k, :], x_all[:, NT * b + k, :]).then_inc(stats_ready, 1)
                for k in range(NT):
                    dve.wait_ge(stats_ready, NT * n + k + 1)
                    dve.bn_aggr(mv[:, u, k, :], stats[:, u, k, :]).then_inc(mv_ready, 1)

            def ln_apply(n):
                u, b = n % 2, n % B
                dve.wait_ge(rstd_ready, n + 1)
                if n >= 2:
                    dve.wait_ge(xnT_psum, n - 1)
                for k in range(NT):
                    i = dve.tensor_scalar(xn[:, u, k, :], x_all[:, NT * b + k, :], mv[:, u, k, 0:1], rstd[:, u, k:k + 1],
                                          ALU.subtract, ALU.mult)
                    if k == NT - 1:
                        i.then_inc(xn_ready, 1)

            def part1(m):
                u = m % 2
                dve.wait_ge(qk_ready, 2 * item(m) + 2)
                if m >= 2:
                    dve.wait_ge(scratch_in[u], 16 * (m // 2))
                dve.tensor_copy(parts[:, u, :, 0, :], qkf[:, u]).then_inc(part1_ready, 1)

            def v_copy(m):
                n = item(m)
                dve.wait_ge(v_psum, n + 1)
                if m == 0:
                    dve.wait_ge(w_in, 48)
                if m in (0, 2):
                    dve.wait_ge(v_aug_ready, m + 2)
                if m >= 4:
                    dve.wait_ge(pv_psum, NG * (m - 3))
                bank = pv_ps[1] if in_middle(n) else prep_ps
                for k in range(NT):
                    i = dve.tensor_tensor(v_aug[:, m % 4, k, :, 0:DH], bank[:, 0, k * D:(k + 1) * D].rearrange("p (h d) -> p h d", d=DH),
                                          b_vo[:, n // B, 0, :].rearrange("p (h d) -> p h d", d=DH), ALU.add)
                    if k == NT - 1:
                        i.then_inc(v_ready, 1)

            def row_max(n, h):
                c = H * n + h
                dve.wait_ge(s1_psum, c + 1)
                if h == 0 and n >= 2:
                    dve.wait_ge(maxT_psum, 2 * (n - 1))
                dve.tensor_reduce(negmax[:, n % 2, :, h], s1_ps[c % 2][:, :, :], axis=AX.X, op=ALU.max,
                                  negate=True).then_inc(max_ready, 1)

            def normalise(n, k):
                u = n % 2
                dve.wait_ge(u_psum, 2 * n + k + 1)
                if n >= 2 and k == 0:
                    dve.wait_ge(oT_psum, n - 1)
                u4 = out_ps[:, :].rearrange("p (h d) -> p h d", d=32)
                dve.reciprocal(den_inv[:, k, :], u4[:, :, DH]).then_inc(inv_ready, 1)
                dve.wait_ge(inv_ready, 2 * n + k + 1)
                dve.tensor_tensor(o_tok[:, u, k, :].rearrange("p (h d) -> p h d", d=DH), u4[:, :, 0:DH],
                                  den_inv[:, k, :].unsqueeze(2).broadcast_to([P, H, DH]), ALU.mult).then_inc(o_ready, 1)

            def residual(n):
                b = n % B
                dve.wait_ge(y_psum, n + 1)
                dve.wait_ge(biased, n + 1)
                x2 = x_all[:, NT * b:NT * b + NT, :]
                dve.tensor_tensor(x2, out_ps[:, 0:S].rearrange("p (t d) -> p t d", d=D), x2, ALU.add).then_inc(x_ready, 1)

            def v_copy_one(n):
                r = n - B
                dve.wait_ge(v_psum, n + 1)
                if r >= 2:
                    dve.wait_ge(o1_psum, r - 1)
                bank = pv_ps[1] if in_middle(n) else prep_ps
                dve.tensor_tensor(v_one[:, r % 2], bank[:, 0, :].rearrange("p (t d) -> p t d", d=D),
                                  b_vo[:, n // B, 0:1, :].broadcast_to([P, NT, D]), ALU.add).then_inc(v_ready, 1)

            def softmax_bias(n):
                r = n - B
                sc = s1_ps[r % 2]
                dve.wait_ge(sc_psum, r + 1)
                if n >= 2 * B:
                    for k in range(NT):
                        dve.tensor_tensor(sc[:, k, k * P:(k + 1) * P], sc[:, k, k * P:(k + 1) * P], causal[:, :],
                                          ALU.add).then_inc(mask_step, 1)
                    dve.wait_ge(mask_step, NT * (n - 2 * B + 1))
                    dve.tensor_reduce(negbias_raw[:, r % 2, 0:1], sc[:, 0, 0:P], axis=AX.X, op=ALU.max,
                                      negate=True).then_inc(negmax1_ready, 1)
                    dve.tensor_reduce(negbias_raw[:, r % 2, 1:2], sc[:, 1, :], axis=AX.X, op=ALU.max,
                                      negate=True).then_inc(negmax1_ready, 1)
                else:
                    dve.tensor_reduce(negbias_raw[:, r % 2, :], sc[:, :, :], axis=AX.X, op=ALU.max,
                                      negate=True).then_inc(negmax1_ready, 2)
                dve.wait_ge(negmax1_ready, 2 * (r + 1))
                if r >= 2:
                    dve.wait_ge(prob_ready, NT * (r - 1))
                dve.tensor_scalar(negbias[:, r % 2, :], negbias_raw[:, r % 2, :], D ** -0.5, None,
                                  ALU.mult).then_inc(bias_ready, 1)

            def residual_one(n):
                r, b = n - B, n % B
                dve.wait_ge(prob_ready, NT * (r + 1))
                dve.reciprocal(den_inv1[:, r % 2, :], den[:, r % 2, :]).then_inc(inv1_ready, 1)
                dve.wait_ge(inv1_ready, r + 1)
                dve.wait_ge(o1_psum, r + 1)
                for k in range(NT):
                    i = dve.scalar_tensor_tensor(out=x_all[:, NT * b + k, :], in0=out_ps[:, k * D:(k + 1) * D],
                                                 scalar=den_inv1[:, r % 2, k:k + 1], in1=x_all[:, NT * b + k, :],
                                                 op0=ALU.mult, op1=ALU.add)
                i.then_inc(x_mid, 1)

            def f_norm():
                dve.wait_ge(x_mid, FT // NT)
                for k in range(FT):
                    dve.bn_stats(f_stats[:, k, :], x_all[:, k, :]).then_inc(f_stats_ready, 1)
                dve.wait_ge(f_stats_ready, FT)
                for k in range(FT):
                    dve.bn_aggr(f_mv[:, k, :], f_stats[:, k, :]).then_inc(f_mv_ready, 1)
                dve.wait_ge(f_rstd_ready, 2)
                for k in range(FT):
                    dve.tensor_scalar(f_xn[:, k, :], x_all[:, k, :], f_mv[:, k, 0:1], f_rstd[:, k:k + 1],
                                      ALU.subtract, ALU.mult).then_inc(f_xn_ready, 1)
                dve.wait_ge(f_in, 48)
                dve.tensor_tensor(f_wsum[:, :], f_ew[:, :, 0], f_ew[:, :, 1], ALU.add).then_inc(f_wsum_ready, 1)

            def f_residual():
                dve.wait_ge(f_wsum_ready, 1)
                dve.wait_ge(f_y_psum, 1)
                for k in range(FT):
                    dve.scalar_tensor_tensor(out=x_all[:, k, :], in0=out_ps[:, k * D:(k + 1) * D], scalar=f_wsum[:, k:k + 1],
                                             in1=x_all[:, k, :], op0=ALU.mult, op1=ALU.add).then_inc(f_x, 1)

            def z_norm_stats(b):
                dve.wait_ge(x_ready, B + b + 1)
                for k in range(NT):
                    dve.bn_stats(z_stats[:, b % 2, k, :], x_all[:, NT * b + k, :]).then_inc(z_stats_ready, 1)
                for k in range(NT):
                    dve.wait_ge(z_stats_ready, NT * b + k + 1)
                    dve.bn_aggr(z_mv[:, b, k, :], z_stats[:, b % 2, k, :]).then_inc(z_mv_ready, 1)

            def z_apply(b):
                dve.wait_ge(rn_ready, b + 1)
                for k in range(NT):
                    i = dve.tensor_scalar(z[:, b % 2, k, :], x_all[:, NT * b + k, :], z_mv[:, b, k, 0:1], z_rstd[:, b, k:k + 1],
                                          ALU.subtract, ALU.mult)
                i.then_inc(z_ready, 1)

            def z_route(b):
                if b == 0:
                    dve.wait_ge(d_in, 96)
                dve.wait_ge(z_ready, b + 1)
                for k in range(NT):
                    c = NT * b + k
                    if c >= 1:
                        dve.wait_ge(s_tok_ready, c)
                    dve.scalar_tensor_tensor(out=s_junk[:, :], in0=z[:, b % 2, k, :], scalar=1.0, in1=route[:, :], op0=ALU.mult,
                                             op1=ALU.mult, accum_out=s_tok[:, b, k:k + 1]).then_inc(s_tok_ready, 1)
                if b >= 2:
                    dve.wait_ge(xrT_psum, b - 1)
                for k in range(NT):
                    i = dve.tensor_scalar(xr[:, b % 2, k, :], z[:, b % 2, k, :], rnorm[:, b, k:k + 1], None, ALU.mult)
                i.then_inc(xr_ready, 1)

            def fold_gamma():
                dve.wait_ge(d_in, 96)
                dve.tensor_scalar(d_w1[:, 0:NC - 1, :], d_w1[:, 0:NC - 1, :], gamma[:, 0:1], D ** 0.5, ALU.mult, ALU.mult).then_inc(d_folded, 1)
                dve.tensor_scalar(d_w1[:, NC - 1, :], d_w1[:, NC - 1, :], gamma[:, 1:2], D ** 0.5, ALU.mult, ALU.mult).then_inc(d_folded, 1)
                dve.memset(ones[:, :], 1.0).then_inc(s_row_ready, 1)
                dve.memset(k_inv[:, :], 1.0 / KEFF).then_inc(s_row_ready, 1)
                dve.memset(level[:, 0:1], S / KEFF * float(np.exp(LEVEL0))).then_inc(chain, 1)

            for lo in MANY:
                if lo == B:
                    fold_gamma()
                    for i in range(B, 3 * B + 1):
                        if i == B + 4:
                            f_residual()
                        if i == B:
                            normalise(B - 1, 0)
                        if B <= i < 3 * B:
                            softmax_bias(i)
                        if i == B:
                            normalise(B - 1, 1)
                        for n in ahead(i, 3):
                            ln_stats(n)
                        if B <= i - 1 < 3 * B:
                            residual_one(i - 1)
                        for n in ahead(i, 1):
                            if n < 3 * B:
                                v_copy_one(n)
                            else:
                                part1(many(n))
                                v_copy(many(n))
                        for n in ahead(i, 3):
                            ln_apply(n)
                        if i == B:
                            residual(B - 1)
                        if i == B + 3:
                            f_norm()
                for i in steps_of(lo):
                    x = prepared(i, lo)
                    for h in range(H):
                        ln = x if lo else i + 3
                        if h == 0 and ln is not None:
                            ln_stats(ln)
                        if has(i + 1, lo):
                            row_max(i + 1, h)
                        if h == 2 and ln is not None:
                            ln_apply(ln)
                        if h == 3 and i == -3:
                            prepare_v_aug(slice(2, 4), 2)
                        if h == 5 and has(i - 1, lo):
                            normalise(i - 1, 0)
                        if h == 7 and has(i - 1, lo):
                            normalise(i - 1, 1)
                        if h == 10 and x is not None and has(i + 3, lo):
                            part1(i + 3)
                        if h == 14 and x is not None:
                            if has(i + 3, lo):
                                v_copy(i + 3)
                            else:
                                v_copy_one(i + 3)
                        if h == 15 and has(i - 1, lo):
                            residual(i - 1)
                        if lo == B and has(i - 2, lo):
                            if h == 1:
                                z_norm_stats(i - 2 - B)
                            if h == 6:
                                z_apply(i - 2 - B)
                            if h == 8:
                                z_route(i - 2 - B)

            dve.wait_ge(s_row_psum, 1)
            dve.tensor_copy(s_row[:, :], pv_ps[0][0:B, 0, :]).then_inc(s_row_ready, 1)
            dve.wait_ge(s_row_ready, 3)
            dve.tensor_reduce(shift[:, :], s_row[:, :], axis=AX.X, op=ALU.max).then_inc(s_row_ready, 1)
            dve.wait_ge(s_row_ready, 4)
            dve.tensor_scalar(shift[:, :], shift[:, :], 0.0, -LEVEL0, ALU.min, ALU.add).then_inc(s_row_ready, 1)
            dve.wait_ge(s_row_ready, 5)

            def reshift():
                dve.tensor_scalar(shifted[:, :], s_row[:, :], shift[:, 0:1], TOP, ALU.subtract, ALU.min).then_inc(shifted_ready, 1)

            def top_half(m):
                r = m // 2
                src = s_row[:, :] if r == 0 else work[(r - 1) % 2][:, :]
                if m >= 1:
                    dve.wait_ge(top_step, m)
                if m % 2 == 0:
                    dve.max(out=top8[:, :], in_=src).then_inc(top_step, 1)
                else:
                    dve.match_replace(out=work[r % 2][:, :], in_to_replace=top8[:, :], in_values=src,
                                      imm_value=NEVER).then_inc(top_step, 1)

            reshift()
            steps, halves = 0, 0
            for j, count in enumerate(BLOCKS):
                for _ in range(TOP_HALVES_AHEAD[j]):
                    top_half(halves)
                    halves += 1
                dve.wait_ge(e_ready, j + 1)
                for k in range(count):
                    a = steps % 2
                    dve.wait_ge(chain, steps + 2 * j + 1)
                    dve.scalar_tensor_tensor(out=min_junk[:, :], in0=e_row[:, :], scalar=level[:, a:a + 1], in1=k_inv[:, :],
                                             op0=ALU.min, op1=ALU.mult, accum_out=level[:, 1 - a:2 - a]).then_inc(chain, 1)
                    steps += 1
                    if halves < 2 * (TOPK // 8) - sum(TOP_HALVES_AHEAD[j + 1:]):
                        top_half(halves)
                        halves += 1
                a = steps % 2
                if j == len(BLOCKS) - 1:
                    break
                bits = level[:, a:a + 1].bitcast(int32)
                dve.wait_ge(chain, steps + 2 * j + 1)
                dve.tensor_scalar(exponent[:, :], bits, 23, None, ALU.logical_shift_right).then_inc(shift_step, 1)
                dve.tensor_scalar(bits, bits, 0x7FFFFF, 0x3F800000, ALU.bitwise_and, ALU.bitwise_or).then_inc(chain, 1)
                dve.wait_ge(shift_step, 3 * j + 1)
                dve.tensor_scalar(expo_f[:, :], exponent[:, :], LN2, -127 * LN2 - LEVEL0, ALU.mult, ALU.add).then_inc(shift_step, 1)
                dve.wait_ge(shift_step, 3 * j + 2)
                dve.tensor_tensor(shift[:, :], shift[:, :], expo_f[:, :], ALU.add).then_inc(shift_step, 1)
                dve.wait_ge(shift_step, 3 * j + 3)
                reshift()
                dve.wait_ge(chain, steps + 2 * j + 2)
                dve.tensor_scalar(level[:, a:a + 1], level[:, a:a + 1], float(np.exp(LEVEL0)), None, ALU.mult).then_inc(chain, 1)
            dve.wait_ge(top_step, 2 * (TOPK // 8))
            dve.tensor_scalar(highest[:, :], work[(TOPK // 8 - 1) % 2][:, :], NEVER, None, ALU.is_equal).then_inc(pick_step, 1)
            assert halves == 2 * (TOPK // 8)
            dve.wait_ge(chain, steps + 2 * (len(BLOCKS) - 1) + 1)
            last_level = level[:, steps % 2:steps % 2 + 1]
            dve.scalar_tensor_tensor(out=at_one[:, :], in0=e_row[:, :], scalar=last_level, in1=ones[:, :], op0=ALU.is_ge,
                                     op1=ALU.mult, accum_out=n_at_one[:, :]).then_inc(pick_step, 1)
            dve.reciprocal(inv_level[:, :], last_level).then_inc(score_step, 1)
            dve.wait_ge(pick_step, 2)
            dve.tensor_tensor_scan(out=place[:, :], data0=ones[:, :], data1=at_one[:, :], initial=0.0, op0=ALU.mult,
                                   op1=ALU.add).then_inc(pick_step, 1)
            dve.tensor_scalar(n_at_one[:, :], n_at_one[:, :], float(TOPK), None, ALU.is_le).then_inc(pick_step, 1)
            dve.wait_ge(score_step, 1)
            dve.tensor_scalar(score[:, :], e_row[:, :], inv_level[:, :], 1.0, ALU.mult, ALU.min).then_inc(score_step, 1)
            dve.wait_ge(pick_step, 4)
            dve.scalar_tensor_tensor(out=at_one[:, :], in0=place[:, :], scalar=float(TOPK), in1=at_one[:, :], op0=ALU.is_le,
                                     op1=ALU.mult).then_inc(pick_step, 1)
            dve.wait_ge(score_step, 2)
            dve.tensor_scalar(weight[:, :], score[:, :], -1.0, 1.0, ALU.mult, ALU.add).then_inc(score_step, 1)
            dve.wait_ge(pick_step, 5)
            dve.scalar_tensor_tensor(out=at_one[:, :], in0=highest[:, :], scalar=n_at_one[:, :], in1=at_one[:, :], op0=ALU.mult,
                                     op1=ALU.max).then_inc(pick_step, 1)
            dve.wait_ge(score_step, 3)
            dve.tensor_tensor(weight[:, :], weight[:, :], score[:, :], ALU.add).then_inc(score_step, 1)
            dve.wait_ge(pick_step, 6)
            dve.wait_ge(score_step, 4)
            dve.tensor_tensor(weight[:, :], at_one[:, :], weight[:, :], ALU.mult).then_inc(weight_ready, 1)
            dve.wait_ge(w_psum, 1)
            dve.tensor_copy(w_tok[:, :, :].rearrange("p t b -> p (t b)"), pv_ps[1][:, 0, 0:NT * B]).then_inc(w_ready, 1)
            dve.wait_ge(w_ready, 1)
            for b in range(B):
                for k in range(NT):
                    c = NT * b + k
                    if k == 0:
                        dve.wait_ge(heavy_ready, b + 1)
                        dve.wait_ge(light_done, b + 1)
                    dve.scalar_tensor_tensor(out=x_all[:, c, :], in0=heavy[:, c, :], scalar=w_tok[:, k, b:b + 1], in1=x_all[:, c, :],
                                             op0=ALU.mult, op1=ALU.add).then_inc(x_final, 1)

        @block.tensor
        def _(pe):
            pe.wait_ge(pool_const, 4)

            def xn_transpose(n):
                u = n % 2
                bank = pv_ps[0] if in_middle(n) else prep_ps
                pe.wait_ge(xn_ready, n + 1)
                for k in range(NT):
                    i = pe.transpose(bank[:, 0, k * P:(k + 1) * P], xn[:, u, k, :], ident[:, :])
                i.then_inc(xnT_psum, 1)

            def qk_project(n):
                u, l = n % 2, n // B
                pe.wait_ge(xnT_ready, n + 1)
                if n == 0:
                    pe.wait_ge(w_in, 48)
                pe.matmul(prep_ps[:, 0, :], w_att[:, l, 0, :], xnT[:, u, :], start=True, stop=True)
                pe.matmul(prep_ps[:, 1, :], w_att[:, l, 1, :], xnT[:, u, :] if l in SELF else ctxT[:, S * (n % B):S * (n % B + 1)],
                          start=True, stop=True).then_inc(qk_psum, 1)

            def v_project(n):
                u, l = n % 2, n // B
                bank = pv_ps[1] if in_middle(n) else prep_ps
                for k in range(NT):
                    src = xnT[:, u, k * P:(k + 1) * P] if l in SELF else ctxT[:, S * (n % B) + k * P:S * (n % B) + (k + 1) * P]
                    i = pe.matmul(bank[:, 0, k * D:(k + 1) * D], src, w_att[:, l, 2, :], start=True, stop=True)
                i.then_inc(v_psum, 1)

            def scores_for_max(n, h):
                c, s3 = H * n + h, n % 3
                if h == 0:
                    pe.wait_ge(stacked[s3], 96 * (n // 3 + 1))
                    if n < 3:
                        pe.wait_ge(filled[s3], 32)
                if c >= 2:
                    pe.wait_ge(max_ready, c - 1)
                for k in range(NT):
                    i = pe.matmul(s1_ps[c % 2][:, k, :], stack[0:96, s3, 0, h, k * P:(k + 1) * P], stack[0:96, s3, 1, h, :],
                                  start=True, stop=True)
                i.then_inc(s1_psum, 1)

            def max_transpose(n, hf):
                pe.wait_ge(max_ready, H * n + 8 * hf + 8)
                for k in range(NT):
                    i = pe.transpose(prep_bf[0:8, 0, k * P:(k + 1) * P], negmax[:, n % 2, k, 8 * hf:8 * hf + 8], ident_bf[:, :])
                i.then_inc(maxT_psum, 1)

            def scores(n, h):
                c, s3 = H * n + h, n % 3
                if h % 8 == 0:
                    pe.wait_ge(max_in[s3][h // 8], 16 * (n // 3 + 1))
                if c >= 2:
                    pe.wait_ge(exp_ready, c - 1)
                for k in range(NT):
                    i = pe.matmul(s2_ps[c % 2][:, k, :], stack[0:97, s3, 1, h, k * P:(k + 1) * P], stack[0:97, s3, 0, h, :],
                                  start=True, stop=True)
                i.then_inc(s2_psum, 1)

            def weighted_sum(n, g):
                pe.wait_ge(exp_ready, H * n + G * (g + 1))
                if g == 0:
                    pe.wait_ge(v_ready, item(n) + 1)
                if g % 2 == 0 and n >= 1:
                    pe.wait_ge(uT_ready, 2 * (n - 1) + g // 2 + 1)
                for k in range(NT):
                    for j in range(G):
                        i = pe.matmul(pv_ps[g // 2][32 * j:32 * j + 32, g % 2, :], v_aug[:, n % 4, k, G * g + j, :],
                                      probT[:, (G * g + j) % 8, k, :], start=(k == 0), stop=(k == NT - 1))
                i.then_inc(pv_psum, 1)

            def u_transpose(n, k):
                if k == 0:
                    pe.wait_ge(uT_ready, 2 * n + 2)
                    if n >= 1:
                        pe.wait_ge(x_ready, n)
                else:
                    pe.wait_ge(o_ready, 2 * n + 1)
                for g in range(NG):
                    i = pe.transpose(out_ps[:, g * P:(g + 1) * P], uT[:, n % 2, g, k * P:(k + 1) * P], ident[:, :])
                i.then_inc(u_psum, 1)

            def o_transpose(n):
                pe.wait_ge(o_ready, 2 * n + 2)
                for k in range(NT):
                    i = pe.transpose(out_ps[:, k * P:(k + 1) * P], o_tok[:, n % 2, k, :], ident[:, :])
                i.then_inc(oT_psum, 1)

            def xr_transpose(b):
                pe.wait_ge(xr_ready, b + 1)
                for k in range(NT):
                    i = pe.transpose(prep_ps[:, 0, k * P:(k + 1) * P], xr[:, b % 2, k, :], ident[:, :])
                i.then_inc(xrT_psum, 1)

            def out_project(n):
                pe.wait_ge(oT_ready, n + 1)
                for k in range(NT):
                    i = pe.matmul(out_ps[:, k * D:(k + 1) * D], oT[:, n % 2, k * P:(k + 1) * P], w_att[:, item(n) // B, 3, :],
                                  start=True, stop=True)
                i.then_inc(y_psum, 1)

            def scores_one(n):
                r, u = n - B, n % 2
                pe.wait_ge(qk_ready, 2 * n + 2)
                if r >= 2:
                    pe.wait_ge(prob_ready, NT * (r - 1))
                for k in range(NT):
                    w = P if n >= 2 * B and k == 0 else S
                    i = pe.matmul(s1_ps[r % 2][:, k, 0:w], qkf[:, u, 0, k * P:(k + 1) * P], qkf[:, u, 1, 0:w], start=True, stop=True)
                i.then_inc(sc_psum, 1)

            def prob_tiles(n):
                tiles = [(0, 0), (1, 0), (1, 1)] if n >= 2 * B else [(0, 0), (1, 0), (1, 1), (0, 1)]
                return [(q, k, c * P) for c, (q, k) in enumerate(tiles)]

            def prob_transpose(n):
                r = n - B
                pe.wait_ge(prob_ready, NT * (r + 1))
                if r >= 2:
                    pe.wait_ge(probT_ready, r - 1)
                bank = s2_ps[r % 2][:, :, :].rearrange("p t q -> p (t q)")
                for q, k, c in prob_tiles(n):
                    i = pe.transpose(bank[:, c:c + P], prob[:, r % 2, q, k * P:(k + 1) * P], ident[:, :])
                i.then_inc(probT_psum, 1)

            def weighted_sum_one(n):
                r = n - B
                pe.wait_ge(probT_ready, r + 1)
                pe.wait_ge(v_ready, n + 1)
                if r >= 1:
                    pe.wait_ge(x_mid, r)
                for q in range(NT):
                    tiles = sorted((k, c) for q2, k, c in prob_tiles(n) if q2 == q)
                    for k, c in tiles:
                        i = pe.matmul(out_ps[:, q * D:(q + 1) * D], probT1[:, r % 2, c:c + P], v_one[:, r % 2, k, :],
                                      start=(k == 0), stop=(k == tiles[-1][0]))
                i.then_inc(o1_psum, 1)

            def expert_ffn():
                pe.wait_ge(f_xn_ready, FT)
                pe.wait_ge(qk_ready, 2 * (B + 5))
                for k in range(FT):
                    i = pe.transpose(prep_ps[:, k // 2, (k % 2) * P:(k % 2 + 1) * P], f_xn[:, k, :], ident[:, :])
                i.then_inc(f_xnT_psum, 1)
                pe.wait_ge(f_xnT_ready, 1)
                pe.wait_ge(f_in, 48)
                pe.wait_ge(probT_ready, 4)
                for f in range(NF):
                    if f >= 2:
                        pe.wait_ge(f_h_ready, f - 1)
                    pe.matmul(s2_ps[f % 2][:, :, :].rearrange("p t q -> p (t q)"), f_w1[:, f, :], f_xnT[:, :],
                              start=True, stop=True).then_inc(f_h_psum, 1)
                pe.wait_ge(f_h_ready, NF)
                pe.wait_ge(x_mid, 3)
                for k in range(FT):
                    for f in range(NF):
                        i = pe.matmul(out_ps[:, k * D:(k + 1) * D], f_hT[:, f, k * P:(k + 1) * P], f_w2[:, f, :],
                                      start=(f == 0), stop=(f == NF - 1))
                i.then_inc(f_y_psum, 1)

            for lo in MANY:
                if lo == B:
                    for i in range(B, 3 * B + 1):
                        if i == B:
                            weighted_sum(B - 1, 3)
                            pe.wait_ge(max_ready, H * B)
                        if i == B + 4:
                            expert_ffn()
                            pe.wait_ge(f_h_ready, NF)
                            pe.wait_ge(f_x, FT)
                        if B <= i < 3 * B:
                            scores_one(i)
                        if i == B:
                            u_transpose(B - 1, 0)
                        if i == B + 1:
                            pe.wait_ge(v_ready, B + AHEAD)
                            pe.wait_ge(uT_ready, 2 * B)
                            pe.wait_ge(x_ready, B)
                        for n in ahead(i, 1):
                            pe.wait_ge(qk_ready, 2 * n)
                            qk_project(n)
                        if B <= i - 1 < 3 * B:
                            weighted_sum_one(i - 1)
                        for n in ahead(i, 2):
                            pe.wait_ge(xnT_ready, n)
                            if i == B:
                                pe.wait_ge(uT_ready, 2 * B - 1)
                            xn_transpose(n)
                        if i == B:
                            u_transpose(B - 1, 1)
                            pe.wait_ge(exp_ready, H * B)
                        for n in ahead(i, 1):
                            pe.wait_ge(v_ready, n)
                            v_project(n)
                        if B <= i < 3 * B:
                            prob_transpose(i)
                        if i == B:
                            o_transpose(B - 1)
                            out_project(B - 1)
                    pe.wait_ge(prob_ready, NT * 2 * B)
                prep_free = (qk_ready, 2 * (3 * B + AHEAD_C)) if lo else None
                for i in steps_of(lo):
                    x = prepared(i, lo)
                    if i == B:
                        pe.wait_ge(probT_ready, 2 * B)
                        pe.wait_ge(xnT_ready, 3 * B + AHEAD_C)
                        pe.wait_ge(v_ready, 3 * B + AHEAD_C)
                        pe.wait_ge(x_mid, 2 * B)
                    if x == B:
                        pe.wait_ge(ctx_in, 16)
                        pe.wait_ge(w_rest_in, 16)
                    for h in range(H):
                        if has(i, lo):
                            scores(i, h)
                        if has(i + 1, lo):
                            scores_for_max(i + 1, h)
                        if h == 1 and has(i - 1, lo):
                            weighted_sum(i - 1, 3)
                        if h == 2 and has(i, lo):
                            if prep_free:
                                pe.wait_ge(*prep_free)
                            max_transpose(i, 1)
                            prep_free = (maxT_ready, 2 * i + 2)
                        if h == 4 and has(i - 1, lo):
                            u_transpose(i - 1, 0)
                        if h == 5 and x is not None:
                            if prep_free:
                                pe.wait_ge(*prep_free)
                            xn_transpose(x)
                            prep_free = (xnT_ready, x + 1)
                        if h % 4 == 1 and h >= 5 and has(i, lo):
                            weighted_sum(i, (h - 5) // 4)
                        if h == 6 and has(i - 1, lo):
                            u_transpose(i - 1, 1)
                        if h == 8 and x is not None:
                            qk_project(x)
                            prep_free = (qk_ready, 2 * (x + 1))
                        if h == 10 and has(i - 1, lo):
                            o_transpose(i - 1)
                        if h == 10 and has(i + 1, lo):
                            if prep_free:
                                pe.wait_ge(*prep_free)
                            max_transpose(i + 1, 0)
                            prep_free = (maxT_ready, 2 * (i + 1) + 1)
                        if h == 13 and x is not None:
                            if prep_free:
                                pe.wait_ge(*prep_free)
                            v_project(x)
                            prep_free = (v_ready, x + 1)
                        if h == 14 and has(i - 1, lo):
                            out_project(i - 1)
                        if h == 15 and lo == B and has(i - 2, lo) and i - 2 < lo + B - 1:
                            if prep_free:
                                pe.wait_ge(*prep_free)
                            xr_transpose(i - 2 - B)
                            prep_free = (xrT_ready, i - 2 - B + 1)
            pe.wait_ge(x_ready, 2 * B)
            pe.wait_ge(v_ready, 4 * B)
            pe.wait_ge(maxT_ready, 4 * B)
            pe.wait_ge(max_ready, 2 * H * B)
            pe.wait_ge(exp_ready, 2 * H * B)
            pe.wait_ge(uT_ready, 4 * B)
            def up(q):
                pe.wait_ge(xrT_ready, 2 * q + 2)
                for f in range(NC):
                    c = NC * q + f
                    if c >= 2:
                        pe.wait_ge(d_h_ready, c - 1)
                    pe.matmul(s2_ps[c % 2][:, :, :].rearrange("p t q -> p (t q)"), d_w1[:, f, :], xrT[:, 2 * S * q:2 * S * (q + 1)],
                              start=True, stop=True).then_inc(d_h_psum, 1)

            def weight_transpose():
                pe.wait_ge(weight_ready, 1)
                for k in range(NT):
                    i = pe.transpose(pv_ps[1][:, 0, k * B:(k + 1) * B], weight[:, k * P:(k + 1) * P], ident[0:B, 0:B])
                i.then_inc(w_psum, 1)

            def down(q):
                pe.wait_ge(xrT_ready, B)
                for e in range(2):
                    b = 2 * q + e
                    pe.wait_ge(d_h_ready, NC * (q + 1))
                    if b >= 2:
                        pe.wait_ge(light_done, b - 1)
                        pe.wait_ge(heavy_copied, b - 1)
                    toks = [slice((NT * e + k) * P, (NT * e + k + 1) * P) for k in range(NT)]
                    for k in range(NT):
                        for f in range(NC - 1):
                            i = pe.matmul(heavy_bank(b)[:, k, :], d_hT[:, q % 2, f, toks[k]], d_w2[:, f, :],
                                          start=(f == 0), stop=(f == NC - 2))
                    i.then_inc(d_y_psum, 1)
                    if b == B - 1:
                        weight_transpose()
                    pe.wait_ge(light_bias, b + 1)
                    for k in range(NT):
                        pe.matmul(light_bank(b)[:, k, :], ident[:, :], x_all[:, NT * b + k, :], start=True, stop=False)
                        i = pe.matmul(light_bank(b)[:, k, :], d_hT[:, q % 2, NC - 1, toks[k]], d_w2[:, NC - 1, :],
                                      start=False, stop=True)
                    i.then_inc(d_y_psum, 1)

            pe.wait_ge(d_folded, 2)
            up(0)
            xr_transpose(B - 1)
            pe.wait_ge(s_tok_ready, NT * B)
            for k in range(NT):
                i = pe.transpose(pv_ps[0][0:B, 0, k * P:(k + 1) * P], s_tok[:, :, k], ident[:, :])
            i.then_inc(s_row_psum, 1)
            for q in range(5):
                if 1 <= q < 4:
                    up(q)
                if q >= 1:
                    down(q - 1)


def laid_out(i):
    def pad(a, axis):
        return np.concatenate([a, np.zeros(a.shape[:axis] + (P - a.shape[axis],) + a.shape[axis + 1:], a.dtype)], axis)

    perm = np.arange(D).reshape(H, DH).T.reshape(-1)
    wqkv = i["L0_attn_W_qkv"].T
    bqkv = i["L0_attn_b_qkv"]
    out = {"x": i["x"], "ctxT": i["ctx_1024"].reshape(B * S, D).T}
    none, nob = np.zeros((D, D), np.float32), np.zeros(D, np.float32)
    w3, b3 = i["L1_attn_W_qkv"].T, i["L1_attn_b_qkv"]
    out["w_att"] = np.stack([
        np.stack([wqkv[:, 0:D][:, perm], wqkv[:, D:2 * D][:, perm], wqkv[:, 2 * D:], i["L0_attn_W_out"].T]),
        np.stack([i["L0_xattn_Wq"], i["L0_xattn_Wk"], i["L0_xattn_Wv"], none]),
        np.stack([w3[:, 0:D], w3[:, D:2 * D], w3[:, 2 * D:], none]),
        np.stack([i["L1_xattn_Wq"][:, perm], i["L1_xattn_Wk"][:, perm], i["L1_xattn_Wv"], i["L1_xattn_Wo"]])])
    out["b_qk"] = np.stack([np.stack([bqkv[0:D][perm], bqkv[D:2 * D][perm]], -1),
                            np.stack([i["L0_xattn_bq"], i["L0_xattn_bk"]], -1),
                            np.stack([b3[0:D], b3[D:2 * D]], -1),
                            np.stack([i["L1_xattn_bq"][perm], i["L1_xattn_bk"][perm]], -1)], 1)
    out["b_vo"] = np.stack([np.stack([bqkv[2 * D:], i["L0_attn_b_out"]]), np.stack([i["L0_xattn_bv"], nob]),
                            np.stack([b3[2 * D:], nob]), np.stack([i["L1_xattn_bv"], i["L1_xattn_bo"]])])
    out["f_w1"] = i["L0_ffn_w1"].reshape(D, NF, P)
    out["f_w2"] = i["L0_ffn_w2"].reshape(NF, P, D).transpose(1, 0, 2)
    out["f_ew"] = i["L0_ffn_expert_weights"].reshape(FT, P, 2).transpose(1, 0, 2)
    out["d_w1"] = np.concatenate([i["L1_ffn_w1_h"].T, pad(i["L1_ffn_w1_l"].T, 1)], 1).reshape(D, NC, P)
    out["d_w2"] = np.concatenate([i["L1_ffn_w2_h"].T, pad(i["L1_ffn_w2_l"].T, 0)], 0).reshape(NC, P, D).transpose(1, 0, 2)
    out["d_b1"] = np.concatenate([i["L1_ffn_b1_h"], pad(i["L1_ffn_b1_l"], 0)]).reshape(NC, P).T
    out["d_b2"] = np.stack([i["L1_ffn_b2_h"], i["L1_ffn_b2_l"]])
    out["gamma"] = np.stack([i["L1_ffn_gamma_h"], i["L1_ffn_gamma_l"]], -1)
    out["route"] = i["L1_ffn_routing_token"]
    return {k: np.ascontiguousarray(v) for k, v in out.items()}


def kernel(**inputs):
    import concourse.bacc as bacc
    from concourse.bass_utils import run_bass_kernel_spmd
    arrays = laid_out({k: np.asarray(v) for k, v in inputs.items()})
    nc = bacc.Bacc("TRN2", target_bir_lowering=False, num_devices=1)
    dram = {k: nc.dram_tensor(k, a.shape, mybir.dt.from_np(a.dtype), kind="ExternalInput").ap() for k, a in arrays.items()}
    dram["out"] = nc.dram_tensor("out", (B, S, D), fp32, kind="ExternalOutput").ap()
    build(nc, dram)
    r = run_bass_kernel_spmd(nc, [arrays], core_ids=[0])
    return r.results[0]["out"]
```

```python
import concourse.bass as bass
from concourse import mybir
from contextlib import ExitStack
import numpy as np

fp32 = mybir.dt.float32
bf16 = mybir.dt.bfloat16
int32 = mybir.dt.int32
ALU = mybir.AluOpType
ACT = mybir.ActivationFunctionType
AX = mybir.AxisListType

B, S, D = 8, 256, 128
P = 128
NT = S // P
H, DH = 16, 8
G = 4
NG = H // G
EPS = 1e-5
L = 4
FT = 4
NF = 8
NC = 5
KEFF = 144.0
TOPK = 128
NEVER = -3e38
TOP_HALVES_AHEAD = (3, 1)
BLOCKS = (25, 24)
LEVEL0 = 62.0
SHIFT_AT = (2, 4)
TOP = 80.0
LN2 = float(np.log(2.0))
KV_AT = {-2: (8, 14), -1: (0, 2, 4, 10, 12, 14)}
FIRST = (0, B)
UP_AT = (2, 5, 8, 12, 14)
AHEAD = 2
AHEAD_C = 3
SELF = (0, 2)


def build(nc, t):
    ctx = ExitStack()
    with ctx:
        def sb(name, shape, dt=fp32):
            return ctx.enter_context(nc.sbuf_tensor(name + "_sb", shape, dt))

        def ps(name, shape, dt=fp32):
            return ctx.enter_context(nc.psum_tensor(name, shape, dt))

        def sem(name):
            return ctx.enter_context(nc.semaphore(name))

        x_all = sb("x_all", [P, B * NT, D])
        ctxT = sb("ctxT", [P, B * S])
        ident = sb("ident", [P, P])
        ident_bf = sb("ident_bf", [P, P], bf16)
        minus_half = sb("minus_half", [P, FT])
        fill = sb("fill", [97, S], bf16)
        w_att = sb("w_att", [P, L, 4, D])
        b_qk = sb("b_qk", [P, L, 2])
        b_vo = sb("b_vo", [P, L, 2, D])

        stats = sb("stats", [P, 2, NT, 6])
        mv = sb("mv", [P, 2, NT, 2])
        rstd = sb("rstd", [P, 2, NT])
        xn = sb("xn", [P, 2, NT, D])
        xnT = sb("xnT", [P, 2, S])
        qkf = sb("qkf", [P, 2, 2, S])
        rest = sb("rest", [P, 2, S])
        parts = sb("parts", [P, 2, 2, 3, S], bf16)
        stack = sb("stack", [P, 3, 2, H, S], bf16)
        v_aug = sb("v_aug", [P, 4, NT, H, 32])
        negmax = sb("negmax", [P, 2, NT, H], bf16)
        maxrow = sb("maxrow", [DH, 2, 2, S], bf16)
        probT = sb("probT", [P, 8, NT, S])
        uT = sb("uT", [P, 2, NG, S])
        den_inv = sb("den_inv", [P, NT, H])
        o_tok = sb("o_tok", [P, 2, NT, D])
        oT = sb("oT", [P, 2, S])

        k_ctx = sb("k_ctx", [P, B * S])
        v_ctx = sb("v_ctx", [P, B, NT, D])
        v_one = sb("v_one", [P, 2, NT, D])
        negbias = sb("negbias", [P, 2, NT])
        negbias_raw = sb("negbias_raw", [P, 2, NT])
        prob = sb("prob", [P, 2, NT, S])
        probT1 = sb("probT1", [P, 2, NT * S])
        den = sb("den", [P, 2, NT])
        den_inv1 = sb("den_inv1", [P, 2, NT])
        causal = sb("causal", [P, P])

        f_stats = sb("f_stats", [P, FT, 6])
        f_mv = sb("f_mv", [P, FT, 2])
        f_rstd = sb("f_rstd", [P, FT])
        f_xn = sb("f_xn", [P, FT, D])
        f_xnT = sb("f_xnT", [P, FT * P])
        f_hT = probT[:, :, :, :].rearrange("p h t q -> p (h t q)").rearrange("p (f q) -> p f q", f=NF)
        f_w1 = sb("f_w1", [P, NF, P])
        f_w2 = sb("f_w2", [P, NF, D])
        f_ew = sb("f_ew", [P, FT, 2])
        f_wsum = sb("f_wsum", [P, FT])

        route = sb("route", [P, D])
        s_tok = sb("s_tok", [P, B, NT])
        z = sb("z", [P, 2, NT, D])
        z_stats = sb("z_stats", [P, 2, NT, 6])
        z_mv = sb("z_mv", [P, B, NT, 2])
        z_rstd = sb("z_rstd", [P, B, NT])
        s_junk = sb("s_junk", [P, D])
        rnorm = sb("rnorm", [P, B, NT])
        xr = sb("xr", [P, 2, NT, D])
        xrT = sb("xrT", [P, B * S])
        d_w1 = sb("d_w1", [P, NC, P])
        d_b1 = sb("d_b1", [P, NC])
        d_w2 = sb("d_w2", [P, NC, D])
        d_b2 = sb("d_b2", [P, 2, D])
        gamma = sb("gamma", [P, 2])
        stack_free = stack[:, :, :, :, :].rearrange("p s a h n -> p (s a h n)").bitcast(fp32)
        d_hT = stack_free[:, 0:8 * NC * P].rearrange("p (u f q) -> p u f q", u=2, f=NC)
        heavy = stack_free[:, 8 * NC * P:8 * NC * P + B * S].rearrange("p (t d) -> p t d", d=D)

        rows_free = iter(range(8 * NC * P + B * S, 3 * H * S, S))

        def row():
            first = next(rows_free)
            return stack_free[0:B, first:first + S]

        s_row = row()
        shifted = row()
        e_row = row()
        k_inv = sb("k_inv", [B, S])
        min_junk = row()
        level = sb("level", [B, 2])
        exponent = sb("exponent", [B, 1], int32)
        expo_f = sb("expo_f", [B, 1])
        shift = sb("shift", [B, 1])
        ones = sb("ones", [B, S])
        at_one = row()
        n_at_one = sb("n_at_one", [B, 1])
        place = row()
        highest = row()
        inv_level = sb("inv_level", [B, 1])
        score = row()
        work = [row(), row()]
        top8 = sb("top8", [B, 8])
        weight = row()
        w_tok = sb("w_tok", [P, NT, B])

        s1_ps = [ps(f"s1_ps{i}", [P, NT, S]) for i in range(2)]
        s2_ps = [ps(f"s2_ps{i}", [P, NT, S]) for i in range(2)]
        pv_ps = [ps(f"pv_ps{i}", [P, 2, S]) for i in range(2)]
        prep_ps = ps("prep_ps", [P, 2, S])
        out_ps = ps("out_ps", [P, 512])
        prep_bf = prep_ps[:, :, :].bitcast(bf16)

        scratch = [nc.dram_tensor(f"scratch{i}", [2, 3, DH, H, S], bf16).ap() for i in range(2)]

        x_in = [sem(f"x_in{i}") for i in range(4)]
        w_in, w_cross_in, w_rest_in = sem("w_in"), sem("w_cross_in"), sem("w_rest_in")
        ctx_in = [sem(f"ctx_in{i}") for i in range(2)]
        kv_psum, kv_copied, v_ctx_ready = sem("kv_psum"), sem("kv_copied"), sem("v_ctx_ready")
        fill_ready = sem("fill_ready")
        filled = [sem(f"filled{i}") for i in range(3)]
        v_aug_ready, pool_const = sem("v_aug_ready"), sem("pool_const")
        stats_ready, mv_ready, rstd_step, rstd_ready, xn_ready = (
            sem("stats_ready"), sem("mv_ready"), sem("rstd_step"), sem("rstd_ready"), sem("xn_ready"))
        xnT_psum, xnT_ready, qk_psum, qk_ready = sem("xnT_psum"), sem("xnT_ready"), sem("qk_psum"), sem("qk_ready")
        part1_ready, rest_ready, parts_ready = sem("part1_ready"), sem("rest_ready"), sem("parts_ready")
        v_psum, v_ready = sem("v_psum"), sem("v_ready")
        scratch_in = [sem(f"scratch_in{i}") for i in range(2)]
        stacked = [sem(f"stacked{i}") for i in range(3)]
        s1_psum, max_ready, maxT_psum, maxT_ready = sem("s1_psum"), sem("max_ready"), sem("maxT_psum"), sem("maxT_ready")
        max_in = [[sem(f"max_in{i}{hf}") for hf in range(2)] for i in range(3)]
        s2_psum, exp_ready, pv_psum, uT_ready = sem("s2_psum"), sem("exp_ready"), sem("pv_psum"), sem("uT_ready")
        u_psum, inv_ready, o_ready = sem("u_psum"), sem("inv_ready"), sem("o_ready")
        oT_psum, oT_ready, y_psum = sem("oT_psum"), sem("oT_ready"), sem("y_psum")
        biased, x_ready = sem("biased"), sem("x_ready")
        causal_step = sem("causal_step")
        sc_psum, mask_step, negmax1_ready, bias_ready, prob_ready = (
            sem("sc_psum"), sem("mask_step"), sem("negmax1_ready"), sem("bias_ready"), sem("prob_ready"))
        probT_psum, probT_ready, o1_psum, inv1_ready, x_mid = (
            sem("probT_psum"), sem("probT_ready"), sem("o1_psum"), sem("inv1_ready"), sem("x_mid"))
        f_in, f_stats_ready, f_mv_ready, f_rstd_ready, f_xn_ready = (
            sem("f_in"), sem("f_stats_ready"), sem("f_mv_ready"), sem("f_rstd_ready"), sem("f_xn_ready"))
        f_xnT_psum, f_xnT_ready, f_h_psum, f_h_ready, f_y_psum, f_wsum_ready, f_x = (
            sem("f_xnT_psum"), sem("f_xnT_ready"), sem("f_h_psum"), sem("f_h_ready"), sem("f_y_psum"), sem("f_wsum_ready"), sem("f_x"))
        d_in, d_folded, s_tok_ready, z_stats_ready, z_mv_ready, z_ready, rn_step, rn_ready = (
            sem("d_in"), sem("d_folded"), sem("s_tok_ready"), sem("z_stats_ready"), sem("z_mv_ready"), sem("z_ready"), sem("rn_step"), sem("rn_ready"))
        xr_ready, xrT_psum, xrT_ready, light_bias = sem("xr_ready"), sem("xrT_psum"), sem("xrT_ready"), sem("light_bias")
        d_h_psum, d_h_ready, d_y_psum, light_done, heavy_copied, heavy_ready = (
            sem("d_h_psum"), sem("d_h_ready"), sem("d_y_psum"), sem("light_done"), sem("heavy_copied"), sem("heavy_ready"))
        shift_step, top_step, pick_step, score_step = sem("shift_step"), sem("top_step"), sem("pick_step"), sem("score_step")
        s_row_psum, s_row_ready, chain, shifted_ready, e_ready = (
            sem("s_row_psum"), sem("s_row_ready"), sem("chain"), sem("shifted_ready"), sem("e_ready"))
        weight_ready, w_psum, w_ready, x_final = (
            sem("weight_ready"), sem("w_psum"), sem("w_ready"), sem("x_final"))
        out_done = [sem(f"out_done{i}") for i in range(4)]

        block = ctx.enter_context(nc.Block())
        MANY = (0, B)

        def has(n, lo):
            return lo <= n < lo + B

        def prepared(i, lo):
            if lo == 0 and i + 3 < B + AHEAD:
                return i + 3
            if lo == B and lo + AHEAD_C <= i + 3 < lo + B:
                return item(i + 3)
            return None

        def v_count(n):
            return n + 1 if n < B else max(B, n + 1 - B)

        def in_middle(n):
            return B + AHEAD <= n < 3 * B + AHEAD_C

        def ahead(i, d):
            return [n for n in (i + d, i + d + 1) if n - i == d + (n >= 3 * B) and in_middle(n)]

        FFN_STEP = B + 5

        def at(lo, first, second):
            return second if lo else first

        def steps_of(lo):
            return range(-3, B) if lo == 0 else range(B - 1, 2 * B + 2)

        def item(m):
            return m if m < B else m + 2 * B

        def batch(n):
            return n % B if n < 2 * B else (n + FT // NT) % B

        def tiles(n):
            return slice(NT * batch(n), NT * batch(n) + NT)

        def last_tiles(b):
            return tiles(3 * B + b)

        def many(n):
            return n if n < B else n - 2 * B

        out_ps2 = out_ps[:, :].rearrange("p (t q) -> p t q", q=S)

        def up_bank(c):
            return (s1_ps if c < NC else s2_ps)[c % 2][:, :, :].rearrange("p t q -> p (t q)")

        def heavy_bank(b):
            return s1_ps[b % 2][:, 0, :].rearrange("p (t d) -> p t d", d=D)

        def light_bank(b):
            return (prep_ps, out_ps2)[b % 2][:, 0, :].rearrange("p (t d) -> p t d", d=D)

        def split(eng, m):
            n, u = m, m % 2
            eng.wait_ge(part1_ready, n + 1)
            eng.tensor_tensor(rest[:, :, :], qkf[:, u], parts[:, u, :, 0, :], ALU.subtract).then_inc(rest_ready, 1)
            eng.tensor_tensor(parts[:, u, :, 1, :], qkf[:, u], parts[:, u, :, 0, :], ALU.subtract).then_inc(rest_ready, 1)
            eng.wait_ge(rest_ready, 2 * n + 2)
            eng.tensor_tensor(parts[:, u, :, 2, :], rest[:, :, :], parts[:, u, :, 1, :], ALU.subtract).then_inc(parts_ready, 1)
            eng.wait_ge(parts_ready, n + 1)

        @block.sync
        def _(sp):
            def load_x(c):
                tiles = slice(4 * c, 4 * c + 4)
                sp.dma_start(x_all[:, tiles, :], t["x"].rearrange("b (t p) d -> p (b t) d", p=P)[:, tiles, :]).then_inc(x_in[c], 16)

            load_x(0)
            sp.dma_start(w_att[:, 0:1, :, :], t["w_att"][0:1].rearrange("l w p d -> p l w d")).then_inc(w_in, 16)
            sp.dma_start(b_qk[:, :, :], t["b_qk"]).then_inc(w_in, 16)
            sp.dma_start(b_vo[:, :, :, :].rearrange("p l w d -> p (l w d)"), t["b_vo"].rearrange("l w d -> (l w d)").partition_broadcast(P)).then_inc(w_in, 16)
            def fill_stack(s3):
                sp.dma_start(stack[6 * DH:96, s3].rearrange("p a h n -> p (a h) n"),
                             fill[6 * DH:96, :].unsqueeze(1).broadcast_to([96 - 6 * DH, 2 * H, S])).then_inc(filled[s3], 16)
                sp.dma_start(stack[96:97, s3, 1], fill[96:97, :].unsqueeze(1).broadcast_to([1, H, S])).then_inc(filled[s3], 16)

            sp.wait_ge(fill_ready, 2)
            fill_stack(0)
            load_x(1)
            sp.dma_start(w_att[:, 1:2, :, :], t["w_att"][1:2].rearrange("l w p d -> p l w d")).then_inc(w_cross_in, 16)

            def load_ctx(part):
                half = slice(part * B * S // 2, (part + 1) * B * S // 2)
                sp.dma_start(ctxT[:, half], t["ctxT"][:, half]).then_inc(ctx_in[part], 16)

            load_ctx(0)

            def load_for_later(i):
                if i == -2:
                    load_ctx(1)
                if i in (-2, -1):
                    fill_stack(i + 3)
                    load_x(i + 4)
                if i == 0:
                    sp.dma_start(w_att[:, 2:L, :, :], t["w_att"][2:L].rearrange("l w p d -> p l w d")).then_inc(w_rest_in, 16)
                if i == 3:
                    sp.dma_start(f_w1[:, :, :], t["f_w1"]).then_inc(f_in, 16)
                    sp.dma_start(f_ew[:, :, :], t["f_ew"]).then_inc(f_in, 16)
                if i == 4:
                    sp.dma_start(f_w2[:, :, :], t["f_w2"]).then_inc(f_in, 16)
                if i == 5:
                    for dst, name in ((d_w1[:, :, :], "d_w1"), (d_b1[:, :], "d_b1"), (gamma[:, :], "gamma")):
                        sp.dma_start(dst, t[name]).then_inc(d_in, 16)
                if i == 6:
                    sp.dma_start(d_w2[:, :, :], t["d_w2"]).then_inc(d_in, 16)
                    sp.dma_start(d_b2[:, :, :].rearrange("p l d -> p (l d)"), t["d_b2"].rearrange("l d -> (l d)").partition_broadcast(P)).then_inc(d_in, 16)
                    sp.dma_start(route[:, :], t["route"].partition_broadcast(P)).then_inc(d_in, 16)

            def bounce(n):
                u, s3 = n % 2, n % 3
                sp.wait_ge(parts_ready, n + 1)
                if n >= 2:
                    sp.wait_ge(stacked[(n - 2) % 3], 96 * ((n - 2) // 3 + 1))
                sp.dma_start(scratch[u].rearrange("a j d h n -> (d h) (a j) n"),
                             parts[:, u].rearrange("p a j n -> p (a j) n")).then_inc(scratch_in[u], 16)

            def load_stack(n):
                u, s3 = n % 2, n % 3
                sp.wait_ge(scratch_in[u], 16 * (n // 2 + 1))
                if n >= 3:
                    sp.wait_ge(s2_psum, H * (n - 2))
                for r, m, j in ((0, 3, 0), (3, 2, 1), (5, 1, 2)):
                    sp.dma_start(stack[DH * r:DH * (r + m), s3, 1], scratch[u][1, 0:m].rearrange("j d h n -> (j d) h n")
                                 ).then_inc(stacked[s3], 16)
                    sp.dma_start(stack[DH * r:DH * (r + m), s3, 0].rearrange("p h n -> p (h n)"),
                                 scratch[u][0, j:j + 1].rearrange("j d h n -> j d (h n)").broadcast_to([m, DH, H * S])
                                 ).then_inc(stacked[s3], 16)

            def place_max(n, hf):
                u, s3 = n % 2, n % 3
                sp.wait_ge(maxT_ready, 2 * n + hf + 1)
                sp.dma_start(stack[96:97, s3, 0, 8 * hf:8 * hf + 8, :],
                             maxrow[:, u, hf, :]).then_inc(max_in[s3][hf], 16)

            for lo in MANY:
                for i in range(lo - 3, lo + B):
                    if has(i + 2, lo):
                        load_stack(i + 2)
                    if has(i, lo):
                        place_max(i, 1)
                    if lo == 0:
                        load_for_later(i)
                    if has(i + 1, lo):
                        place_max(i + 1, 0)
                    if has(i + 3, lo):
                        bounce(i + 3)
            for c in range(4):
                sp.wait_ge(x_final, 4 * c + 4)
                two = slice(last_tiles(2 * c).start, last_tiles(2 * c + 1).stop)
                sp.dma_start(t["out"].rearrange("b (t p) d -> p (b t) d", p=P)[:, two, :], x_all[:, two, :]).then_inc(out_done[c], 16)
            for c in range(4):
                sp.wait_ge(out_done[c], 16)

        @block.gpsimd
        def _(pool):
            pool.memset(ident[:, :], 0.0).then_inc(pool_const, 1)
            pool.memset(minus_half[:, :], -0.5).then_inc(pool_const, 1)
            pool.wait_ge(pool_const, 2)
            pool.affine_select(out=ident[:, :], in_=ident[:, :], compare_op=ALU.not_equal, fill=1.0, base=0,
                               pattern=[[-1, P]], channel_multiplier=1).then_inc(pool_const, 1)
            pool.wait_ge(pool_const, 3)
            pool.tensor_copy(ident_bf[:, :], ident[:, :]).then_inc(pool_const, 1)

            pool.memset(causal[:, :], 0.0).then_inc(causal_step, 1)
            pool.wait_ge(causal_step, 1)
            pool.affine_select(out=causal[:, :], in_=causal[:, :], compare_op=ALU.is_ge, fill=-1e30, base=0,
                               pattern=[[-1, P]], channel_multiplier=1).then_inc(causal_step, 1)

            def rstd_step_(n):
                u = n % 2
                pool.wait_ge(mv_ready, NT * (n + 1))
                pool.tensor_scalar(rstd[:, u, :], mv[:, u, :, 1], EPS, None, ALU.add).then_inc(rstd_step, 1)
                pool.wait_ge(rstd_step, n + 1)
                pool.tensor_tensor(rstd[:, u, :], rstd[:, u, :], minus_half[:, 0:NT], ALU.pow).then_inc(rstd_ready, 1)

            def add_bias(m):
                n = item(m)
                l = n // B
                if m == 0:
                    pool.wait_ge(w_in, 48)
                pool.wait_ge(xn_ready, n + 1)
                x2 = x_all[:, tiles(n), :]
                pool.tensor_tensor(x2, x2, b_vo[:, l, 1:2, :].broadcast_to([P, NT, D]), ALU.add).then_inc(biased, 1)

            def v_ctx_bias(b):
                pool.wait_ge(kv_copied, 2 * b + 2)
                pool.tensor_tensor(v_ctx[:, b], v_ctx[:, b], b_vo[:, 1, 0:1, :].broadcast_to([P, NT, D]), ALU.add).then_inc(v_ctx_ready, 1)

            def z_norms(b):
                if b == 0:
                    pool.wait_ge(d_in, 96)
                pool.wait_ge(z_mv_ready, NT * (b + 1))
                rs, rn, var = z_rstd[:, b, :], rnorm[:, b, :], z_mv[:, b, :, 1]
                pool.tensor_scalar(rs, var, EPS, None, ALU.add).then_inc(rn_step, 1)
                pool.wait_ge(rn_step, 5 * b + 1)
                pool.tensor_tensor(rs, rs, minus_half[:, 0:NT], ALU.pow).then_inc(rn_step, 1)
                pool.wait_ge(rn_step, 5 * b + 2)
                pool.tensor_tensor(rn, var, rs, ALU.mult).then_inc(rn_step, 1)
                pool.wait_ge(rn_step, 5 * b + 3)
                pool.tensor_tensor(rn, rn, rs, ALU.mult).then_inc(rn_step, 1)
                pool.wait_ge(rn_step, 5 * b + 4)
                pool.tensor_scalar(rn, rn, float(D), 1e-24, ALU.mult, ALU.max).then_inc(rn_step, 1)
                pool.wait_ge(rn_step, 5 * b + 5)
                pool.tensor_tensor(rn, rn, minus_half[:, 0:NT], ALU.pow).then_inc(rn_ready, 1)
                pool.wait_ge(z_ready, b + 1)
                x2 = x_all[:, last_tiles(b), :]
                pool.tensor_tensor(x2, x2, d_b2[:, 1:2, :].broadcast_to([P, NT, D]), ALU.add).then_inc(light_bias, 1)

            def f_rstd_step():
                pool.wait_ge(f_mv_ready, FT)
                pool.tensor_scalar(f_rstd[:, :], f_mv[:, :, 1], EPS, None, ALU.add).then_inc(f_rstd_ready, 1)
                pool.wait_ge(f_rstd_ready, 1)
                pool.tensor_tensor(f_rstd[:, :], f_rstd[:, :], minus_half[:, :], ALU.pow).then_inc(f_rstd_ready, 1)

            for lo in MANY:
                if lo == B:
                    for n in range(B, 3 * B + AHEAD_C):
                        rstd_step_(n)
                        if n == B + 6:
                            f_rstd_step()
                for n in range(lo, lo + B):
                    if n < B or n >= B + AHEAD_C:
                        rstd_step_(item(n))
                    add_bias(n)
                    if lo == B and n >= lo + 5:
                        z_norms(n - lo - 5)
                    if n not in FIRST:
                        split(pool, n)
                    if lo == 0 and B // 2 > n - 3 >= 0:
                        v_ctx_bias(2 * (n - 3))
                        v_ctx_bias(2 * (n - 3) + 1)

            for b in range(3, B):
                z_norms(b)
            for b in range(B):
                pool.wait_ge(heavy_copied, b + 1)
                h2 = heavy[:, NT * b:NT * b + NT, :]
                pool.tensor_tensor(h2, h2, d_b2[:, 0:1, :].broadcast_to([P, NT, D]), ALU.add).then_inc(heavy_ready, 1)

        @block.scalar
        def _(act):
            def exps(n, h):
                c = H * n + h
                act.wait_ge(s2_psum, c + 1)
                if c >= 8:
                    act.wait_ge(pv_psum, c // G - 1)
                act.activation(probT[:, c % 8], s2_ps[c % 2][:, :, :], ACT.Exp, scale=DH ** -0.5).then_inc(exp_ready, 1)

            def xnT_copy(n):
                bank = pv_ps[0] if in_middle(n) else prep_ps
                act.wait_ge(xnT_psum, n + 1)
                if n >= 2:
                    if (n - 2) // B == 1:
                        act.wait_ge(qk_psum, n - 1)
                    else:
                        act.wait_ge(v_psum, v_count(n - 2))
                act.activation(xnT[:, n % 2, :], bank[:, 0, :], ACT.Copy).then_inc(xnT_ready, 1)

            def qk_copy(n):
                act.wait_ge(qk_psum, n + 1)
                if n >= 2:
                    if B <= n - 2 < 3 * B:
                        act.wait_ge(sc_psum, n - 2 - B + 1)
                    else:
                        act.wait_ge(parts_ready, many(n - 2) + 1)
                if n == 0:
                    act.wait_ge(w_in, 48)
                for a in range(1 if n // B == 1 else 2):
                    act.activation(qkf[:, n % 2, a, :], prep_ps[:, a, :], ACT.Identity,
                                   bias=b_qk[:, n // B, a:a + 1]).then_inc(qk_ready, 2 if n // B == 1 else 1)

            def kv_copy(b):
                act.wait_ge(kv_psum, b + 1)
                act.activation(k_ctx[:, S * b:S * b + S], s2_ps[b % 2][:, 0, :], ACT.Identity,
                               bias=b_qk[:, 1, 1:2]).then_inc(kv_copied, 1)
                act.activation(v_ctx[:, b].rearrange("p t d -> p (t d)"), s2_ps[b % 2][:, 1, :], ACT.Copy).then_inc(kv_copied, 1)

            def max_copy(n, hf):
                act.wait_ge(maxT_psum, 2 * n + hf + 1)
                if n >= 2:
                    act.wait_ge(max_in[(n - 2) % 3][hf], 16 * ((n - 2) // 3 + 1))
                act.activation(maxrow[:, n % 2, hf, :], prep_bf[0:8, 0, 0:S], ACT.Copy).then_inc(maxT_ready, 1)

            def u_copy(n, gb):
                act.wait_ge(pv_psum, NG * n + 2 * gb + 2)
                if n >= 2:
                    act.wait_ge(u_psum, 2 * (n - 1))
                act.activation(uT[:, n % 2, 2 * gb:2 * gb + 2, :], pv_ps[gb][:, :, :], ACT.Copy).then_inc(uT_ready, 1)

            def xrT_copy(b):
                act.wait_ge(xrT_psum, b + 1)
                act.activation(xrT[:, S * b:S * b + S], prep_ps[:, 0, :], ACT.Copy).then_inc(xrT_ready, 1)

            def hidden(q, f):
                c = NC * q + f
                act.wait_ge(d_h_psum, c + 1)
                if q >= 2:
                    act.wait_ge(d_y_psum, 4 * (q - 1))
                act.activation(d_hT[:, q % 2, f, :], up_bank(c), ACT.Gelu, bias=d_b1[:, f:f + 1]).then_inc(d_h_ready, 1)

            def oT_copy(n):
                act.wait_ge(oT_psum, n + 1)
                if n >= 2:
                    act.wait_ge(y_psum, n - 1)
                act.activation(oT[:, n % 2, :], out_ps[:, 0:S], ACT.Copy).then_inc(oT_ready, 1)

            def softmax_exps(n):
                r = n - B
                act.wait_ge(bias_ready, r + 1)
                if r >= 2:
                    act.wait_ge(probT_psum, r - 1)
                for k in range(NT):
                    w = P if n >= 2 * B and k == 0 else S
                    act.activation(prob[:, r % 2, k, 0:w], s1_ps[r % 2][:, k, 0:w], ACT.Exp, bias=negbias[:, r % 2, k:k + 1],
                                   scale=D ** -0.5, accum_out=den[:, r % 2, k:k + 1]).then_inc(prob_ready, 1)

            def probT_copy(n):
                r = n - B
                w = 3 * P if n >= 2 * B else 4 * P
                act.wait_ge(probT_psum, r + 1)
                if r >= 2:
                    act.wait_ge(o1_psum, r - 1)
                act.activation(probT1[:, r % 2, 0:w], s2_ps[r % 2][:, :, :].rearrange("p t q -> p (t q)")[:, 0:w],
                               ACT.Copy).then_inc(probT_ready, 1)

            def f_xnT_copy():
                act.wait_ge(f_xnT_psum, 1)
                act.activation(f_xnT[:, :], prep_ps[:, :, :].rearrange("p t q -> p (t q)"), ACT.Copy).then_inc(f_xnT_ready, 1)

            def expert_gelus(first, end):
                for f in range(first, end):
                    act.wait_ge(f_h_psum, f + 1)
                    act.activation(f_hT[:, f, :], s2_ps[f % 2][:, :, :].rearrange("p t q -> p (t q)"),
                                   ACT.Gelu_apprx_tanh).then_inc(f_h_ready, 1)

            for lo in MANY:
                if lo == B:
                    for i in range(B, 3 * B + 1):
                        expert = i == FFN_STEP
                        if expert:
                            probT_copy(i - 1)
                            softmax_exps(i)
                            f_xnT_copy()
                            expert_gelus(0, 4)
                            for n in ahead(i, 1):
                                qk_copy(n)
                            expert_gelus(4, 6)
                            for n in ahead(i, 2):
                                xnT_copy(n)
                            expert_gelus(6, NF)
                        else:
                            if B <= i - 1 < 3 * B:
                                probT_copy(i - 1)
                            if i == B:
                                u_copy(B - 1, 1)
                            for n in ahead(i, 1):
                                qk_copy(n)
                            if i < 3 * B:
                                softmax_exps(i)
                            for n in ahead(i, 2):
                                xnT_copy(n)
                            if i == B:
                                oT_copy(B - 1)
                ups = 0
                kv_done = 0 if lo == 0 else B
                for i in steps_of(lo):
                    x = prepared(i, lo)
                    for h in range(H):
                        if has(i, lo):
                            exps(i, h)
                        if i == 2 * B and h in UP_AT:
                            if ups == 0:
                                act.wait_ge(d_in, 96)
                                act.wait_ge(s2_psum, 2 * H * B)
                            hidden(0, ups)
                            ups += 1
                        if h == 3 and has(i, lo):
                            max_copy(i, 1)
                        if h == 1 and has(i - 1, lo):
                            u_copy(i - 1, 1)
                        if h == 3 and x is not None:
                            xnT_copy(x)
                        if h in KV_AT.get(i, ()):
                            kv_copy(kv_done)
                            kv_done += 1
                        if h == 7 and x is not None:
                            qk_copy(x)
                        if h == 13 and has(i, lo):
                            u_copy(i, 0)
                        if h == 11 and has(i + 1, lo):
                            max_copy(i + 1, 0)
                        if h == 11 and has(i - 1, lo):
                            oT_copy(i - 1)
                        if h == 0 and lo == B and has(i - 3, lo):
                            xrT_copy(i - 3 - B)

            def shift_exp(j):
                act.wait_ge(shifted_ready, j + 1)
                act.activation(e_row[:, :], shifted[:, :], ACT.Exp).then_inc(e_ready, 1)

            def branch_copies(q):
                for b in (2 * q, 2 * q + 1):
                    act.wait_ge(d_y_psum, 2 * b + 1)
                    act.activation(heavy[:, NT * b:NT * b + NT, :], heavy_bank(b), ACT.Copy).then_inc(heavy_copied, 1)
                    act.wait_ge(d_y_psum, 2 * b + 2)
                    act.activation(x_all[:, last_tiles(b), :], light_bank(b), ACT.Copy).then_inc(light_done, 1)

            for q in range(4):
                for f in range(NC):
                    if (q, f) == SHIFT_AT:
                        shift_exp(1)
                    if q >= 1:
                        hidden(q, f)
                if q == 0:
                    xrT_copy(B - 1)
                    shift_exp(0)
                if q >= 1:
                    branch_copies(q - 1)
            branch_copies(3)

        @block.vector
        def _(dve):
            dve.memset(fill[0:96, :], 0.0).then_inc(fill_ready, 1)
            dve.memset(fill[96:97, :], 1.0).then_inc(fill_ready, 1)

            def prepare_v_aug(slots, count):
                dve.memset(v_aug[:, slots].rearrange("p s t h d -> p (s t h d)"), 0.0).then_inc(v_aug_ready, 1)
                dve.wait_ge(v_aug_ready, count + 1)
                dve.memset(v_aug[:, slots, :, :, DH:DH + 1].rearrange("p s t h d -> p (s t h) d"), 1.0).then_inc(v_aug_ready, 1)

            prepare_v_aug(slice(0, 2), 0)

            def ln_stats(n):
                u, l = n % 2, n // B
                if l == 0 and n % 2 == 0:
                    dve.wait_ge(x_in[n // 2], 16)
                if l == 1:
                    dve.wait_ge(x_ready, n - B + 1)
                if l == 2:
                    dve.wait_ge(x_mid, batch(n) + 1)
                    if batch(n) < FT // NT:
                        dve.wait_ge(f_x, FT)
                if l == 3:
                    dve.wait_ge(x_mid, n - 2 * B + 1)
                for k in range(NT):
                    dve.bn_stats(stats[:, u, k, :], x_all[:, tiles(n).start + k, :]).then_inc(stats_ready, 1)
                for k in range(NT):
                    dve.wait_ge(stats_ready, NT * n + k + 1)
                    dve.bn_aggr(mv[:, u, k, :], stats[:, u, k, :]).then_inc(mv_ready, 1)

            def ln_apply(n):
                u = n % 2
                dve.wait_ge(rstd_ready, n + 1)
                if n >= 2:
                    dve.wait_ge(xnT_psum, n - 1)
                for k in range(NT):
                    i = dve.tensor_scalar(xn[:, u, k, :], x_all[:, tiles(n).start + k, :], mv[:, u, k, 0:1], rstd[:, u, k:k + 1],
                                          ALU.subtract, ALU.mult)
                    if k == NT - 1:
                        i.then_inc(xn_ready, 1)

            def part1(m):
                u = m % 2
                dve.wait_ge(qk_ready, 2 * item(m) + 2)
                if m >= 2:
                    dve.wait_ge(scratch_in[u], 16 * (m // 2))
                dve.tensor_copy(parts[:, u, :, 0, :], qkf[:, u]).then_inc(part1_ready, 1)
                if m in FIRST:
                    split(dve, m)

            def v_copy(m):
                n = item(m)
                dve.wait_ge(v_psum, v_count(n))
                if m == 0:
                    dve.wait_ge(w_in, 48)
                if m in (0, 2):
                    dve.wait_ge(v_aug_ready, m + 2)
                if m >= 4:
                    dve.wait_ge(pv_psum, NG * (m - 3))
                bank = pv_ps[1] if in_middle(n) else prep_ps
                for k in range(NT):
                    i = dve.tensor_tensor(v_aug[:, m % 4, k, :, 0:DH], bank[:, 0, k * D:(k + 1) * D].rearrange("p (h d) -> p h d", d=DH),
                                          b_vo[:, n // B, 0, :].rearrange("p (h d) -> p h d", d=DH), ALU.add)
                    if k == NT - 1:
                        i.then_inc(v_ready, 1)

            def row_max(n, h):
                c = H * n + h
                dve.wait_ge(s1_psum, c + 1)
                if h == 0 and n >= 2:
                    dve.wait_ge(maxT_psum, 2 * (n - 1))
                dve.tensor_reduce(negmax[:, n % 2, :, h], s1_ps[c % 2][:, :, :], axis=AX.X, op=ALU.max,
                                  negate=True).then_inc(max_ready, 1)

            def normalise(n, k):
                u = n % 2
                dve.wait_ge(u_psum, 2 * n + k + 1)
                if n >= 2 and k == 0:
                    dve.wait_ge(oT_psum, n - 1)
                u4 = out_ps[:, :].rearrange("p (h d) -> p h d", d=32)
                dve.reciprocal(den_inv[:, k, :], u4[:, :, DH]).then_inc(inv_ready, 1)
                dve.wait_ge(inv_ready, 2 * n + k + 1)
                dve.tensor_tensor(o_tok[:, u, k, :].rearrange("p (h d) -> p h d", d=DH), u4[:, :, 0:DH],
                                  den_inv[:, k, :].unsqueeze(2).broadcast_to([P, H, DH]), ALU.mult).then_inc(o_ready, 1)

            def residual(n):
                dve.wait_ge(y_psum, n + 1)
                dve.wait_ge(biased, n + 1)
                x2 = x_all[:, tiles(item(n)), :]
                dve.tensor_tensor(x2, out_ps[:, 0:S].rearrange("p (t d) -> p t d", d=D), x2, ALU.add).then_inc(x_ready, 1)

            def v_copy_one(n):
                r = n - B
                dve.wait_ge(v_psum, v_count(n))
                if r >= 2:
                    dve.wait_ge(o1_psum, r - 1)
                bank = pv_ps[1] if in_middle(n) else prep_ps
                dve.tensor_tensor(v_one[:, r % 2], bank[:, 0, :].rearrange("p (t d) -> p t d", d=D),
                                  b_vo[:, n // B, 0:1, :].broadcast_to([P, NT, D]), ALU.add).then_inc(v_ready, 1)

            def softmax_bias(n):
                r = n - B
                sc = s1_ps[r % 2]
                dve.wait_ge(sc_psum, r + 1)
                if n >= 2 * B:
                    for k in range(NT):
                        dve.tensor_tensor(sc[:, k, k * P:(k + 1) * P], sc[:, k, k * P:(k + 1) * P], causal[:, :],
                                          ALU.add).then_inc(mask_step, 1)
                    dve.wait_ge(mask_step, NT * (n - 2 * B + 1))
                    dve.tensor_reduce(negbias_raw[:, r % 2, 0:1], sc[:, 0, 0:P], axis=AX.X, op=ALU.max,
                                      negate=True).then_inc(negmax1_ready, 1)
                    dve.tensor_reduce(negbias_raw[:, r % 2, 1:2], sc[:, 1, :], axis=AX.X, op=ALU.max,
                                      negate=True).then_inc(negmax1_ready, 1)
                else:
                    dve.tensor_reduce(negbias_raw[:, r % 2, :], sc[:, :, :], axis=AX.X, op=ALU.max,
                                      negate=True).then_inc(negmax1_ready, 2)
                dve.wait_ge(negmax1_ready, 2 * (r + 1))
                if r >= 2:
                    dve.wait_ge(prob_ready, NT * (r - 1))
                dve.tensor_scalar(negbias[:, r % 2, :], negbias_raw[:, r % 2, :], D ** -0.5, None,
                                  ALU.mult).then_inc(bias_ready, 1)

            def residual_one(n):
                r, first = n - B, tiles(n).start
                dve.wait_ge(prob_ready, NT * (r + 1))
                dve.reciprocal(den_inv1[:, r % 2, :], den[:, r % 2, :]).then_inc(inv1_ready, 1)
                dve.wait_ge(inv1_ready, r + 1)
                dve.wait_ge(o1_psum, r + 1)
                for k in range(NT):
                    i = dve.scalar_tensor_tensor(out=x_all[:, first + k, :], in0=out_ps[:, k * D:(k + 1) * D],
                                                 scalar=den_inv1[:, r % 2, k:k + 1], in1=x_all[:, first + k, :],
                                                 op0=ALU.mult, op1=ALU.add)
                i.then_inc(x_mid, 1)

            def f_norm_stats():
                dve.wait_ge(x_mid, FT // NT)
                for k in range(FT):
                    dve.bn_stats(f_stats[:, k, :], x_all[:, k, :]).then_inc(f_stats_ready, 1)
                dve.wait_ge(f_stats_ready, FT)
                for k in range(FT):
                    dve.bn_aggr(f_mv[:, k, :], f_stats[:, k, :]).then_inc(f_mv_ready, 1)

            def f_apply():
                dve.wait_ge(f_rstd_ready, 2)
                for k in range(FT):
                    dve.tensor_scalar(f_xn[:, k, :], x_all[:, k, :], f_mv[:, k, 0:1], f_rstd[:, k:k + 1],
                                      ALU.subtract, ALU.mult).then_inc(f_xn_ready, 1)
                dve.wait_ge(f_in, 48)
                dve.tensor_tensor(f_wsum[:, :], f_ew[:, :, 0], f_ew[:, :, 1], ALU.add).then_inc(f_wsum_ready, 1)

            def f_residual(k):
                if k == 0:
                    dve.wait_ge(f_wsum_ready, 1)
                dve.wait_ge(f_y_psum, k + 1)
                dve.scalar_tensor_tensor(out=x_all[:, k, :], in0=out_ps[:, S:S + D], scalar=f_wsum[:, k:k + 1],
                                         in1=x_all[:, k, :], op0=ALU.mult, op1=ALU.add).then_inc(f_x, 1)

            def z_norm_stats(b):
                dve.wait_ge(x_ready, B + b + 1)
                for k in range(NT):
                    dve.bn_stats(z_stats[:, b % 2, k, :], x_all[:, last_tiles(b).start + k, :]).then_inc(z_stats_ready, 1)
                for k in range(NT):
                    dve.wait_ge(z_stats_ready, NT * b + k + 1)
                    dve.bn_aggr(z_mv[:, b, k, :], z_stats[:, b % 2, k, :]).then_inc(z_mv_ready, 1)

            def z_apply(b):
                dve.wait_ge(rn_step, 5 * b + 2)
                for k in range(NT):
                    i = dve.tensor_scalar(z[:, b % 2, k, :], x_all[:, last_tiles(b).start + k, :], z_mv[:, b, k, 0:1], z_rstd[:, b, k:k + 1],
                                          ALU.subtract, ALU.mult)
                i.then_inc(z_ready, 1)

            def z_route(b):
                if b == 0:
                    dve.wait_ge(d_in, 96)
                dve.wait_ge(z_ready, b + 1)
                for k in range(NT):
                    c = NT * b + k
                    if c >= 1:
                        dve.wait_ge(s_tok_ready, c)
                    dve.scalar_tensor_tensor(out=s_junk[:, :], in0=z[:, b % 2, k, :], scalar=1.0, in1=route[:, :], op0=ALU.mult,
                                             op1=ALU.mult, accum_out=s_tok[:, b, k:k + 1]).then_inc(s_tok_ready, 1)
                dve.wait_ge(rn_ready, b + 1)
                if b >= 2:
                    dve.wait_ge(xrT_psum, b - 1)
                for k in range(NT):
                    i = dve.tensor_scalar(xr[:, b % 2, k, :], z[:, b % 2, k, :], rnorm[:, b, k:k + 1], None, ALU.mult)
                i.then_inc(xr_ready, 1)

            def fold_gamma():
                dve.wait_ge(d_in, 96)
                dve.tensor_scalar(d_w1[:, 0:NC - 1, :], d_w1[:, 0:NC - 1, :], gamma[:, 0:1], D ** 0.5, ALU.mult, ALU.mult).then_inc(d_folded, 1)
                dve.tensor_scalar(d_w1[:, NC - 1, :], d_w1[:, NC - 1, :], gamma[:, 1:2], D ** 0.5, ALU.mult, ALU.mult).then_inc(d_folded, 1)
                dve.memset(ones[:, :], 1.0).then_inc(s_row_ready, 1)
                dve.memset(k_inv[:, :], 1.0 / KEFF).then_inc(s_row_ready, 1)
                dve.memset(level[:, 0:1], S / KEFF * float(np.exp(LEVEL0))).then_inc(chain, 1)

            for lo in MANY:
                if lo == B:
                    fold_gamma()
                    for i in range(B, 3 * B + 1):
                        if i == B:
                            normalise(B - 1, 0)
                        if B <= i < 3 * B:
                            softmax_bias(i)
                        if i == B:
                            normalise(B - 1, 1)
                        for n in ahead(i, 3):
                            ln_stats(n)
                        if B <= i - 1 < 3 * B:
                            residual_one(i - 1)
                        if 0 < i - FFN_STEP <= FT:
                            f_residual(i - FFN_STEP - 1)
                        for n in ahead(i, 1):
                            if 2 * B <= n < 3 * B:
                                v_copy_one(n)
                            elif n >= 3 * B:
                                part1(many(n))
                                v_copy(many(n))
                        for n in ahead(i, 3):
                            ln_apply(n)
                        if i == B:
                            residual(B - 1)
                        if i == B + 3:
                            f_norm_stats()
                        if i == B + 4:
                            f_apply()
                for i in steps_of(lo):
                    x = prepared(i, lo)
                    for h in range(H):
                        ln = x if lo else i + 3
                        if h == at(lo, 0, 1) and ln is not None:
                            ln_stats(ln)
                        if has(i + 1, lo):
                            row_max(i + 1, h)
                        if h == 2 and ln is not None:
                            ln_apply(ln)
                        if h == 3 and i == -3:
                            prepare_v_aug(slice(2, 4), 2)
                        if h == 4 and has(i - 1, lo):
                            normalise(i - 1, 0)
                        if h == 7 and has(i - 1, lo):
                            normalise(i - 1, 1)
                        if h == at(lo, 9, 8) and x is not None and has(i + 3, lo):
                            part1(i + 3)
                        if h == 14 and x is not None:
                            if has(i + 3, lo):
                                v_copy(i + 3)
                        if h == 15 and has(i - 1, lo):
                            residual(i - 1)
                        if lo == B and has(i - 2, lo):
                            if h == 3:
                                z_norm_stats(i - 2 - B)
                            if h == 7:
                                z_apply(i - 2 - B)
                            if h == 13:
                                z_route(i - 2 - B)

            dve.wait_ge(s_row_psum, 1)
            dve.tensor_copy(s_row[:, :], pv_ps[0][0:B, 0, :]).then_inc(s_row_ready, 1)
            dve.wait_ge(s_row_ready, 3)
            dve.tensor_reduce(shift[:, :], s_row[:, :], axis=AX.X, op=ALU.max).then_inc(s_row_ready, 1)
            dve.wait_ge(s_row_ready, 4)
            dve.tensor_scalar(shift[:, :], shift[:, :], 0.0, -LEVEL0, ALU.min, ALU.add).then_inc(s_row_ready, 1)
            dve.wait_ge(s_row_ready, 5)

            def reshift():
                dve.tensor_scalar(shifted[:, :], s_row[:, :], shift[:, 0:1], TOP, ALU.subtract, ALU.min).then_inc(shifted_ready, 1)

            def top_half(m):
                r = m // 2
                src = s_row[:, :] if r == 0 else work[(r - 1) % 2][:, :]
                if m >= 1:
                    dve.wait_ge(top_step, m)
                if m % 2 == 0:
                    dve.max(out=top8[:, :], in_=src).then_inc(top_step, 1)
                else:
                    dve.match_replace(out=work[r % 2][:, :], in_to_replace=top8[:, :], in_values=src,
                                      imm_value=NEVER).then_inc(top_step, 1)

            reshift()
            steps, halves = 0, 0
            for j, count in enumerate(BLOCKS):
                for _ in range(TOP_HALVES_AHEAD[j]):
                    top_half(halves)
                    halves += 1
                dve.wait_ge(e_ready, j + 1)
                for k in range(count):
                    a = steps % 2
                    dve.wait_ge(chain, steps + 2 * j + 1)
                    dve.scalar_tensor_tensor(out=min_junk[:, :], in0=e_row[:, :], scalar=level[:, a:a + 1], in1=k_inv[:, :],
                                             op0=ALU.min, op1=ALU.mult, accum_out=level[:, 1 - a:2 - a]).then_inc(chain, 1)
                    steps += 1
                    if halves < 2 * (TOPK // 8) - sum(TOP_HALVES_AHEAD[j + 1:]):
                        top_half(halves)
                        halves += 1
                a = steps % 2
                if j == len(BLOCKS) - 1:
                    break
                bits = level[:, a:a + 1].bitcast(int32)
                dve.wait_ge(chain, steps + 2 * j + 1)
                dve.tensor_scalar(exponent[:, :], bits, 23, None, ALU.logical_shift_right).then_inc(shift_step, 1)
                dve.tensor_scalar(bits, bits, 0x7FFFFF, 0x3F800000, ALU.bitwise_and, ALU.bitwise_or).then_inc(chain, 1)
                dve.wait_ge(shift_step, 3 * j + 1)
                dve.tensor_scalar(expo_f[:, :], exponent[:, :], LN2, -127 * LN2 - LEVEL0, ALU.mult, ALU.add).then_inc(shift_step, 1)
                dve.wait_ge(shift_step, 3 * j + 2)
                dve.tensor_tensor(shift[:, :], shift[:, :], expo_f[:, :], ALU.add).then_inc(shift_step, 1)
                dve.wait_ge(shift_step, 3 * j + 3)
                reshift()
                dve.wait_ge(chain, steps + 2 * j + 2)
                dve.tensor_scalar(level[:, a:a + 1], level[:, a:a + 1], float(np.exp(LEVEL0)), None, ALU.mult).then_inc(chain, 1)
            dve.wait_ge(top_step, 2 * (TOPK // 8))
            dve.tensor_scalar(highest[:, :], work[(TOPK // 8 - 1) % 2][:, :], NEVER, None, ALU.is_equal).then_inc(pick_step, 1)
            assert halves == 2 * (TOPK // 8)
            dve.wait_ge(chain, steps + 2 * (len(BLOCKS) - 1) + 1)
            last_level = level[:, steps % 2:steps % 2 + 1]
            dve.scalar_tensor_tensor(out=at_one[:, :], in0=e_row[:, :], scalar=last_level, in1=ones[:, :], op0=ALU.is_ge,
                                     op1=ALU.mult, accum_out=n_at_one[:, :]).then_inc(pick_step, 1)
            dve.reciprocal(inv_level[:, :], last_level).then_inc(score_step, 1)
            dve.wait_ge(pick_step, 2)
            dve.tensor_tensor_scan(out=place[:, :], data0=ones[:, :], data1=at_one[:, :], initial=0.0, op0=ALU.mult,
                                   op1=ALU.add).then_inc(pick_step, 1)
            dve.tensor_scalar(n_at_one[:, :], n_at_one[:, :], float(TOPK), None, ALU.is_le).then_inc(pick_step, 1)
            dve.wait_ge(score_step, 1)
            dve.tensor_scalar(score[:, :], e_row[:, :], inv_level[:, :], 1.0, ALU.mult, ALU.min).then_inc(score_step, 1)
            dve.wait_ge(pick_step, 4)
            dve.scalar_tensor_tensor(out=at_one[:, :], in0=place[:, :], scalar=float(TOPK), in1=at_one[:, :], op0=ALU.is_le,
                                     op1=ALU.mult).then_inc(pick_step, 1)
            dve.wait_ge(score_step, 2)
            dve.tensor_scalar(weight[:, :], score[:, :], -1.0, 1.0, ALU.mult, ALU.add).then_inc(score_step, 1)
            dve.wait_ge(pick_step, 5)
            dve.scalar_tensor_tensor(out=at_one[:, :], in0=highest[:, :], scalar=n_at_one[:, :], in1=at_one[:, :], op0=ALU.mult,
                                     op1=ALU.max).then_inc(pick_step, 1)
            dve.wait_ge(score_step, 3)
            dve.tensor_tensor(weight[:, :], weight[:, :], score[:, :], ALU.add).then_inc(score_step, 1)
            dve.wait_ge(pick_step, 6)
            dve.wait_ge(score_step, 4)
            dve.tensor_tensor(weight[:, :], at_one[:, :], weight[:, :], ALU.mult).then_inc(weight_ready, 1)
            dve.wait_ge(w_psum, 1)
            dve.tensor_copy(w_tok[:, :, :].rearrange("p t b -> p (t b)"), pv_ps[1][:, 0, 0:NT * B]).then_inc(w_ready, 1)
            dve.wait_ge(w_ready, 1)
            for b in range(B):
                for k in range(NT):
                    c = NT * b + k
                    if k == 0:
                        dve.wait_ge(heavy_ready, b + 1)
                        dve.wait_ge(light_done, b + 1)
                    x1 = x_all[:, last_tiles(b).start + k, :]
                    dve.scalar_tensor_tensor(out=x1, in0=heavy[:, c, :], scalar=w_tok[:, k, b:b + 1], in1=x1,
                                             op0=ALU.mult, op1=ALU.add).then_inc(x_final, 1)

        @block.tensor
        def _(pe):
            pe.wait_ge(pool_const, 4)

            def xn_transpose(n):
                u = n % 2
                bank = pv_ps[0] if in_middle(n) else prep_ps
                pe.wait_ge(xn_ready, n + 1)
                for k in range(NT):
                    i = pe.transpose(bank[:, 0, k * P:(k + 1) * P], xn[:, u, k, :], ident[:, :])
                i.then_inc(xnT_psum, 1)

            def qk_project(n):
                u, l = n % 2, n // B
                pe.wait_ge(xnT_ready, n + 1)
                if n == 0:
                    pe.wait_ge(w_in, 48)
                i = pe.matmul(prep_ps[:, 0, :], w_att[:, l, 0, :], xnT[:, u, :], start=True, stop=True)
                if l == 1:
                    i.then_inc(qk_psum, 1)
                    return
                pe.matmul(prep_ps[:, 1, :], w_att[:, l, 1, :], xnT[:, u, :] if l in SELF else ctxT[:, S * batch(n):S * batch(n) + S],
                          start=True, stop=True).then_inc(qk_psum, 1)

            def kv_project(b):
                if b == 0:
                    pe.wait_ge(w_cross_in, 16)
                if b % (B // 2) == 0:
                    pe.wait_ge(ctx_in[b // (B // 2)], 16)
                if b >= 2:
                    pe.wait_ge(kv_copied, 2 * (b - 1))
                first = S * b
                pe.matmul(s2_ps[b % 2][:, 0, :], w_att[:, 1, 1, :], ctxT[:, first:first + S], start=True, stop=True)
                for k in range(NT):
                    i = pe.matmul(s2_ps[b % 2][:, 1, k * D:(k + 1) * D], ctxT[:, first + k * P:first + (k + 1) * P], w_att[:, 1, 2, :],
                                  start=True, stop=True)
                i.then_inc(kv_psum, 1)

            def v_project(n):
                u, l = n % 2, n // B
                bank = pv_ps[1] if in_middle(n) else prep_ps
                for k in range(NT):
                    src = xnT[:, u, k * P:(k + 1) * P] if l in SELF else ctxT[:, S * batch(n) + k * P:S * batch(n) + (k + 1) * P]
                    i = pe.matmul(bank[:, 0, k * D:(k + 1) * D], src, w_att[:, l, 2, :], start=True, stop=True)
                i.then_inc(v_psum, 1)

            def scores_for_max(n, h):
                c, s3 = H * n + h, n % 3
                if h == 0:
                    pe.wait_ge(stacked[s3], 96 * (n // 3 + 1))
                    if n < 3:
                        pe.wait_ge(filled[s3], 32)
                if c >= 2:
                    pe.wait_ge(max_ready, c - 1)
                for k in range(NT):
                    i = pe.matmul(s1_ps[c % 2][:, k, :], stack[0:96, s3, 0, h, k * P:(k + 1) * P], stack[0:96, s3, 1, h, :],
                                  start=True, stop=True)
                i.then_inc(s1_psum, 1)

            def max_transpose(n, hf):
                pe.wait_ge(max_ready, H * n + 8 * hf + 8)
                for k in range(NT):
                    i = pe.transpose(prep_bf[0:8, 0, k * P:(k + 1) * P], negmax[:, n % 2, k, 8 * hf:8 * hf + 8], ident_bf[:, :])
                i.then_inc(maxT_psum, 1)

            def scores(n, h):
                c, s3 = H * n + h, n % 3
                if h % 8 == 0:
                    pe.wait_ge(max_in[s3][h // 8], 16 * (n // 3 + 1))
                if c >= 2:
                    pe.wait_ge(exp_ready, c - 1)
                for k in range(NT):
                    i = pe.matmul(s2_ps[c % 2][:, k, :], stack[0:97, s3, 1, h, k * P:(k + 1) * P], stack[0:97, s3, 0, h, :],
                                  start=True, stop=True)
                i.then_inc(s2_psum, 1)

            def weighted_sum(n, g):
                pe.wait_ge(exp_ready, H * n + G * (g + 1))
                if g == 0:
                    pe.wait_ge(v_ready, v_count(item(n)))
                if g % 2 == 0 and n >= 1:
                    pe.wait_ge(uT_ready, 2 * (n - 1) + g // 2 + 1)
                for k in range(NT):
                    for j in range(G):
                        i = pe.matmul(pv_ps[g // 2][32 * j:32 * j + 32, g % 2, :], v_aug[:, n % 4, k, G * g + j, :],
                                      probT[:, (G * g + j) % 8, k, :], start=(k == 0), stop=(k == NT - 1))
                i.then_inc(pv_psum, 1)

            def u_transpose(n, k):
                if k == 0:
                    pe.wait_ge(uT_ready, 2 * n + 2)
                    if n >= 1:
                        pe.wait_ge(x_ready, n)
                else:
                    pe.wait_ge(o_ready, 2 * n + 1)
                for g in range(NG):
                    i = pe.transpose(out_ps[:, g * P:(g + 1) * P], uT[:, n % 2, g, k * P:(k + 1) * P], ident[:, :])
                i.then_inc(u_psum, 1)

            def o_transpose(n):
                pe.wait_ge(o_ready, 2 * n + 2)
                for k in range(NT):
                    i = pe.transpose(out_ps[:, k * P:(k + 1) * P], o_tok[:, n % 2, k, :], ident[:, :])
                i.then_inc(oT_psum, 1)

            def xr_transpose(b):
                pe.wait_ge(xr_ready, b + 1)
                for k in range(NT):
                    i = pe.transpose(prep_ps[:, 0, k * P:(k + 1) * P], xr[:, b % 2, k, :], ident[:, :])
                i.then_inc(xrT_psum, 1)

            def out_project(n):
                pe.wait_ge(oT_ready, n + 1)
                for k in range(NT):
                    i = pe.matmul(out_ps[:, k * D:(k + 1) * D], oT[:, n % 2, k * P:(k + 1) * P], w_att[:, item(n) // B, 3, :],
                                  start=True, stop=True)
                i.then_inc(y_psum, 1)

            def up(q, chunks=range(NC)):
                for f in chunks:
                    c = NC * q + f
                    if c >= 2:
                        pe.wait_ge(d_h_ready, c - 1)
                    pe.matmul(up_bank(c), d_w1[:, f, :], xrT[:, 2 * S * q:2 * S * (q + 1)],
                              start=True, stop=True).then_inc(d_h_psum, 1)

            def scores_one(n):
                r, u = n - B, n % 2
                pe.wait_ge(qk_ready, 2 * n + 2)
                if r >= 2:
                    pe.wait_ge(prob_ready, NT * (r - 1))
                for k in range(NT):
                    w = P if n >= 2 * B and k == 0 else S
                    keys = k_ctx[:, S * batch(n):S * batch(n) + S] if n < 2 * B else qkf[:, u, 1, 0:w]
                    i = pe.matmul(s1_ps[r % 2][:, k, 0:w], qkf[:, u, 0, k * P:(k + 1) * P], keys, start=True, stop=True)
                i.then_inc(sc_psum, 1)

            def prob_tiles(n):
                tiles = [(0, 0), (1, 0), (1, 1)] if n >= 2 * B else [(0, 0), (1, 0), (1, 1), (0, 1)]
                return [(q, k, c * P) for c, (q, k) in enumerate(tiles)]

            def prob_transpose(n):
                r = n - B
                pe.wait_ge(prob_ready, NT * (r + 1))
                if r >= 2:
                    pe.wait_ge(probT_ready, r - 1)
                bank = s2_ps[r % 2][:, :, :].rearrange("p t q -> p (t q)")
                for q, k, c in prob_tiles(n):
                    i = pe.transpose(bank[:, c:c + P], prob[:, r % 2, q, k * P:(k + 1) * P], ident[:, :])
                i.then_inc(probT_psum, 1)

            def weighted_sum_one(n):
                r = n - B
                pe.wait_ge(probT_ready, r + 1)
                if n < 2 * B:
                    pe.wait_ge(v_ctx_ready, r + 1)
                else:
                    pe.wait_ge(v_ready, v_count(n))
                if r >= 1:
                    pe.wait_ge(x_mid, r)
                if FFN_STEP < n <= FFN_STEP + FT:
                    pe.wait_ge(f_x, n - FFN_STEP)
                for q in range(NT):
                    tiles = sorted((k, c) for q2, k, c in prob_tiles(n) if q2 == q)
                    for k, c in tiles:
                        i = pe.matmul(out_ps[:, q * D:(q + 1) * D], probT1[:, r % 2, c:c + P], v_ctx[:, batch(n), k, :] if n < 2 * B else v_one[:, r % 2, k, :],
                                      start=(k == 0), stop=(k == tiles[-1][0]))
                i.then_inc(o1_psum, 1)

            def expert_transpose():
                pe.wait_ge(f_xn_ready, FT)
                pe.wait_ge(qk_ready, 2 * (FFN_STEP + 1))
                for k in range(FT):
                    i = pe.transpose(prep_ps[:, k // 2, (k % 2) * P:(k % 2 + 1) * P], f_xn[:, k, :], ident[:, :])
                i.then_inc(f_xnT_psum, 1)
                pe.wait_ge(f_xnT_ready, 1)
                pe.wait_ge(f_in, 48)
                pe.wait_ge(probT_ready, FFN_STEP - B)

            def expert_up(f):
                if f >= 2:
                    pe.wait_ge(f_h_ready, f - 1)
                pe.matmul(s2_ps[f % 2][:, :, :].rearrange("p t q -> p (t q)"), f_w1[:, f, :], f_xnT[:, :],
                          start=True, stop=True).then_inc(f_h_psum, 1)

            def expert_down(k, n):
                pe.wait_ge(x_mid, n - B)
                if k >= 1:
                    pe.wait_ge(f_x, k)
                for f in range(NF):
                    i = pe.matmul(out_ps[:, S:S + D], f_hT[:, f, k * P:(k + 1) * P], f_w2[:, f, :],
                                  start=(f == 0), stop=(f == NF - 1))
                i.then_inc(f_y_psum, 1)

            for lo in MANY:
                if lo == B:
                    for i in range(B, 3 * B + 1):
                        if i == B:
                            weighted_sum(B - 1, 3)
                            pe.wait_ge(max_ready, H * B)
                        expert = i == FFN_STEP
                        if i == B + 1:
                            pe.wait_ge(uT_ready, 2 * B)
                            pe.wait_ge(x_ready, B)
                        if B <= i < 3 * B:
                            scores_one(i)
                        if expert:
                            expert_transpose()
                            expert_up(0)
                            expert_up(1)
                        if i == B:
                            u_transpose(B - 1, 0)
                        if expert:
                            expert_up(2)
                            expert_up(3)
                        for n in ahead(i, 1):
                            pe.wait_ge(qk_ready, 2 * n)
                            qk_project(n)
                        if expert:
                            expert_up(4)
                            expert_up(5)
                        for n in ahead(i, 2):
                            pe.wait_ge(xnT_ready, n)
                            if i == B:
                                pe.wait_ge(uT_ready, 2 * B - 1)
                            xn_transpose(n)
                        if i == B:
                            u_transpose(B - 1, 1)
                            pe.wait_ge(exp_ready, H * B)
                        if expert:
                            expert_up(6)
                            expert_up(7)
                        if 0 < i - FFN_STEP <= FT:
                            expert_down(i - FFN_STEP - 1, i - 1)
                        if B <= i - 1 < 3 * B:
                            weighted_sum_one(i - 1)
                        for n in ahead(i, 1):
                            if n >= 2 * B:
                                pe.wait_ge(v_ready, v_count(n - 1))
                                v_project(n)
                        if expert:
                            pe.wait_ge(f_h_ready, NF)
                        if B <= i < 3 * B:
                            prob_transpose(i)
                        if i == B:
                            o_transpose(B - 1)
                            out_project(B - 1)
                    pe.wait_ge(prob_ready, NT * 2 * B)
                ups = 0
                prep_free = (qk_ready, 2 * (3 * B + AHEAD_C)) if lo else None
                kv_done = 0 if lo == 0 else B
                for i in steps_of(lo):
                    x = prepared(i, lo)
                    if i == B:
                        pe.wait_ge(probT_ready, 2 * B)
                        pe.wait_ge(xnT_ready, 3 * B + AHEAD_C)
                        pe.wait_ge(v_ready, v_count(3 * B + AHEAD_C - 1))
                        pe.wait_ge(x_mid, 2 * B)
                    if x == B:
                        pe.wait_ge(w_rest_in, 16)
                    for h in range(H):
                        if (i, h) == (0, 0):
                            pe.wait_ge(kv_copied, 2 * B)
                        if has(i, lo):
                            scores(i, h)
                        if has(i + 1, lo):
                            scores_for_max(i + 1, h)
                        if i == 2 * B and h in UP_AT:
                            if ups == 0:
                                pe.wait_ge(d_folded, 2)
                                pe.wait_ge(xrT_ready, 2)
                                pe.wait_ge(max_ready, 2 * H * B)
                            up(0, [ups])
                            ups += 1
                        if h == 1 and has(i - 1, lo):
                            weighted_sum(i - 1, 3)
                        if h == 3 and has(i, lo):
                            if prep_free:
                                pe.wait_ge(*prep_free)
                            max_transpose(i, 1)
                            prep_free = (maxT_ready, 2 * i + 2)
                        if h == 3 and has(i - 1, lo):
                            u_transpose(i - 1, 0)
                        if h == 4 and x is not None:
                            if prep_free:
                                pe.wait_ge(*prep_free)
                            xn_transpose(x)
                            prep_free = (xnT_ready, x + 1)
                        if h % G == 1 and h >= G and has(i, lo):
                            weighted_sum(i, h // G - 1)
                        if h == 6 and has(i - 1, lo):
                            u_transpose(i - 1, 1)
                        if h == 7 and x is not None:
                            qk_project(x)
                            prep_free = (qk_ready, 2 * (x + 1))
                        if h == 11 and has(i - 1, lo):
                            o_transpose(i - 1)
                        if h == 10 and has(i + 1, lo):
                            if prep_free:
                                pe.wait_ge(*prep_free)
                            max_transpose(i + 1, 0)
                            prep_free = (maxT_ready, 2 * (i + 1) + 1)
                        if h in KV_AT.get(i, ()):
                            kv_project(kv_done)
                            kv_done += 1
                        if h == 14 and x is not None and x // B != 1:
                            if prep_free:
                                pe.wait_ge(*prep_free)
                            v_project(x)
                            prep_free = (v_ready, v_count(x))
                        if h == 15 and has(i - 1, lo):
                            out_project(i - 1)
                        if h == 15 and lo == B and has(i - 2, lo) and i - 2 < lo + B - 1:
                            if prep_free:
                                pe.wait_ge(*prep_free)
                            xr_transpose(i - 2 - B)
                            prep_free = (xrT_ready, i - 2 - B + 1)
            pe.wait_ge(x_ready, 2 * B)
            pe.wait_ge(v_ready, v_count(4 * B - 1))
            pe.wait_ge(maxT_ready, 4 * B)
            pe.wait_ge(max_ready, 2 * H * B)
            pe.wait_ge(exp_ready, 2 * H * B)
            pe.wait_ge(uT_ready, 4 * B)
            def weight_transpose():
                pe.wait_ge(weight_ready, 1)
                for k in range(NT):
                    i = pe.transpose(pv_ps[1][:, 0, k * B:(k + 1) * B], weight[:, k * P:(k + 1) * P], ident[0:B, 0:B])
                i.then_inc(w_psum, 1)

            def down(q):
                pe.wait_ge(xrT_ready, B)
                for e in range(2):
                    b = 2 * q + e
                    pe.wait_ge(d_h_ready, NC * (q + 1))
                    if b >= 2:
                        pe.wait_ge(light_done, b - 1)
                        pe.wait_ge(heavy_copied, b - 1)
                    toks = [slice((NT * e + k) * P, (NT * e + k + 1) * P) for k in range(NT)]
                    for k in range(NT):
                        for f in range(NC - 1):
                            i = pe.matmul(heavy_bank(b)[:, k, :], d_hT[:, q % 2, f, toks[k]], d_w2[:, f, :],
                                          start=(f == 0), stop=(f == NC - 2))
                    i.then_inc(d_y_psum, 1)
                    if b == B - 1:
                        weight_transpose()
                    pe.wait_ge(light_bias, b + 1)
                    for k in range(NT):
                        pe.matmul(light_bank(b)[:, k, :], ident[:, :], x_all[:, last_tiles(b).start + k, :], start=True, stop=False)
                        i = pe.matmul(light_bank(b)[:, k, :], d_hT[:, q % 2, NC - 1, toks[k]], d_w2[:, NC - 1, :],
                                      start=False, stop=True)
                    i.then_inc(d_y_psum, 1)

            pe.wait_ge(s_tok_ready, NT * B)
            for k in range(NT):
                i = pe.transpose(pv_ps[0][0:B, 0, k * P:(k + 1) * P], s_tok[:, :, k], ident[:, :])
            i.then_inc(s_row_psum, 1)
            pe.wait_ge(xrT_ready, B - 1)
            xr_transpose(B - 1)
            for q in range(5):
                if 1 <= q < 4:
                    pe.wait_ge(xrT_ready, 2 * q + 2)
                    up(q)
                if q >= 1:
                    down(q - 1)


def laid_out(i):
    def pad(a, axis):
        return np.concatenate([a, np.zeros(a.shape[:axis] + (P - a.shape[axis],) + a.shape[axis + 1:], a.dtype)], axis)

    perm = np.arange(D).reshape(H, DH).T.reshape(-1)
    wqkv = i["L0_attn_W_qkv"].T
    bqkv = i["L0_attn_b_qkv"]
    out = {"x": i["x"], "ctxT": i["ctx_1024"].reshape(B * S, D).T}
    none, nob = np.zeros((D, D), np.float32), np.zeros(D, np.float32)
    w3, b3 = i["L1_attn_W_qkv"].T, i["L1_attn_b_qkv"]
    out["w_att"] = np.stack([
        np.stack([wqkv[:, 0:D][:, perm], wqkv[:, D:2 * D][:, perm], wqkv[:, 2 * D:], i["L0_attn_W_out"].T]),
        np.stack([i["L0_xattn_Wq"], i["L0_xattn_Wk"], i["L0_xattn_Wv"], none]),
        np.stack([w3[:, 0:D], w3[:, D:2 * D], w3[:, 2 * D:], none]),
        np.stack([i["L1_xattn_Wq"][:, perm], i["L1_xattn_Wk"][:, perm], i["L1_xattn_Wv"], i["L1_xattn_Wo"]])])
    out["b_qk"] = np.stack([np.stack([bqkv[0:D][perm], bqkv[D:2 * D][perm]], -1),
                            np.stack([i["L0_xattn_bq"], i["L0_xattn_bk"]], -1),
                            np.stack([b3[0:D], b3[D:2 * D]], -1),
                            np.stack([i["L1_xattn_bq"][perm], i["L1_xattn_bk"][perm]], -1)], 1)
    out["b_vo"] = np.stack([np.stack([bqkv[2 * D:], i["L0_attn_b_out"]]), np.stack([i["L0_xattn_bv"], nob]),
                            np.stack([b3[2 * D:], nob]), np.stack([i["L1_xattn_bv"], i["L1_xattn_bo"]])])
    out["f_w1"] = i["L0_ffn_w1"].reshape(D, NF, P)
    out["f_w2"] = i["L0_ffn_w2"].reshape(NF, P, D).transpose(1, 0, 2)
    out["f_ew"] = i["L0_ffn_expert_weights"].reshape(FT, P, 2).transpose(1, 0, 2)
    out["d_w1"] = np.concatenate([i["L1_ffn_w1_h"].T, pad(i["L1_ffn_w1_l"].T, 1)], 1).reshape(D, NC, P)
    out["d_w2"] = np.concatenate([i["L1_ffn_w2_h"].T, pad(i["L1_ffn_w2_l"].T, 0)], 0).reshape(NC, P, D).transpose(1, 0, 2)
    out["d_b1"] = np.concatenate([i["L1_ffn_b1_h"], pad(i["L1_ffn_b1_l"], 0)]).reshape(NC, P).T
    out["d_b2"] = np.stack([i["L1_ffn_b2_h"], i["L1_ffn_b2_l"]])
    out["gamma"] = np.stack([i["L1_ffn_gamma_h"], i["L1_ffn_gamma_l"]], -1)
    out["route"] = i["L1_ffn_routing_token"]
    return {k: np.ascontiguousarray(v) for k, v in out.items()}


def kernel(**inputs):
    import concourse.bacc as bacc
    from concourse.bass_utils import run_bass_kernel_spmd
    arrays = laid_out({k: np.asarray(v) for k, v in inputs.items()})
    nc = bacc.Bacc("TRN2", target_bir_lowering=False, num_devices=1)
    dram = {k: nc.dram_tensor(k, a.shape, mybir.dt.from_np(a.dtype), kind="ExternalInput").ap() for k, a in arrays.items()}
    dram["out"] = nc.dram_tensor("out", (B, S, D), fp32, kind="ExternalOutput").ap()
    build(nc, dram)
    r = run_bass_kernel_spmd(nc, [arrays], core_ids=[0])
    return r.results[0]["out"]
```
